# Optimizing a Trainium2 kernel written in Bass

```python
import numpy as np
import jax
import jax.numpy as jnp

def _softmax(x, axis=-1):
    return jax.nn.softmax(x, axis=axis)

def _gelu(x):
    return jax.nn.gelu(x, approximate=True)

def _silu(x):
    return jax.nn.silu(x)

def _sigmoid(x):
    return jax.nn.sigmoid(x)

def _layernorm(x, axis=-1, eps=1e-05):
    m = jnp.mean(x, axis=axis, keepdims=True)
    v = jnp.var(x, axis=axis, keepdims=True)
    return (x - m) / jnp.sqrt(v + eps)

def _scatter_add(tgt, idx, src, axis=0):
    return tgt.at[idx].add(src)

def _segment_sum(src, seg, n):
    return jax.ops.segment_sum(src, seg, n)
kernel_name = 'mk_macaron_d2_jaxref_r8_ff3409'

def setup_inputs(seed: int=0):
    np.random.seed(seed)
    _w = jnp.asarray

    def _L0_attn_setup():
        import jax, jax.numpy as jnp
        import numpy as np
        NUM_HEADS = 16
        EPS = float(jnp.finfo(jnp.float32).eps)

        def rms_norm(x, w):
            ms = jnp.mean(x * x, axis=-1, keepdims=True)
            return x * jax.lax.rsqrt(ms + EPS) * w
        key = jax.random.key(seed)
        k = jax.random.split(key, 5)
        B, N, D = (4, 256, 128)
        Dh = D // NUM_HEADS
        return {'x': jax.random.normal(k[0], (B, N, D), dtype=jnp.float32), 'Wq': jax.random.normal(k[1], (D, D), dtype=jnp.float32) * 0.02, 'Wk': jax.random.normal(k[2], (D, D), dtype=jnp.float32) * 0.02, 'Wv': jax.random.normal(k[3], (D, D), dtype=jnp.float32) * 0.02, 'Wo': jax.random.normal(k[4], (D, D), dtype=jnp.float32) * 0.02, 'qn_w': jnp.ones((Dh,), dtype=jnp.float32), 'kn_w': jnp.ones((Dh,), dtype=jnp.float32)}
    _L0_attn_in = _L0_attn_setup()

    def _L0_ffn_setup():
        import jax, jax.numpy as jnp
        import numpy as np
        B, T, C, I, E = (4, 256, 128, 352, 7)

        def _swiglu(h, w1, w2, w3):
            return jax.nn.silu(h @ w1.T) * (h @ w3.T) @ w2.T
        key = jax.random.key(seed)
        ks = jax.random.split(key, 9)
        sc_c = 1.0 / np.sqrt(C)
        sc_i = 1.0 / np.sqrt(I)
        return {'x': jax.random.normal(ks[0], (B, T, C), jnp.float32), 'router_w': jax.random.normal(ks[1], (E, C), jnp.float32) * sc_c, 'routing_bias': jnp.zeros((E,), jnp.float32), 'sw1': jax.random.normal(ks[2], (I, C), jnp.float32) * sc_c, 'sw2': jax.random.normal(ks[3], (C, I), jnp.float32) * sc_i, 'sw3': jax.random.normal(ks[4], (I, C), jnp.float32) * sc_c, 'ew1': jax.random.normal(ks[5], (E, I, C), jnp.float32) * sc_c, 'ew2': jax.random.normal(ks[6], (E, C, I), jnp.float32) * sc_i, 'ew3': jax.random.normal(ks[7], (E, I, C), jnp.float32) * sc_c}
    _L0_ffn_in = _L0_ffn_setup()

    def _L1_attn_setup():
        import jax, jax.numpy as jnp
        import numpy as np
        EPS = 1e-08

        def polar_orth(W):
            u, s, vt = jnp.linalg.svd(W.astype(jnp.float32), full_matrices=False)
            return u @ vt

        def rms(z):
            return z * jax.lax.rsqrt(jnp.mean(z * z, axis=-1, keepdims=True) + EPS)

        def _reference_tuple_inner(x, Wq, Wv, Wc, Wp1, Wp2, identity):
            B, T, D = x.shape
            P1 = polar_orth(Wp1).astype(x.dtype)
            P2 = polar_orth(Wp2).astype(x.dtype)
            q = jnp.einsum('btd,ed->bte', x, Wq)
            v = jnp.einsum('btd,ed->bte', x, Wv)

            def combine(left, right):
                z = left @ P1.T + right @ P2.T
                return rms(z)
            seq = jnp.concatenate([jnp.broadcast_to(identity.astype(x.dtype), (B, 1, D)), q], axis=1)
            h = jax.lax.associative_scan(combine, seq, axis=1)
            qs = h[:, 1:]
            Y = jnp.einsum('btd,ed->bte', qs * v, Wc)
            return (Y, qs)
        key = jax.random.key(seed)
        ks = jax.random.split(key, 7)
        B, T, D = (4, 512, 128)
        scale = 1.0 / np.sqrt(D)
        x = jax.random.normal(ks[0], (B, T, D), jnp.float32)
        Wq = jax.random.normal(ks[1], (D, D), jnp.float32) * scale
        Wv = jax.random.normal(ks[2], (D, D), jnp.float32) * scale
        Wc = jax.random.normal(ks[3], (D, D), jnp.float32) * scale
        Wp1 = jax.random.normal(ks[4], (D, D), jnp.float32) * scale
        Wp2 = jax.random.normal(ks[5], (D, D), jnp.float32) * scale
        identity = jax.random.uniform(ks[6], (D,), jnp.float32)
        return {'x': x, 'Wq': Wq, 'Wv': Wv, 'Wc': Wc, 'Wp1': Wp1, 'Wp2': Wp2, 'identity': identity}
    _L1_attn_in = _L1_attn_setup()

    def _L1_ffn_setup():
        import jax, jax.numpy as jnp
        import numpy as np
        NUM_EXPERTS = 64
        TOP_K = 8
        HIDDEN = 128
        INTER = 96
        BATCH, SEQ = (1, 128)
        CAPACITY = 32

        def _moe_forward(hidden_states, gate_w, w_gate, w_up, w_down):
            B, S, H = hidden_states.shape
            x = hidden_states.reshape(-1, H)
            T = x.shape[0]
            logits = (x @ gate_w.T).astype(jnp.float32)
            probs = jax.nn.softmax(logits, axis=-1)
            topk_p, topk_i = jax.lax.top_k(probs, TOP_K)
            topk_p = topk_p / jnp.sum(topk_p, axis=-1, keepdims=True)
            flat_e = topk_i.reshape(-1)
            onehot = jax.nn.one_hot(flat_e, NUM_EXPERTS, dtype=jnp.int32)
            pos_all = jnp.cumsum(onehot, axis=0) - 1
            pos = jnp.take_along_axis(pos_all, flat_e[:, None], axis=1)[:, 0]
            x_rep = jnp.repeat(x, TOP_K, axis=0)
            dispatch = jnp.zeros((NUM_EXPERTS, CAPACITY, H), x.dtype)
            dispatch = dispatch.at[flat_e, pos].set(x_rep, mode='drop')
            g = jax.nn.silu(jnp.einsum('ech,eih->eci', dispatch, w_gate))
            u = jnp.einsum('ech,eih->eci', dispatch, w_up)
            y = jnp.einsum('eci,ehi->ech', g * u, w_down)
            valid = pos < CAPACITY
            y_tok = y[flat_e, jnp.minimum(pos, CAPACITY - 1)]
            w = (topk_p.reshape(-1) * valid.astype(topk_p.dtype)).astype(x.dtype)
            out = (y_tok * w[:, None]).reshape(T, TOP_K, H).sum(axis=1)
            return out.reshape(B, S, H)
        key = jax.random.key(seed)
        k1, k2, k3, k4, k5 = jax.random.split(key, 5)
        scale = 0.02
        return {'hidden_states': jax.random.normal(k1, (BATCH, SEQ, HIDDEN), dtype=jnp.float32), 'gate_w': jax.random.normal(k2, (NUM_EXPERTS, HIDDEN), dtype=jnp.float32) * scale, 'w_gate': jax.random.normal(k3, (NUM_EXPERTS, INTER, HIDDEN), dtype=jnp.float32) * scale, 'w_up': jax.random.normal(k4, (NUM_EXPERTS, INTER, HIDDEN), dtype=jnp.float32) * scale, 'w_down': jax.random.normal(k5, (NUM_EXPERTS, HIDDEN, INTER), dtype=jnp.float32) * scale}
    _L1_ffn_in = _L1_ffn_setup()
    _d = {'L0_attn_x': _L0_attn_in['x'], 'L0_attn_Wq': _L0_attn_in['Wq'], 'L0_attn_Wk': _L0_attn_in['Wk'], 'L0_attn_Wv': _L0_attn_in['Wv'], 'L0_attn_Wo': _L0_attn_in['Wo'], 'L0_attn_qn_w': _L0_attn_in['qn_w'], 'L0_attn_kn_w': _L0_attn_in['kn_w'], 'L0_ffn_router_w': _L0_ffn_in['router_w'], 'L0_ffn_routing_bias': _L0_ffn_in['routing_bias'], 'L0_ffn_sw1': _L0_ffn_in['sw1'], 'L0_ffn_sw2': _L0_ffn_in['sw2'], 'L0_ffn_sw3': _L0_ffn_in['sw3'], 'L0_ffn_ew1': _L0_ffn_in['ew1'], 'L0_ffn_ew2': _L0_ffn_in['ew2'], 'L0_ffn_ew3': _L0_ffn_in['ew3'], 'L1_attn_Wq': _L1_attn_in['Wq'], 'L1_attn_Wv': _L1_attn_in['Wv'], 'L1_attn_Wc': _L1_attn_in['Wc'], 'L1_attn_Wp1': _L1_attn_in['Wp1'], 'L1_attn_Wp2': _L1_attn_in['Wp2'], 'L1_attn_identity': _L1_attn_in['identity'], 'L1_ffn_gate_w': _L1_ffn_in['gate_w'], 'L1_ffn_w_gate': _L1_ffn_in['w_gate'], 'L1_ffn_w_up': _L1_ffn_in['w_up'], 'L1_ffn_w_down': _L1_ffn_in['w_down']}
    _x0 = _d['L0_attn_x']
    _d['L0_attn_x'] = jax.random.normal(jax.random.fold_in(jax.random.key(seed), 1), (4, 1024, 128), dtype=_x0.dtype)
    del _x0
    return _d

def reference(L0_attn_x, L0_attn_Wq, L0_attn_Wk, L0_attn_Wv, L0_attn_Wo, L0_attn_qn_w, L0_attn_kn_w, L0_ffn_router_w, L0_ffn_routing_bias, L0_ffn_sw1, L0_ffn_sw2, L0_ffn_sw3, L0_ffn_ew1, L0_ffn_ew2, L0_ffn_ew3, L1_attn_Wq, L1_attn_Wv, L1_attn_Wc, L1_attn_Wp1, L1_attn_Wp2, L1_attn_identity, L1_ffn_gate_w, L1_ffn_w_gate, L1_ffn_w_up, L1_ffn_w_down):

    def _L0_attn_ref(x, Wq, Wk, Wv, Wo, qn_w, kn_w):
        import jax, jax.numpy as jnp
        import numpy as np
        NUM_HEADS = 16
        EPS = float(jnp.finfo(jnp.float32).eps)

        def rms_norm(x, w):
            ms = jnp.mean(x * x, axis=-1, keepdims=True)
            return x * jax.lax.rsqrt(ms + EPS) * w
        B, N, D = x.shape
        H = NUM_HEADS
        Dh = D // H
        scale = Dh ** (-0.5)

        def proj(W):
            return (x @ W.T).reshape(B, N, H, Dh).transpose(0, 2, 1, 3)
        q = rms_norm(proj(Wq), qn_w)
        k = rms_norm(proj(Wk), kn_w)
        v = proj(Wv)
        scores = jnp.einsum('bhnd,bhmd->bhnm', q, k) * scale
        attn = jax.nn.softmax(scores, axis=-1)
        out = jnp.einsum('bhnm,bhmd->bhnd', attn, v)
        out = out.transpose(0, 2, 1, 3).reshape(B, N, D)
        return out @ Wo.T

    def _L0_ffn_ref(x, router_w, routing_bias, sw1, sw2, sw3, ew1, ew2, ew3):
        import jax, jax.numpy as jnp
        import numpy as np
        B, T, C, I, E = (4, 256, 128, 352, 7)

        def _swiglu(h, w1, w2, w3):
            return jax.nn.silu(h @ w1.T) * (h @ w3.T) @ w2.T
        b, t, c = x.shape
        shared_out = _swiglu(x, sw1, sw2, sw3)
        logits = jnp.clip(x @ router_w.T + routing_bias, -50.0, 50.0)
        probs = jax.nn.sigmoid(logits)
        num_switched = 1
        topk_probs, topk_idx = jax.lax.top_k(probs, num_switched)
        topk_probs = jnp.clip(topk_probs, 1e-08, 1.0 - 1e-08)
        xf = x.reshape(-1, c)
        sel = topk_idx.reshape(-1)
        p = topk_probs.reshape(-1)
        switched = jnp.zeros_like(xf)
        n_experts = ew1.shape[0]
        for e in range(n_experts):
            y = _swiglu(xf, ew1[e], ew2[e], ew3[e])
            w = jnp.where(sel == e, p, 0.0)
            switched = switched + w[:, None] * y
        switched = switched.reshape(b, t, c)
        total_weight = 0.5 + topk_probs.sum(axis=-1)
        total_weight = jnp.clip(total_weight[..., None] + 1e-08, 0.5, 2.0)
        return 0.5 / total_weight * shared_out + switched / total_weight

    def _L1_attn_ref(x, Wq, Wv, Wc, Wp1, Wp2, identity):
        import jax, jax.numpy as jnp
        import numpy as np
        EPS = 1e-08

        def polar_orth(W):
            u, s, vt = jnp.linalg.svd(W.astype(jnp.float32), full_matrices=False)
            return u @ vt

        def rms(z):
            return z * jax.lax.rsqrt(jnp.mean(z * z, axis=-1, keepdims=True) + EPS)

        def _reference_tuple_inner(x, Wq, Wv, Wc, Wp1, Wp2, identity):
            B, T, D = x.shape
            P1 = polar_orth(Wp1).astype(x.dtype)
            P2 = polar_orth(Wp2).astype(x.dtype)
            q = jnp.einsum('btd,ed->bte', x, Wq)
            v = jnp.einsum('btd,ed->bte', x, Wv)

            def combine(left, right):
                z = left @ P1.T + right @ P2.T
                return rms(z)
            seq = jnp.concatenate([jnp.broadcast_to(identity.astype(x.dtype), (B, 1, D)), q], axis=1)
            h = jax.lax.associative_scan(combine, seq, axis=1)
            qs = h[:, 1:]
            Y = jnp.einsum('btd,ed->bte', qs * v, Wc)
            return (Y, qs)
        return _reference_tuple_inner(x, Wq, Wv, Wc, Wp1, Wp2, identity)[0]

    def _L1_ffn_ref(hidden_states, gate_w, w_gate, w_up, w_down):
        import jax, jax.numpy as jnp
        import numpy as np
        NUM_EXPERTS = 64
        TOP_K = 8
        HIDDEN = 128
        INTER = 96
        BATCH, SEQ = (1, 128)
        CAPACITY = 32

        def _moe_forward(hidden_states, gate_w, w_gate, w_up, w_down):
            B, S, H = hidden_states.shape
            x = hidden_states.reshape(-1, H)
            T = x.shape[0]
            logits = (x @ gate_w.T).astype(jnp.float32)
            probs = jax.nn.softmax(logits, axis=-1)
            topk_p, topk_i = jax.lax.top_k(probs, TOP_K)
            topk_p = topk_p / jnp.sum(topk_p, axis=-1, keepdims=True)
            flat_e = topk_i.reshape(-1)
            onehot = jax.nn.one_hot(flat_e, NUM_EXPERTS, dtype=jnp.int32)
            pos_all = jnp.cumsum(onehot, axis=0) - 1
            pos = jnp.take_along_axis(pos_all, flat_e[:, None], axis=1)[:, 0]
            x_rep = jnp.repeat(x, TOP_K, axis=0)
            dispatch = jnp.zeros((NUM_EXPERTS, CAPACITY, H), x.dtype)
            dispatch = dispatch.at[flat_e, pos].set(x_rep, mode='drop')
            g = jax.nn.silu(jnp.einsum('ech,eih->eci', dispatch, w_gate))
            u = jnp.einsum('ech,eih->eci', dispatch, w_up)
            y = jnp.einsum('eci,ehi->ech', g * u, w_down)
            valid = pos < CAPACITY
            y_tok = y[flat_e, jnp.minimum(pos, CAPACITY - 1)]
            w = (topk_p.reshape(-1) * valid.astype(topk_p.dtype)).astype(x.dtype)
            out = (y_tok * w[:, None]).reshape(T, TOP_K, H).sum(axis=1)
            return out.reshape(B, S, H)
        return _moe_forward(hidden_states, gate_w, w_gate, w_up, w_down)
    x = L0_attn_x
    x = x + 0.5 * _L0_ffn_ref(_layernorm(x, axis=-1), L0_ffn_router_w, L0_ffn_routing_bias, L0_ffn_sw1, L0_ffn_sw2, L0_ffn_sw3, L0_ffn_ew1, L0_ffn_ew2, L0_ffn_ew3)
    x = x + _L0_attn_ref(_layernorm(x, axis=-1), L0_attn_Wq, L0_attn_Wk, L0_attn_Wv, L0_attn_Wo, L0_attn_qn_w, L0_attn_kn_w)
    x = x + 0.5 * _L0_ffn_ref(_layernorm(x, axis=-1), L0_ffn_router_w, L0_ffn_routing_bias, L0_ffn_sw1, L0_ffn_sw2, L0_ffn_sw3, L0_ffn_ew1, L0_ffn_ew2, L0_ffn_ew3)
    x = x + 0.5 * _L1_ffn_ref(_layernorm(x, axis=-1), L1_ffn_gate_w, L1_ffn_w_gate, L1_ffn_w_up, L1_ffn_w_down)
    x = x + _L1_attn_ref(_layernorm(x, axis=-1), L1_attn_Wq, L1_attn_Wv, L1_attn_Wc, L1_attn_Wp1, L1_attn_Wp2, L1_attn_identity)
    x = x + 0.5 * _L1_ffn_ref(_layernorm(x, axis=-1), L1_ffn_gate_w, L1_ffn_w_gate, L1_ffn_w_up, L1_ffn_w_down)
    return x

_drawn_inputs = setup_inputs


def setup_inputs(seed=0):
    import zlib

    import numpy as np

    out = dict(_drawn_inputs(seed))
    spreads = {'L0_attn_qn_w': (1.0, 0.6), 'L0_attn_kn_w': (1.0, 0.6), 'L0_ffn_routing_bias': (0.0, 0.1)}
    factors = {'L0_attn_Wq': 5.076,
     'L0_attn_Wk': 5.015,
     'L0_attn_Wv': 4.185,
     'L0_attn_Wo': 4.748,
     'L1_attn_identity': 4.891,
     'L1_ffn_gate_w': 8.0,
     'L1_ffn_w_gate': 8.0,
     'L1_ffn_w_up': 8.0,
     'L1_ffn_w_down': 8.0}
    for name, (base, spread) in spreads.items():
        noise = np.random.default_rng([zlib.crc32(name.encode()), seed]).standard_normal(out[name].shape)
        drawn = base * np.exp(spread * noise) if base else spread * noise
        out[name] = jnp.asarray(drawn.astype(out[name].dtype))
    for name, factor in factors.items():
        out[name] = (out[name] * factor).astype(out[name].dtype)
    return out
```

```python
from contextlib import ExitStack

import concourse.bass as bass
from concourse import mybir

F32 = mybir.dt.float32
BF16 = mybir.dt.bfloat16
I32 = mybir.dt.int32
ALU = mybir.AluOpType
ACT = mybir.ActivationFunctionType
AX = mybir.AxisListType
ds = bass.ds

P = 128
D = 128
B, N = 4, 1024
T = B * N
TILES = T // P
CT = 4
CW = CT * P
CHUNKS = TILES // CT
LN_EPS = 1e-5

I = 352
E = 7
IC = [(0, 128), (128, 128), (256, 96)]


def bcast(ap, at, n):
    dims = [list(x) for x in ap.ap]
    dims.insert(at, [0, n])
    return bass.AP(ap.tensor, ap.offset, dims)


class Pool_:

    def __init__(self, nc, stack, sems, tag):
        self.nc, self.stack, self.sems, self.tag = nc, stack, sems, tag
        self.seeds = None

    def sb(self, name, shape, dt=F32):
        return self.stack.enter_context(self.nc.sbuf_tensor(f"{self.tag}_{name}", shape, dt))

    def ps(self, name, shape, dt=F32):
        return self.stack.enter_context(self.nc.psum_tensor(f"{self.tag}_{name}", shape, dt))

    def seed(self, sem, n):
        if self.seeds is None:
            self.seeds, self.n = self.sb("seeds", [P, 12]), 0
        self.nc.vector.memset(self.seeds[:, self.n:self.n + 1], 0.0).then_inc(sem, n)
        self.n += 1

    def sem(self, name):
        return self.nc.alloc_semaphore(name=f"{self.tag}_{name}")


class Norm:

    def __init__(self, m, X, ident, transposed=True):
        self.X, self.ident = X, ident
        self.stats = m.sb("stats", [P, 2, CT, 6])
        self.mv = m.sb("mv", [P, 2, CT, 2])
        self.std = m.sb("std", [P, 2, CT])
        self.rstd = m.sb("rstd", [P, 2, CT])
        self.h = m.sb("h", [P, 2, CT, D])
        self.hT = m.sb("hT", [P, 2, CW])
        self.eps = m.sb("eps", [P, 1])
        self.tick = m.sb("tick", [P, 1])
        self.s_stats = m.sem("s_stats")
        self.s_mv = m.sem("s_mv")
        self.s_std = m.sem("s_std")
        self.s_rstd = m.sem("s_rstd")
        self.s_h = m.sem("s_h")
        self.s_tr = m.sem("s_tr")
        self.s_hT = m.sem("s_hT")
        self.s_eps = m.sem("s_eps")

    def dve_eps(self, nc):
        nc.vector.memset(self.eps[:, :], LN_EPS).then_inc(self.s_eps, 1)

    def dve_stats(self, nc, c, u):
        for j in range(CT):
            nc.vector.bn_stats(self.stats[:, u, j, :], self.X[:, ds(c * CT + j, 1), :]).then_inc(self.s_stats, 1)
        nc.vector.wait_ge(self.s_stats, (c + 1) * CT)
        nc.vector.memset(self.tick[:, :], 0.0)
        for j in range(CT):
            nc.vector.bn_aggr(self.mv[:, u, j, :], self.stats[:, u, j, :]).then_inc(self.s_mv, 1)

    def act_std(self, nc, c, u):
        nc.scalar.wait_ge(self.s_mv, (c + 1) * CT)
        nc.scalar.activation(self.std[:, u, :], self.mv[:, u, :, 1], ACT.Sqrt,
                             bias=self.eps[:, 0:1]).then_inc(self.s_std, 1)

    def dve_apply(self, nc, c, u):
        nc.vector.wait_ge(self.s_std, c + 1)
        nc.vector.reciprocal(self.rstd[:, u, :], self.std[:, u, :]).then_inc(self.s_rstd, 1)
        nc.vector.wait_ge(self.s_rstd, c + 1)
        for j in range(CT):
            nc.vector.tensor_scalar(out=self.h[:, u, j, :], in0=self.X[:, ds(c * CT + j, 1), :],
                                    scalar1=self.mv[:, u, j, 0:1], scalar2=self.rstd[:, u, j:j + 1],
                                    op0=ALU.subtract, op1=ALU.mult).then_inc(self.s_h, 1)

    def pe_transpose(self, nc, c, u, tr):
        nc.tensor.wait_ge(self.s_h, (c + 1) * CT)
        for j in range(CT):
            last = nc.tensor.transpose(tr[:, j * P:(j + 1) * P], self.h[:, u, j, :], self.ident[:, :])
        last.then_inc(self.s_tr, 1)

    def act_hT(self, nc, c, u, tr):
        nc.scalar.wait_ge(self.s_tr, c + 1)
        nc.scalar.activation(self.hT[:, u, :], tr[:, :], ACT.Copy).then_inc(self.s_hT, 1)


def stage_load(nc, sems, W, consts):
    st = ExitStack()
    with st:
        m = Pool_(nc, st, sems, "ld")
        s_in = m.sem("s_in")
        block = st.enter_context(nc.Block())

        @block.sync
        def _(sp):
            xin = W["x"].rearrange("b (n p) d -> p (b n) d", p=P)
            for q in range(4):
                sp.dma_start(consts["X"][:, q * 8:q * 8 + 8, :], xin[:, q * 8:q * 8 + 8, :]).then_inc(s_in, 16)
            for name in ("ident", "ones", "triu", "iota"):
                sp.dma_start(consts[name][:, :], W[name]).then_inc(s_in, 16)
            sp.wait_ge(s_in, 16 * 8)

        @block.vector
        def _(dve):
            nc.vector.memset(consts["zero"][:, :], 0.0)
            dve.wait_ge(s_in, 16 * 8)
            for name in ("ident", "ones", "triu"):
                nc.vector.tensor_copy(consts[name + "b"][:, :], consts[name][:, :])


def stage_ffn(nc, sems, tag, W, K, R, load, M=None):
    X, ident, ones = K["X"], K["ident"], K["ones"]
    w1, w3, w2, wr, br = R["w1"], R["w3"], R["w2"], R["wr"], R["br"]
    NE = E + 1
    G = NE * len(IC)
    st = ExitStack()
    with st:
        m = Pool_(nc, st, sems, tag)
        norm = Norm(m, X, ident)
        silu = m.sb("silu", [P, 2, CW])
        gu = m.sb("gu", [P, 2, len(IC), CW])
        lg = m.sb("lg", [P, 2, CT, E])
        pr = m.sb("pr", [P, 2, CT, E])
        pmax = m.sb("pmax", [P, 2, CT])
        eq = m.sb("eq", [P, 2, CT, E])
        smax = m.sb("smax", [P, 2, CT])
        pc = m.sb("pc", [P, 2, CT])
        tw = m.sb("tw", [P, 2, CT])
        rt = m.sb("rt", [P, 2, CT])
        ph = m.sb("ph", [P, 2, CT])
        wt = m.sb("wt", [P, 2, CT, NE])
        ps_a = m.ps("ps_a", [P, 2, CW])
        ps_b = m.ps("ps_b", [P, 2, CW])
        ps_y = m.ps("ps_y", [P, 2, CT, D])
        ps_tr = m.ps("ps_tr", [P, CW])
        ps_lg = m.ps("ps_lg", [P, CT, E])
        s_w = m.sem("s_w")
        s_lgm = m.sem("s_lgm")
        s_lg = m.sem("s_lg")
        s_pr = m.sem("s_pr")
        s_r = m.sem("s_r")
        s_ab = m.sem("s_ab")
        s_silu = m.sem("s_silu")
        s_gu = m.sem("s_gu")
        s_y = m.sem("s_y")
        s_yu = m.sem("s_yu")
        RS = 10
        block = st.enter_context(nc.Block())

        @block.sync
        def _(sp):
            if M is not None:
                sp.dma_start(M["wr"][:, :], W["xwr"]).then_inc(s_w, 16)
                for q in range(4):
                    for n in ("wg", "wu", "wd"):
                        sp.dma_start(M[n][:, q * 16:q * 16 + 16, :], W["x" + n][:, q * 16:q * 16 + 16, :]
                                     ).then_inc(s_w, 16)
                sp.wait_ge(s_w, 16 * 13)
            if load:
                sp.dma_start(w1[:, :, :], W["w1"]).then_inc(s_w, 16)
                sp.dma_start(w3[:, :, :], W["w3"]).then_inc(s_w, 16)
                for j, (i0, n) in enumerate(IC):
                    sp.dma_start(w2[0:n, j, :, :], W["w2"][i0:i0 + n, :, :]).then_inc(s_w, 16)
                sp.dma_start(wr[:, :], W["wr"]).then_inc(s_w, 16)
                sp.dma_start(br[:, :], W["br"]).then_inc(s_w, 16)
                sp.dma_start(R["rev"][:, :], W["rev"]).then_inc(s_w, 16)
                sp.wait_ge(s_w, 128)

        @block.vector
        def _(dve):
            norm.dve_eps(nc)
            m.seed(s_gu, 2)
            m.seed(s_y, 2)
            m.seed(s_yu, 8)
            if load:
                dve.wait_ge(s_w, 128)

            def route(c, u):
                def step(k, ins):
                    ins.then_inc(s_r, 1)
                    dve.wait_ge(s_r, c * RS + k)
                dve.wait_ge(s_lgm, c + 1)
                nc.vector.tensor_scalar(out=lg[:, u], in0=ps_lg[:, :, :], scalar1=-50.0, scalar2=50.0,
                                        op0=ALU.max, op1=ALU.min).then_inc(s_lg, 1)
                dve.wait_ge(s_pr, c + 1)
                step(1, nc.vector.tensor_reduce(out=pmax[:, u, :], in_=pr[:, u], axis=AX.X, op=ALU.max))
                step(2, nc.vector.tensor_tensor(out=eq[:, u], in0=pr[:, u], in1=bcast(pmax[:, u, :], 2, E),
                                                op=ALU.is_equal))
                step(3, nc.vector.tensor_tensor(out=eq[:, u], in0=eq[:, u], in1=bcast(R["rev"][:, :], 1, CT),
                                                op=ALU.mult))
                step(4, nc.vector.tensor_reduce(out=smax[:, u, :], in_=eq[:, u], axis=AX.X, op=ALU.max))
                step(5, nc.vector.tensor_tensor(out=eq[:, u], in0=eq[:, u], in1=bcast(smax[:, u, :], 2, E),
                                                op=ALU.is_equal))
                step(6, nc.vector.tensor_scalar(out=pc[:, u, :], in0=pmax[:, u, :], scalar1=1e-8,
                                                scalar2=1.0 - 1e-8, op0=ALU.max, op1=ALU.min))
                step(7, nc.vector.tensor_scalar(out=tw[:, u, :], in0=pc[:, u, :], scalar1=0.5, scalar2=1e-8,
                                                op0=ALU.add, op1=ALU.add))
                step(8, nc.vector.tensor_scalar(out=tw[:, u, :], in0=tw[:, u, :], scalar1=0.5, scalar2=2.0,
                                                op0=ALU.max, op1=ALU.min))
                step(9, nc.vector.reciprocal(rt[:, u, :], tw[:, u, :]))
                nc.vector.tensor_scalar_mul(wt[:, u, :, E], rt[:, u, :], 0.25)
                step(10, nc.vector.scalar_tensor_tensor(out=ph[:, u, :], in0=pc[:, u, :], scalar=0.5,
                                                        in1=rt[:, u, :], op0=ALU.mult, op1=ALU.mult))
                nc.vector.tensor_tensor(out=wt[:, u, :, 0:E], in0=eq[:, u], in1=bcast(ph[:, u, :], 2, E),
                                        op=ALU.mult).then_inc(s_wt, 1)
                dve.wait_ge(s_wt, c + 1)

            def gate(c, u, e, j):
                g, n = e * 3 + j, IC[j][1]
                dve.wait_ge(s_silu, c * G + g + 1)
                if j == 0:
                    dve.wait_ge(s_y, c * NE + e + 1)
                nc.vector.tensor_tensor(out=gu[0:n, e % 2, j, :], in0=ps_b[0:n, g % 2, :],
                                        in1=silu[0:n, g % 2, :], op=ALU.mult).then_inc(s_gu, 1)

            def add(c, u, e):
                dve.wait_ge(s_y, c * NE + e + 3)
                dve.wait_ge(s_yu, (c * NE + e) * CT + 8)
                for j in range(CT):
                    xt = X[:, ds(c * CT + j, 1), :]
                    nc.vector.scalar_tensor_tensor(out=xt, in0=ps_y[:, e % 2, j:j + 1, :],
                                                   scalar=wt[:, u, j, e:e + 1], in1=xt,
                                                   op0=ALU.mult, op1=ALU.add).then_inc(s_yu, 1)

            s_wt = K["s_wt_" + tag]
            norm.dve_stats(nc, 0, 0)
            norm.dve_apply(nc, 0, 0)

            def chunk(c, u, more):
                route(c, u)
                for e in range(NE):
                    for j in range(3):
                        gate(c, u, e, j)
                    if e:
                        add(c, u, e - 1)
                    if more and e == 2:
                        norm.dve_stats(nc, c + 1, 1 - u)
                    if more and e == 3:
                        norm.dve_apply(nc, c + 1, 1 - u)
                add(c, u, NE - 1)

            with dve.Fori(0, CHUNKS // 2 - 1) as k:
                for u in range(2):
                    chunk(k * 2 + u, u, True)
            chunk(CHUNKS - 2, 0, True)
            chunk(CHUNKS - 1, 1, False)

        @block.scalar
        def _(act):
            act.wait_ge(norm.s_eps, 1)
            norm.act_std(nc, 0, 0)
            norm.act_hT(nc, 0, 0, ps_tr)

            def chunk(c, u, more):
                act.wait_ge(s_lg, c + 1)
                nc.scalar.activation(pr[:, u], lg[:, u], ACT.Sigmoid).then_inc(s_pr, 1)
                for e in range(NE):
                    for j in range(3):
                        g, n = e * 3 + j, IC[j][1]
                        act.wait_ge(s_ab, c * G + g + 1)
                        act.wait_ge(s_gu, c * G + g + 1)
                        nc.scalar.activation(silu[0:n, g % 2, :], ps_a[0:n, g % 2, :],
                                             ACT.Silu).then_inc(s_silu, 1)
                    if more and e == 2:
                        norm.act_std(nc, c + 1, 1 - u)
                    if more and e == 5:
                        norm.act_hT(nc, c + 1, 1 - u, ps_tr)

            with act.Fori(0, CHUNKS // 2 - 1) as k:
                for u in range(2):
                    chunk(k * 2 + u, u, True)
            chunk(CHUNKS - 2, 0, True)
            chunk(CHUNKS - 1, 1, False)

        @block.tensor
        def _(pe):
            if load:
                pe.wait_ge(s_w, 128)
            norm.pe_transpose(nc, 0, 0, ps_tr)

            def down(c, u, e):
                pe.wait_ge(s_gu, c * G + e * 3 + 5)
                pe.wait_ge(s_yu, (c * NE + e) * CT + 4)
                for s in range(CT):
                    for j, (_, n) in enumerate(IC):
                        last = nc.tensor.matmul(ps_y[:, e % 2, s, :], gu[0:n, e % 2, j, s * P:(s + 1) * P],
                                                w2[0:n, j, e, :], start=(j == 0), stop=(j == 2))
                last.then_inc(s_y, 1)

            def chunk(c, u, more):
                pe.wait_ge(norm.s_hT, c + 1)
                if True:
                    for s in range(CT):
                        nc.tensor.matmul(ps_lg[:, s, :], norm.hT[:, u, s * P:(s + 1) * P], wr[:, :],
                                         start=True, stop=False)
                        last = nc.tensor.matmul(ps_lg[:, s, :], ones[0:1, :], br[0:1, :],
                                                start=False, stop=True)
                    last.then_inc(s_lgm, 1)
                for e in range(NE):
                    for j, (i0, n) in enumerate(IC):
                        g = e * 3 + j
                        pe.wait_ge(s_gu, c * G + g + 1)
                        nc.tensor.matmul(ps_a[0:n, g % 2, :], w1[:, e, i0:i0 + n], norm.hT[:, u, :],
                                         start=True, stop=True)
                        nc.tensor.matmul(ps_b[0:n, g % 2, :], w3[:, e, i0:i0 + n], norm.hT[:, u, :],
                                         start=True, stop=True).then_inc(s_ab, 1)
                    if e:
                        down(c, u, e - 1)
                    if more and e == 5:
                        norm.pe_transpose(nc, c + 1, 1 - u, ps_tr)
                down(c, u, NE - 1)

            with pe.Fori(0, CHUNKS // 2 - 1) as k:
                for u in range(2):
                    chunk(k * 2 + u, u, True)
            chunk(CHUNKS - 2, 0, True)
            chunk(CHUNKS - 1, 1, False)


H, DH = 16, 8
PAIRS = B * H // 2
PT_ = N // P
SCALE = DH ** -0.5
RMS_EPS = 1.1920928955078125e-07
SLOTS = 6
KR = SLOTS * DH
KM = KR + 3
HR = 64


def stage_qkv(nc, sems, W, K, A):
    X, ident = K["X"], K["ident"]
    qkv = [A["q"], A["k"], A["v"]]
    st = ExitStack()
    with st:
        m = Pool_(nc, st, sems, "qkv")
        norm = Norm(m, X, ident)
        w = m.sb("w", [P, 3 * D])
        nw = m.sb("nw", [P, 2, DH])
        sq = m.sb("sq", [P, 2, 2 * D])
        ms = m.sb("ms", [P, 2, 2 * H])
        rr = m.sb("rr", [P, 2, 2 * H])
        qk = m.sb("qk", [P, 2, 2 * D])
        reps = m.sb("reps", [P, 1])
        ps_tr = m.ps("ps_tr", [P, CW])
        ps_q = m.ps("ps_q", [P, 2, CW])
        s_w = m.sem("s_w")
        s_c = m.sem("s_c")
        s_p = m.sem("s_p")
        s_sq = m.sem("s_sq")
        s_ms = m.sem("s_ms")
        s_rt = m.sem("s_rt")
        s_rc = m.sem("s_rc")
        s_n = m.sem("s_n")
        s_v = m.sem("s_v")
        s_g = m.sem("s_g")
        block = st.enter_context(nc.Block())

        @block.sync
        def _(sp):
            sp.dma_start(w[:, :], W["wqkv"]).then_inc(s_w, 16)
            sp.dma_start(nw[:, :, :], W["nw"]).then_inc(s_w, 16)
            sp.wait_ge(s_w, 32)

        @block.vector
        def _(dve):
            norm.dve_eps(nc)
            nc.vector.memset(reps[:, :], RMS_EPS).then_inc(s_c, 1)
            m.seed(s_sq, 2)
            m.seed(s_ms, 2)
            m.seed(s_n, 2)
            m.seed(s_v, 2)
            m.seed(s_g, 4)
            norm.dve_stats(nc, 0, 0)
            norm.dve_apply(nc, 0, 0)

            def sums(t, v):
                dve.wait_ge(s_sq, t + 3)
                nc.vector.tensor_reduce(out=ms[:, v, :], in_=sq[:, v, :].rearrange("p (h d) -> p h d", d=DH),
                                        axis=AX.X, op=ALU.add).then_inc(s_ms, 1)

            def scale(t, v):
                dve.wait_ge(s_rt, t + 1)
                nc.vector.reciprocal(rr[:, v, :], ms[:, v, :]).then_inc(s_rc, 1)
                dve.wait_ge(s_rc, t + 1)
                dve.wait_ge(s_g, 2 * t + 2)
                nc.vector.tensor_tensor(out=qk[:, v, :].rearrange("p (h d) -> p h d", d=DH),
                                        in0=ps_q[:, v, 0:2 * D].rearrange("p (h d) -> p h d", d=DH),
                                        in1=bcast(rr[:, v, :], 2, DH), op=ALU.mult).then_inc(s_n, 1)

            def chunk(c, u, more):
                for j in range(CT):
                    sums(c * CT + j, j % 2)
                    if more and j == 1:
                        norm.dve_stats(nc, c + 1, 1 - u)
                    if more and j == 2:
                        norm.dve_apply(nc, c + 1, 1 - u)
                    scale(c * CT + j, j % 2)

            with dve.Fori(0, CHUNKS // 2 - 1) as k:
                for u in range(2):
                    chunk(k * 2 + u, u, True)
            chunk(CHUNKS - 2, 0, True)
            chunk(CHUNKS - 1, 1, False)

        @block.scalar
        def _(act):
            act.wait_ge(norm.s_eps, 1)
            norm.act_std(nc, 0, 0)
            norm.act_hT(nc, 0, 0, ps_tr)
            act.wait_ge(s_c, 1)

            def chunk(c, u, more):
                for j in range(CT):
                    t, v = c * CT + j, j % 2
                    act.wait_ge(s_p, t + 1)
                    act.wait_ge(s_ms, t + 1)
                    nc.scalar.activation(sq[:, v, :], ps_q[:, v, 0:2 * D], ACT.Square).then_inc(s_sq, 1)
                    act_v(c, u, j, v)
                    act.wait_ge(s_ms, t + 3)
                    nc.scalar.activation(ms[:, v, :], ms[:, v, :], ACT.Sqrt, bias=reps[:, 0:1],
                                         scale=1.0 / DH).then_inc(s_rt, 1)
                    if more and j == 1:
                        norm.act_std(nc, c + 1, 1 - u)
                    if more and j == 3:
                        norm.act_hT(nc, c + 1, 1 - u, ps_tr)

            def act_v(c, u, j, v):
                b = (c - u) // 2 if isinstance(c, int) else kk[0]
                dst = A["v"][:, ds(b * 8, 8), 4 * u + j, :]
                nc.scalar.activation(dst, ps_q[:, v, 2 * D:3 * D].rearrange("p (h d) -> p h d", d=16),
                                     ACT.Copy).then_inc(s_v, 1)

            kk = [None]
            with act.Fori(0, CHUNKS // 2 - 1) as k:
                kk[0] = k
                for u in range(2):
                    chunk(k * 2 + u, u, True)
            chunk(CHUNKS - 2, 0, True)
            chunk(CHUNKS - 1, 1, False)

        @block.gpsimd
        def _(pool):
            pool.wait_ge(s_w, 32)

            def chunk(c, u, b):
                for j in range(CT):
                    t, v = c * CT + j, j % 2
                    pool.wait_ge(s_n, t + 3)
                    for r, x in enumerate(("q", "k")):
                        dst = A[x][:, ds(b * 8, 8), 4 * u + j, :].rearrange("p h (a d) -> p h a d", d=DH)
                        src = qk[:, v, r * D:(r + 1) * D].rearrange("p (h a d) -> p h a d", a=2, d=DH)
                        nc.gpsimd.tensor_tensor(out=dst, in0=src, in1=bcast(bcast(nw[:, r, :], 1, 2), 1, 8),
                                                op=ALU.mult).then_inc(s_g, 1)

            with pool.Fori(0, CHUNKS // 2) as k:
                for u in range(2):
                    chunk(k * 2 + u, u, k)

        @block.tensor
        def _(pe):
            pe.wait_ge(s_w, 32)
            norm.pe_transpose(nc, 0, 0, ps_tr)

            def chunk(c, u, more):
                pe.wait_ge(norm.s_hT, c + 1)
                for j in range(CT):
                    t, v = c * CT + j, j % 2
                    pe.wait_ge(s_n, t + 1)
                    pe.wait_ge(s_v, t + 1)
                    nc.tensor.matmul(ps_q[:, v, 0:3 * D], norm.hT[:, u, j * P:(j + 1) * P], w[:, :],
                                     start=True, stop=True).then_inc(s_p, 1)
                    if more and j == 2:
                        norm.pe_transpose(nc, c + 1, 1 - u, ps_tr)

            with pe.Fori(0, CHUNKS // 2 - 1) as k:
                for u in range(2):
                    chunk(k * 2 + u, u, True)
            chunk(CHUNKS - 2, 0, True)
            chunk(CHUNKS - 1, 1, False)


def stage_attention(nc, sems, K, A):
    ident, identb, O = K["ident"], K["identb"], A["o"]
    G8 = PT_
    st = ExitStack()
    with st:
        m = Pool_(nc, st, sems, "at")
        raw = m.sb("raw", [P, 2, 3, G8 * 16])
        qx = m.sb("qx", [P, 2, G8, 2, HR], BF16)
        kx = m.sb("kx", [P, 2, G8, 2, HR], BF16)
        vx = m.sb("vx", [P, 2, G8, 2, 32])
        r1 = m.sb("r1", [P, 4, G8 * 2, DH])
        mr = m.sb("mr", [P, 2, G8 * 2])
        qT1 = m.sb("qT1", [P, 2, N], BF16)
        qT2 = m.sb("qT2", [P, 2, N], BF16)
        qm1 = m.sb("qm1", [P, 2, 2, N], BF16)
        qm2 = m.sb("qm2", [P, 2, 2, N], BF16)
        kT1 = m.sb("kT1", [P, 2, N], BF16)
        kT2 = m.sb("kT2", [P, 2, N], BF16)
        negm = m.sb("negm", [P, 2, G8, 2])
        pT = m.sb("pT", [P, 8, CW])
        oT = m.sb("oT", [P, 2, CW])
        ro = m.sb("ro", [P, 2, 4, 4])
        ps_s = m.ps("ps_s", [P, 2, N])
        ps_p = m.ps("ps_p", [P, 2, CW])
        ps_o = m.ps("ps_o", [P, CW])
        ps_t = m.ps("ps_t", [P, CW])
        tb = ps_t[:, :].bitcast(BF16)
        s_raw = [m.sem(f"s_raw{u}") for u in range(2)]
        s_c = m.sem("s_c")
        s_q1 = m.sem("s_q1")
        s_bld = m.sem("s_bld")
        s_vx = m.sem("s_vx")
        s_msp = m.sem("s_msp")
        s_ms1 = m.sem("s_ms1")
        s_tq1 = m.sem("s_tq1")
        s_tk = m.sem("s_tk")
        s_tq2 = m.sem("s_tq2")
        s_to = m.sem("s_to")
        s_eq1 = m.sem("s_eq1")
        s_ek = m.sem("s_ek")
        s_eq2 = m.sem("s_eq2")
        s_eo = m.sem("s_eo")
        s_m1 = [m.sem(f"s_m1{u}") for u in range(2)]
        s_m2 = [m.sem(f"s_m2{u}") for u in range(2)]
        s_z = m.sem("s_z")
        s_k2 = [m.sem(f"s_k2{u}") for u in range(2)]
        s_s = m.sem("s_s")
        s_mx = m.sem("s_mx")
        s_p = m.sem("s_p")
        s_e = m.sem("s_e")
        s_pv = m.sem("s_pv")
        s_oe = m.sem("s_oe")
        s_ro = m.sem("s_ro")
        LEAD = 3
        NQ = 9
        block = st.enter_context(nc.Block())

        @block.sync
        def _(sp):
            def pair(i, u, h):
                if not isinstance(i, int) or i >= 2:
                    sp.wait_ge(s_vx, i - 1)
                for r, x in enumerate(("q", "k", "v")):
                    sp.dma_start(raw[:, u, r, :], A[x][:, ds(i, 1), :, :].rearrange("p o t w -> p (o t w)")
                                 ).then_inc(s_raw[u], 16)

            def copy_k(i, u, h):
                sp.wait_ge(s_ek, i + 1)
                if not isinstance(i, int) or i >= 2:
                    sp.wait_ge(s_p, 32 * i - 32)
                sp.dma_start(kT2[:, u, :], kT1[:, u, :]).then_inc(s_k2[u], 16)

            def copy_q(i, u, src, dst, out, done):
                sp.wait_ge(out, i + 1)
                for h in range(2):
                    r = slice(h * HR, (h + 1) * HR)
                    sp.dma_start(dst[r, u, h, :], src[r, u, :]).then_inc(done[u], 16)

            def copy_q1(i, u):
                copy_q(i, u, qT1, qm1, s_eq1, s_m1)

            def copy_q2(i, u):
                copy_q(i, u, qT2, qm2, s_eq2, s_m2)

            for i in range(2):
                pair(i, i, 0)
            sp.wait_ge(s_z, 2)
            copy_q1(0, 0)
            copy_k(0, 0, 0)
            pair(2, 0, 1)
            copy_q1(1, 1)
            copy_k(1, 1, 0)
            copy_q2(0, 0)
            with sp.Fori(0, PAIRS // 2 - 2) as k:
                for u in range(2):
                    pair(k * 2 + u + 3, 1 - u, k + 1)
                    copy_q1(k * 2 + u + 2, u)
                    copy_q2(k * 2 + u + 1, 1 - u)
                    copy_k(k * 2 + u + 2, u, 1)
            pair(PAIRS - 1, 1, None)
            copy_q1(PAIRS - 2, 0)
            copy_q2(PAIRS - 3, 1)
            copy_k(PAIRS - 2, 0, None)
            copy_q1(PAIRS - 1, 1)
            copy_q2(PAIRS - 2, 0)
            copy_k(PAIRS - 1, 1, None)
            copy_q2(PAIRS - 1, 1)
            for u in range(2):
                sp.wait_ge(s_k2[u], 16 * (PAIRS // 2))

        @block.gpsimd
        def _(pool):
            nc.gpsimd.memset(qx[:, :, :, :, KR:HR], 0.0).then_inc(s_c, 1)
            nc.gpsimd.memset(kx[:, :, :, :, KR:HR], 0.0).then_inc(s_c, 1)
            nc.gpsimd.memset(vx[:, :, :, :, :], 0.0).then_inc(s_c, 1)
            nc.gpsimd.memset(qm1[:, :, :, :], 0.0).then_inc(s_z, 1)
            nc.gpsimd.memset(qm2[:, :, :, :], 0.0).then_inc(s_z, 1)
            pool.wait_ge(s_c, 3)
            nc.gpsimd.memset(kx[:, :, :, :, KR:KM], 1.0).then_inc(s_c, 1)
            nc.gpsimd.memset(vx[:, :, :, :, DH:DH + 1], 1.0).then_inc(s_c, 1)
            pool.wait_ge(s_c, 5)

            def part(dst, src):
                zero = K["zero"][:, 0:1]
                for at, n in enumerate(src.shape[1:]):
                    zero = bcast(zero, at + 1, n)
                zero = bass.AP(zero.tensor, zero.offset, [list(x) for x in zero.ap][:-1])
                return nc.gpsimd.tensor_tensor(out=dst, in0=src, in1=zero, op=ALU.add)

            def build(i, u, h):
                if not isinstance(i, int) or i >= 2:
                    pool.wait_ge(s_tq2, i - 1)
                pool.wait_ge(s_raw[u], 48 * (h + 1))

                def step(k, ins):
                    ins.then_inc(s_q1, 1)
                    pool.wait_ge(s_q1, i * NQ + k)
                q = raw[:, u, 0, :].rearrange("p (g d) -> p g d", d=DH)
                kk = raw[:, u, 1, :].rearrange("p (g d) -> p g d", d=DH)
                qs = qx[:, u].rearrange("p t h (s d) -> p (t h) s d", d=DH)
                ks = kx[:, u].rearrange("p t h (s d) -> p (t h) s d", d=DH)
                step(1, part(qs[:, :, 0:3, :], bcast(q, 2, 3)))
                step(2, part(ks[:, :, 1:6:2, :], bcast(kk, 2, 3)))
                step(3, nc.gpsimd.tensor_tensor(out=r1[:, 0], in0=q, in1=qs[:, :, 0, :], op=ALU.subtract))
                step(4, nc.gpsimd.tensor_tensor(out=r1[:, 1], in0=kk, in1=ks[:, :, 1, :], op=ALU.subtract))
                step(5, part(qs[:, :, 3:5, :], bcast(r1[:, 0], 2, 2)))
                step(6, part(ks[:, :, 2:5:2, :], bcast(r1[:, 1], 2, 2)))
                step(7, nc.gpsimd.tensor_tensor(out=r1[:, 2], in0=r1[:, 0], in1=qs[:, :, 3, :], op=ALU.subtract))
                step(8, nc.gpsimd.tensor_tensor(out=r1[:, 3], in0=r1[:, 1], in1=ks[:, :, 2, :], op=ALU.subtract))
                step(9, part(qs[:, :, 5, :], r1[:, 2]))
                part(ks[:, :, 0, :], r1[:, 3]).then_inc(s_bld, 1)

            def build_v(i, u):
                if not isinstance(i, int) or i >= 2:
                    pool.wait_ge(s_pv, 8 * i - 6)
                part(vx[:, u].rearrange("p t h s -> p (t h) s")[:, :, 0:DH],
                     raw[:, u, 2, :].rearrange("p (g d) -> p g d", d=DH)).then_inc(s_vx, 1)

            def split_max(i, u):
                pool.wait_ge(s_tq1, i + 1)
                pool.wait_ge(s_mx, 16 * i + 18)

                def step(k, ins):
                    ins.then_inc(s_ms1, 1)
                    pool.wait_ge(s_ms1, i * 4 + k)
                n = negm[:, u].rearrange("p t h -> p (t h)")
                x = qx[:, u].rearrange("p t h s -> p (t h) s")
                step(1, part(x[:, :, KR], n))
                step(2, nc.gpsimd.tensor_tensor(out=mr[:, 0, :], in0=n, in1=x[:, :, KR], op=ALU.subtract))
                step(3, part(x[:, :, KR + 1], mr[:, 0, :]))
                step(4, nc.gpsimd.tensor_tensor(out=mr[:, 1, :], in0=mr[:, 0, :], in1=x[:, :, KR + 1],
                                                op=ALU.subtract))
                part(x[:, :, KR + 2], mr[:, 1, :]).then_inc(s_msp, 1)

            build(0, 0, 0)
            build_v(0, 0)
            build(1, 1, 0)
            build_v(1, 1)
            split_max(0, 0)
            with pool.Fori(1, PAIRS // 2) as k:
                for u in range(2):
                    build(k * 2 + u, u, k)
                    split_max(k * 2 + u - 1, 1 - u)
                    build_v(k * 2 + u, u)
            split_max(PAIRS - 1, 1)

        @block.vector
        def _(dve):
            m.seed(s_mx, 2)
            m.seed(s_e, 2)
            m.seed(s_pv, 2)
            m.seed(s_oe, 1)

            def maxima(i, u, t):
                if t == 0 and (not isinstance(i, int) or i >= 2):
                    dve.wait_ge(s_msp, i - 1)
                for h in range(2):
                    dve.wait_ge(s_s, 16 * i + 2 * t + h + 1)
                    nc.vector.tensor_reduce(out=negm[:, u, t, h:h + 1], in_=ps_s[:, h, :], axis=AX.X,
                                            op=ALU.max, negate=True).then_inc(s_mx, 1)

            def output(i, u):
                dve.wait_ge(s_to, i + 1)
                t = ps_t[:, :].rearrange("p (j h a s) -> p j h a s", j=4, h=2, a=2)
                nc.vector.reciprocal(ro[:, u].rearrange("p j (h a) -> p j h a", h=2), t[:, :, :, :, DH]
                                     ).then_inc(s_ro, 1)
                dve.wait_ge(s_ro, i + 1)
                for a in range(2):
                    src = t[:, :, :, a, 0:DH]
                    r = ro[:, u].rearrange("p j (h a) -> p j h a", h=2)[:, :, :, a]
                    o = O[:, ds(i, 1), 4 * a:4 * a + 4, :].rearrange("p o j (h d) -> p (o j) h d", d=DH)
                    nc.vector.tensor_tensor(out=o, in0=src, in1=bcast(r, 3, DH), op=ALU.mult
                                            ).then_inc(s_eo, 1)

            def pair(i, u, nxt, nxt2, prev):
                for s in range(8):
                    if s + LEAD < 8 and nxt:
                        maxima(i + 1, 1 - u, s + LEAD)
                    if s + LEAD >= 8 and nxt2:
                        maxima(i + 2, u, s + LEAD - 8)
                    if s == 1 and prev:
                        output(i - 1, 1 - u)

            for t in range(8):
                maxima(0, 0, t)
            for t in range(LEAD):
                maxima(1, 1, t)
            pair(0, 0, True, True, False)
            pair(1, 1, True, True, True)
            with dve.Fori(1, PAIRS // 2 - 1) as k:
                for u in range(2):
                    pair(k * 2 + u, u, True, True, True)
            pair(PAIRS - 2, 0, True, False, True)
            pair(PAIRS - 1, 1, False, False, True)
            output(PAIRS - 1, 1)

        @block.scalar
        def _(act):
            def evac_q1(i, u, hh=None):
                if hh is not None:
                    act.wait_ge(s_m1[u], 32 * hh)
                act.wait_ge(s_tq1, i + 1)
                nc.scalar.activation(qT1[:, u, :], tb[:, :], ACT.Copy).then_inc(s_eq1, 1)

            def evac_k(i, u, h):
                if h is not None:
                    act.wait_ge(s_k2[u], 16 * h)
                act.wait_ge(s_tk, i + 1)
                nc.scalar.activation(kT1[:, u, :], tb[:, :], ACT.Copy).then_inc(s_ek, 1)

            def evac_q2(i, u, hh=None):
                if hh is not None:
                    act.wait_ge(s_m2[u], 32 * hh)
                act.wait_ge(s_tq2, i + 1)
                nc.scalar.activation(qT2[:, u, :], tb[:, :], ACT.Copy).then_inc(s_eq2, 1)

            def evac_o(i, u):
                act.wait_ge(s_pv, 8 * i + 10)
                nc.scalar.activation(oT[:, u, :], ps_o[:, :], ACT.Copy).then_inc(s_oe, 1)

            def exps(i, u, s):
                if True:
                    act.wait_ge(s_pv, 8 * i + s + 1)
                for n in range(4):
                    h, half = n % 2, n // 2
                    act.wait_ge(s_p, 32 * i + 4 * s + n + 1)
                    nc.scalar.activation(pT[:, (s % 2) * 4 + n, :], ps_p[:, h, :], ACT.Exp,
                                         scale=SCALE).then_inc(s_e, 1)

            def pair(i, u, h, nxt, nxt2):
                for s in range(8):
                    exps(i, u, s)
                    if s == 3 and nxt2:
                        evac_q1(i + 2, u, h + 1)
                    if s == 4 and nxt2:
                        evac_k(i + 2, u, h + 1)
                    if s == 6 and nxt:
                        evac_q2(i + 1, 1 - u, h + u)
                evac_o(i, u)

            evac_q1(0, 0)
            evac_k(0, 0, None)
            evac_q1(1, 1)
            evac_k(1, 1, None)
            evac_q2(0, 0)
            pair(0, 0, 0, True, True)
            pair(1, 1, 0, True, True)
            with act.Fori(1, PAIRS // 2 - 1) as k:
                for u in range(2):
                    pair(k * 2 + u, u, k, True, True)
            pair(PAIRS - 2, 0, PAIRS // 2 - 1, True, False)
            pair(PAIRS - 1, 1, None, False, False)

        @block.tensor
        def _(pe):
            def rows(h, n):
                return slice(h * HR, h * HR + n)

            def transposes(src, u):
                for t in range(G8):
                    last = nc.tensor.transpose(tb[:, t * P:(t + 1) * P],
                                               src[:, u, t].rearrange("p h s -> p (h s)"), identb[:, :])
                return last

            def q1(i, u, before):
                for s, v in before:
                    pe.wait_ge(s, v)
                pe.wait_ge(s_bld, i + 1)
                transposes(qx, u).then_inc(s_tq1, 1)

            def k1(i, u):
                pe.wait_ge(s_eq1, i + 1)
                transposes(kx, u).then_inc(s_tk, 1)

            def q2(i, u, before):
                pe.wait_ge(*before)
                pe.wait_ge(s_msp, i + 1)
                transposes(qx, u).then_inc(s_tq2, 1)

            def o1(i, u, before):
                pe.wait_ge(*before)
                pe.wait_ge(s_oe, i + 2)
                for j in range(4):
                    last = nc.tensor.transpose(ps_t[:, j * P:(j + 1) * P], oT[:, u, j * P:(j + 1) * P], ident[:, :])
                last.then_inc(s_to, 1)

            def by_query(i, u, hh, t):
                if t == 0:
                    pe.wait_ge(s_m1[u], 32 * (hh + 1))
                    pe.wait_ge(s_ek, i + 1)
                for h in range(2):
                    pe.wait_ge(s_mx, 16 * i + 2 * t + h + 1)
                    for half in range(2):
                        mm = nc.tensor.matmul(ps_s[:, h, half * CW:(half + 1) * CW],
                                              qm1[:, u, h, t * P:(t + 1) * P],
                                              kT1[:, u, half * CW:(half + 1) * CW],
                                              start=True, stop=True)
                    mm.then_inc(s_s, 1)

            def by_key(i, u, hh, s, half):
                if s == 0 and half == 0:
                    pe.wait_ge(s_m2[u], 32 * (hh + 1))
                    pe.wait_ge(s_k2[u], 16 * (hh + 1))
                for h in range(2):
                    n = 2 * half + h
                    pe.wait_ge(s_e, 32 * i + 4 * s + n + 1)
                    nc.tensor.matmul(ps_p[:, h, :], kT2[:, u, s * P:(s + 1) * P],
                                     qm2[:, u, h, half * CW:(half + 1) * CW],
                                     start=True, stop=True).then_inc(s_p, 1)

            def values(i, u, s):
                if s == 0:
                    pe.wait_ge(s_vx, i + 1)
                    pe.wait_ge(s_oe, i + 1)
                pe.wait_ge(s_e, 32 * i + 4 * s + 6)
                for n in range(4):
                    h, half = n % 2, n // 2
                    g = 32 * (2 * h + half)
                    last = nc.tensor.matmul(ps_o[g:g + 32, :], vx[:, u, s, h, :], pT[:, (s % 2) * 4 + n, :],
                                            start=(s == 0), stop=(s == 7))
                last.then_inc(s_pv, 1)

            def pair(i, u, hh, nxt, nxt2, prev):
                for s in range(8):
                    by_key(i, u, hh, s, 0)
                    if s + LEAD < 8 and nxt:
                        by_query(i + 1, 1 - u, hh + u, s + LEAD)
                    if s + LEAD >= 8 and nxt2:
                        by_query(i + 2, u, hh + 1, s + LEAD - 8)
                    by_key(i, u, hh, s, 1)
                    if s:
                        values(i, u, s - 1)
                    if s == 1 and prev:
                        o1(i - 1, 1 - u, (s_eq2, i + 1))
                    if s == 3 and nxt2:
                        q1(i + 2, u, [(s_eo, 2 * i)] if prev else [(s_eq2, i + 1)])
                    if s == 4 and nxt2:
                        k1(i + 2, u)
                    if s == 6 and nxt:
                        q2(i + 1, 1 - u, (s_ek, i + 3) if nxt2 else (s_eo, 2 * i))
                values(i, u, 7)

            q1(0, 0, [])
            k1(0, 0)
            for t in range(8):
                by_query(0, 0, 0, t)
            q1(1, 1, [(s_ek, 1)])
            k1(1, 1)
            for t in range(LEAD):
                by_query(1, 1, 0, t)
            q2(0, 0, (s_ek, 2))
            pair(0, 0, 0, True, True, False)
            pair(1, 1, 0, True, True, True)
            with pe.Fori(1, PAIRS // 2 - 1) as k:
                for u in range(2):
                    pair(k * 2 + u, u, k, True, True, True)
            pair(PAIRS - 2, 0, PAIRS // 2 - 1, True, False, True)
            pair(PAIRS - 1, 1, PAIRS // 2 - 1, False, False, True)
            o1(PAIRS - 1, 1, (s_eo, 2 * (PAIRS - 1)))


def stage_project(nc, sems, W, K, A):
    X, ident, O = K["X"], K["ident"], A["o"]
    st = ExitStack()
    with st:
        m = Pool_(nc, st, sems, "wo")
        w = m.sb("w", [P, D])
        oc = m.sb("oc", [P, 2, CT, D])
        oT = m.sb("oT", [P, 2, CW])
        ps_t = m.ps("ps_t", [P, 2, CW])
        ps_y = m.ps("ps_y", [P, 2, CT, D])
        s_w = m.sem("s_w")
        s_oc = m.sem("s_oc")
        s_t = m.sem("s_t")
        s_oT = m.sem("s_oT")
        s_y = m.sem("s_y")
        s_x = m.sem("s_x")
        block = st.enter_context(nc.Block())

        @block.sync
        def _(sp):
            sp.dma_start(w[:, :], W["wo"]).then_inc(s_w, 16)
            sp.wait_ge(s_w, 16)

        @block.gpsimd
        def _(pool):
            with pool.Fori(0, CHUNKS // 2) as k:
                for u in range(2):
                    c = k * 2 + u
                    pool.wait_ge(s_t, c + 1)
                    for j in range(CT):
                        nc.gpsimd.tensor_tensor(out=oc[:, u, j, :].rearrange("p (h w) -> p h w", w=16),
                                                in0=O[:, ds(k * 8, 8), 4 * u + j, :],
                                                in1=bcast(bcast(K["zero"][:, 0:1], 1, 8), 2, 16)[:, :, :, 0],
                                                op=ALU.add).then_inc(s_oc, 1)

        @block.tensor
        def _(pe):
            pe.wait_ge(s_w, 16)
            with pe.Fori(0, CHUNKS // 2) as k:
                for u in range(2):
                    c = k * 2 + u
                    pe.wait_ge(s_oc, 4 * c + 4)
                    pe.wait_ge(s_oT, c + 1)
                    for j in range(CT):
                        last = nc.tensor.transpose(ps_t[:, u, j * P:(j + 1) * P], oc[:, u, j, :], ident[:, :])
                    last.then_inc(s_t, 1)
                    pe.wait_ge(s_oT, c + 3)
                    pe.wait_ge(s_x, c + 1)
                    for j in range(CT):
                        last = nc.tensor.matmul(ps_y[:, u, j, :], oT[:, u, j * P:(j + 1) * P], w[:, :],
                                                start=True, stop=True)
                    last.then_inc(s_y, 1)

        @block.scalar
        def _(act):
            with act.Fori(0, CHUNKS // 2) as k:
                for u in range(2):
                    c = k * 2 + u
                    act.wait_ge(s_y, c + 1)
                    act.wait_ge(s_t, c + 3)
                    nc.scalar.activation(oT[:, u, :], ps_t[:, u, :], ACT.Copy).then_inc(s_oT, 1)

        @block.vector
        def _(dve):
            m.seed(s_t, 2)
            m.seed(s_oT, 2)
            m.seed(s_x, 2)
            m.seed(s_y, 2)
            with dve.Fori(0, CHUNKS // 2) as k:
                for u in range(2):
                    c = k * 2 + u
                    dve.wait_ge(s_y, c + 3)
                    xc = X[:, ds(c * CT, CT), :]
                    nc.vector.tensor_tensor(out=xc, in0=ps_y[:, u], in1=xc, op=ALU.add).then_inc(s_x, 1)




EX, TOPK, HID, CAP = 64, 8, 96, 32
SLOTS_X = EX * CAP
ST = SLOTS_X // P
FAR = 1000.0


def stage_route(nc, sems, tag, K, M, S):
    X, ident = K["X"], K["ident"]
    pos, wt, H, nact = S["pos"], S["wt"], S["H"], S["nact"]
    st = ExitStack()
    with st:
        m = Pool_(nc, st, sems, tag)
        norm = Norm(m, X, ident)
        lmax = m.sb("lmax", [P, CT])
        ls = m.sb("ls", [P, CT, EX])
        ex = m.sb("ex", [P, CT, EX])
        sm = m.sb("sm", [P, CT])
        rs = m.sb("rs", [P, CT])
        pr = m.sb("pr", [P, CT, EX])
        v8 = m.sb("v8", [P, CT, TOPK])
        rest = m.sb("rest", [P, CT, EX])
        mask = m.sb("mask", [P, CT, EX], BF16)
        s8 = m.sb("s8", [P, CT])
        r8 = m.sb("r8", [P, CT])
        pt = m.sb("pt", [P, CT, EX])
        carry = m.sb("carry", [P, EX])
        low = m.sb("low", [P, 1])
        open_ = m.sb("open", [P, 1])
        cnt = m.sb("cnt", [P, 1])
        ps_tr = m.ps("ps_tr", [P, CW])
        ps_lg = m.ps("ps_lg", [P, CT, EX])
        ps_c = m.ps("ps_c", [P, CT, EX])
        ps_n = m.ps("ps_n", [P, EX])
        s_lg = m.sem("s_lg")
        s_d = m.sem("s_d")
        s_ls = m.sem("s_ls")
        s_ex = m.sem("s_ex")
        s_mk = m.sem("s_mk")
        s_c = m.sem("s_c")
        s_h = [m.sem("s_h0"), m.sem("s_h1")]
        block = st.enter_context(nc.Block())
        STEPS = 21

        @block.sync
        def _(sp):
            with sp.Fori(0, CHUNKS // 2) as k:
                for u in range(2):
                    c = k * 2 + u
                    sp.wait_ge(norm.s_h, (c + 1) * CT)
                    sp.dma_start(H[:, ds(c * CT, CT), :], norm.h[:, u]).then_inc(s_h[u], 16)
            sp.wait_ge(s_h[0], CHUNKS // 2 * 16)
            sp.wait_ge(s_h[1], CHUNKS // 2 * 16 + 16)

        @block.vector
        def _(dve):
            norm.dve_eps(nc)
            m.seed(s_h[1], 16)
            nc.vector.memset(carry[:, :], FAR).then_inc(s_d, 1)
            nc.vector.memset(cnt[:, :], 0.0).then_inc(s_d, 1)
            norm.dve_stats(nc, 0, 0)
            norm.dve_apply(nc, 0, 0)

            def chunk(k, u, more):
                c = k * 2 + u
                base = c * STEPS + 2

                def step(i, ins):
                    ins.then_inc(s_d, 1)
                    dve.wait_ge(s_d, base + i)

                def tick():
                    nc.vector.memset(norm.tick[:, :], 0.0)
                dve.wait_ge(s_d, c * STEPS + 2)
                step(1, nc.vector.tensor_reduce(out=low[:, :], in_=carry[:, :], axis=AX.X, op=ALU.min))
                step(2, nc.vector.tensor_scalar(out=open_[:, :], in0=low[:, :], scalar1=FAR + CAP, scalar2=None,
                                                op0=ALU.is_lt))
                step(3, nc.vector.tensor_tensor(out=cnt[:, :], in0=cnt[:, :], in1=open_[:, :], op=ALU.add))
                dve.wait_ge(s_lg, c + 1)
                step(4, nc.vector.tensor_reduce(out=lmax[:, :], in_=ps_lg[:, :, :], axis=AX.X, op=ALU.max))
                nc.vector.tensor_tensor(out=ls[:, :, :], in0=ps_lg[:, :, :], in1=bcast(lmax[:, :], 2, EX),
                                        op=ALU.subtract).then_inc(s_ls, 1)
                if more:
                    norm.dve_stats(nc, c + 1, 1 - u)
                dve.wait_ge(s_ex, c + 1)
                step(5, nc.vector.tensor_reduce(out=sm[:, :], in_=ex[:, :, :], axis=AX.X, op=ALU.add))
                step(6, nc.vector.reciprocal(rs[:, :], sm[:, :]))
                step(7, nc.vector.tensor_tensor(out=pr[:, :, :], in0=ex[:, :, :], in1=bcast(rs[:, :], 2, EX),
                                                op=ALU.mult))
                tick()
                for j in range(CT):
                    nc.vector.max(v8[:, j, :], pr[:, j, :]).then_inc(s_d, 1)
                dve.wait_ge(s_d, base + 11)
                tick()
                for j in range(CT):
                    nc.vector.match_replace(out=rest[:, j, :], in_to_replace=v8[:, j, :], in_values=pr[:, j, :],
                                            imm_value=-1.0).then_inc(s_d, 1)
                dve.wait_ge(s_d, base + 15)
                nc.vector.tensor_scalar(out=mask[:, :, :], in0=rest[:, :, :], scalar1=0.0, scalar2=None,
                                        op0=ALU.is_lt).then_inc(s_mk, 1)
                step(16, nc.vector.tensor_reduce(out=s8[:, :], in_=v8[:, :, :], axis=AX.X, op=ALU.add))
                step(17, nc.vector.reciprocal(r8[:, :], s8[:, :]))
                step(18, nc.vector.tensor_tensor(out=wt[:, ds(c * CT, CT), :], in0=pr[:, :, :],
                                                 in1=bcast(r8[:, :], 2, EX), op=ALU.mult))
                if more:
                    dve.wait_ge(s_h[1 - u], (k + 1) * 16)
                    norm.dve_apply(nc, c + 1, 1 - u)
                dve.wait_ge(s_mk, c + 1)
                dve.wait_ge(s_c, c + 1)
                step(19, nc.vector.scalar_tensor_tensor(out=pt[:, :, :], in0=mask[:, :, :], scalar=-FAR,
                                                        in1=ps_c[:, :, :], op0=ALU.mult, op1=ALU.add))
                step(20, nc.vector.tensor_tensor(out=pos[:, ds(c * CT, CT), :], in0=pt[:, :, :],
                                                 in1=bcast(carry[:, :], 1, CT), op=ALU.add))
                step(21, nc.vector.tensor_tensor(out=carry[:, :], in0=ps_n[:, :], in1=carry[:, :], op=ALU.add))

            with dve.Fori(0, CHUNKS // 2 - 1) as k:
                for u in range(2):
                    chunk(k, u, True)
            chunk(CHUNKS // 2 - 1, 0, True)
            chunk(CHUNKS // 2 - 1, 1, False)
            nc.vector.tensor_copy(nact[:, :], cnt[:, :])

        @block.scalar
        def _(act):
            act.wait_ge(norm.s_eps, 1)
            norm.act_std(nc, 0, 0)
            norm.act_hT(nc, 0, 0, ps_tr)

            def chunk(c, u, more):
                act.wait_ge(s_ls, c + 1)
                nc.scalar.activation(ex[:, :, :], ls[:, :, :], ACT.Exp).then_inc(s_ex, 1)
                if more:
                    norm.act_std(nc, c + 1, 1 - u)
                    norm.act_hT(nc, c + 1, 1 - u, ps_tr)

            with act.Fori(0, CHUNKS // 2 - 1) as k:
                for u in range(2):
                    chunk(k * 2 + u, u, True)
            chunk(CHUNKS - 2, 0, True)
            chunk(CHUNKS - 1, 1, False)

        @block.tensor
        def _(pe):
            norm.pe_transpose(nc, 0, 0, ps_tr)

            def chunk(c, u, more):
                pe.wait_ge(norm.s_hT, c + 1)
                pe.wait_ge(s_d, c * STEPS + 2)
                for s in range(CT):
                    last = nc.tensor.matmul(ps_lg[:, s, :], norm.hT[:, u, s * P:(s + 1) * P], M["wr"][:, :],
                                            start=True, stop=True)
                last.then_inc(s_lg, 1)
                if more:
                    norm.pe_transpose(nc, c + 1, 1 - u, ps_tr)
                pe.wait_ge(s_mk, c + 1)
                nc.tensor.matmul(ps_c[:, :, :], K["triub"][:, :], mask[:, :, :], start=True, stop=False,
                                 skip_group_check=True)
                for j in range(1, CT):
                    nc.tensor.matmul(ps_c[:, j:CT, :], K["onesb"][:, :],
                                     mask[:, 0:CT - j, :], start=False, stop=(j == CT - 1),
                                     skip_group_check=True)
                for j in range(CT):
                    last = nc.tensor.matmul(ps_n[:, :], K["onesb"][:, :], mask[:, j, :], start=(j == 0),
                                            stop=(j == CT - 1))
                last.then_inc(s_c, 1)

            with pe.Fori(0, CHUNKS // 2 - 1) as k:
                for u in range(2):
                    chunk(k * 2 + u, u, True)
            chunk(CHUNKS - 2, 0, True)
            chunk(CHUNKS - 1, 1, False)


def stage_dispatch(nc, sems, tag, K, S):
    pos, H, XT = S["pos"], S["H"], S["XT"]
    st = ExitStack()
    with st:
        m = Pool_(nc, st, sems, tag)
        hc = m.sb("hc", [P, CT * D])
        hp = m.sb("hp", [P, 3, CT * D], BF16)
        r = m.sb("r", [P, 2, CT * D])
        oh = m.sb("oh", [P, CT, EX, CAP], BF16)
        ps_x = m.ps("ps_x", [P, 4, CW])
        s_h = m.sem("s_h")
        s_p = m.sem("s_p")
        s_oh = m.sem("s_oh")
        s_x = m.sem("s_x")
        s_xa = m.sem("s_xa")
        s_z = m.sem("s_z")
        block = st.enter_context(nc.Block())

        @block.sync
        def _(sp):
            n = sp.value_load(S["nact"][0:1, 0:1], min_val=1, max_val=CHUNKS)
            with sp.Fori(0, n) as c:
                sp.wait_ge(s_xa, c * 4 + 4)
                sp.dma_start(hc[:, :], H[:, ds(c * CT, CT), :].rearrange("p t d -> p (t d)")).then_inc(s_h, 16)

        @block.gpsimd
        def _(pool):
            n = pool.value_load(S["nact"][0:1, 0:1], min_val=1, max_val=CHUNKS)
            zero = bcast(K["zero"][:, 0:1], 1, CT * D)[:, :, 0]
            with pool.Fori(0, n) as c:
                def step(k, ins):
                    ins.then_inc(s_p, 1)
                    pool.wait_ge(s_p, c * 5 + k)
                pool.wait_ge(s_h, c * 16 + 16)
                step(1, nc.gpsimd.tensor_tensor(out=hp[:, 0, :], in0=hc[:, :], in1=zero, op=ALU.add))
                step(2, nc.gpsimd.tensor_tensor(out=r[:, 0, :], in0=hc[:, :], in1=hp[:, 0, :], op=ALU.subtract))
                step(3, nc.gpsimd.tensor_tensor(out=hp[:, 1, :], in0=r[:, 0, :], in1=zero, op=ALU.add))
                step(4, nc.gpsimd.tensor_tensor(out=r[:, 1, :], in0=r[:, 0, :], in1=hp[:, 1, :], op=ALU.subtract))
                step(5, nc.gpsimd.tensor_tensor(out=hp[:, 2, :], in0=r[:, 1, :], in1=zero, op=ALU.add))

        @block.vector
        def _(dve):
            nc.vector.memset(XT[:, :], 0.0).then_inc(s_z, 1)
            m.seed(s_xa, 4)
            dve.wait_ge(s_z, 1)
            n = dve.value_load(S["nact"][0:1, 0:1], min_val=1, max_val=CHUNKS)
            with dve.Fori(0, n) as c:
                dve.wait_ge(s_xa, c * 4 + 4)
                for j in range(CT):
                    row = pos[:, ds(c * CT + j, 1), :].rearrange("p o e -> p (o e)")
                    nc.vector.tensor_tensor(out=oh[:, j], in0=bcast(row, 2, CAP),
                                            in1=bcast(K["iota"][:, :], 1, EX), op=ALU.is_equal).then_inc(s_oh, 1)
                for q in range(4):
                    dve.wait_ge(s_x, c * 4 + q + 1)
                    nc.vector.tensor_tensor(out=XT[:, q * CW:(q + 1) * CW], in0=ps_x[:, q, :],
                                            in1=XT[:, q * CW:(q + 1) * CW], op=ALU.add).then_inc(s_xa, 1)

        @block.tensor
        def _(pe):
            n = pe.value_load(S["nact"][0:1, 0:1], min_val=1, max_val=CHUNKS)
            with pe.Fori(0, n) as c:
                pe.wait_ge(s_p, c * 5 + 5)
                pe.wait_ge(s_oh, c * 4 + 4)
                for q in range(4):
                    for j in range(CT):
                        for a in range(3):
                            last = nc.tensor.matmul(
                                ps_x[:, q, :], hp[:, a, j * D:(j + 1) * D],
                                oh[:, j].rearrange("p e c -> p (e c)")[:, q * CW:(q + 1) * CW],
                                start=(j == 0 and a == 0), stop=(j == CT - 1 and a == 2))
                    last.then_inc(s_x, 1)


def stage_experts(nc, sems, tag, M, S):
    XT, ysb = S["XT"], S["y"]
    wg, wu, wd = M["wg"], M["wu"], M["wd"]
    st = ExitStack()
    with st:
        m = Pool_(nc, st, sems, tag)
        sg = m.sb("sg", [HID, 4, CW])
        gu = m.sb("gu", [HID, 4, CW])
        ps_g = m.ps("ps_g", [HID, 2, CW])
        ps_u = m.ps("ps_u", [HID, 2, CW])
        ps_y = m.ps("ps_y", [P, 2, 4, D])
        s_gu = m.sem("s_gup")
        s_s = m.sem("s_s")
        s_g = m.sem("s_g")
        s_y = m.sem("s_y")
        s_ye = m.sem("s_ye")
        block = st.enter_context(nc.Block())

        @block.tensor
        def _(pe):
            def up(q):
                if q >= 2:
                    pe.wait_ge(s_g, q - 1)
                for e in range(16):
                    x = XT[:, q * CW + e * CAP:q * CW + (e + 1) * CAP]
                    nc.tensor.matmul(ps_g[:, q % 2, e * CAP:(e + 1) * CAP], wg[:, q * 16 + e, :], x,
                                     start=True, stop=True)
                    last = nc.tensor.matmul(ps_u[:, q % 2, e * CAP:(e + 1) * CAP], wu[:, q * 16 + e, :], x,
                                            start=True, stop=True)
                last.then_inc(s_gu, 1)

            def down(q):
                pe.wait_ge(s_g, q + 1)
                if q >= 2:
                    pe.wait_ge(s_ye, q - 1)
                for t in range(4):
                    for e in range(4):
                        n = t * 4 + e
                        last = nc.tensor.matmul(ps_y[e * CAP:(e + 1) * CAP, q % 2, t, :],
                                                gu[:, q, n * CAP:(n + 1) * CAP], wd[:, q * 16 + n, :],
                                                start=True, stop=True)
                last.then_inc(s_y, 1)

            for q in range(4):
                up(q)
                if q:
                    down(q - 1)
            down(3)

        @block.scalar
        def _(act):
            for q in range(4):
                act.wait_ge(s_gu, q + 1)
                nc.scalar.activation(sg[:, q, :], ps_g[:, q % 2, :], ACT.Silu).then_inc(s_s, 1)

        @block.vector
        def _(dve):
            for q in range(4):
                dve.wait_ge(s_s, q + 1)
                nc.vector.tensor_tensor(out=gu[:, q, :], in0=ps_u[:, q % 2, :], in1=sg[:, q, :],
                                        op=ALU.mult).then_inc(s_g, 1)
                if q:
                    dve.wait_ge(s_y, q)
                    nc.vector.tensor_copy(ysb[:, 4 * q - 4:4 * q, :], ps_y[:, (q - 1) % 2]).then_inc(s_ye, 1)
            dve.wait_ge(s_y, 4)
            nc.vector.tensor_copy(ysb[:, 12:16, :], ps_y[:, 1]).then_inc(s_ye, 1)


def stage_combine(nc, sems, tag, K, S):
    X, ident = K["X"], K["ident"]
    pos, wt, ysb = S["pos"], S["wt"], S["y"]
    st = ExitStack()
    with st:
        m = Pool_(nc, st, sems, tag)
        oh = m.sb("oh", [P, 2, EX, CAP])
        wT = m.sb("wT", [P, 4, CW])
        ps_t = m.ps("ps_t", [P, 4, CW])
        ps_o = m.ps("ps_o", [P, D])
        s_e = m.sem("s_e")
        s_w = m.sem("s_w")
        s_t = m.sem("s_t")
        s_v = m.sem("s_v")
        s_o = m.sem("s_o")
        s_x = m.sem("s_x")
        block = st.enter_context(nc.Block())

        @block.vector
        def _(dve):
            m.seed(s_t, 4)
            m.seed(s_v, 4)
            m.seed(s_o, 1)
            m.seed(s_x, 1)
            n = dve.value_load(S["nact"][0:1, 0:1], min_val=1, max_val=CHUNKS)
            with dve.Fori(0, n) as c:
                for j in range(CT):
                    t, v = c * CT + j, j % 2
                    row = pos[:, ds(t, 1), :].rearrange("p o e -> p (o e)")
                    w = wt[:, ds(t, 1), :].rearrange("p o e -> p (o e)")
                    dve.wait_ge(s_t, 4 * t + 4)
                    nc.vector.tensor_tensor(out=oh[:, 0], in0=bcast(row, 2, CAP),
                                            in1=bcast(K["iota"][:, :], 1, EX), op=ALU.is_equal).then_inc(s_e, 1)
                    dve.wait_ge(s_e, t + 1)
                    nc.vector.tensor_tensor(out=oh[:, 1], in0=oh[:, 0], in1=bcast(w, 2, CAP),
                                            op=ALU.mult).then_inc(s_w, 1)
                    dve.wait_ge(s_o, t + 2)
                    xt = X[:, ds(t, 1), :].rearrange("p o d -> p (o d)")
                    nc.vector.scalar_tensor_tensor(out=xt, in0=ps_o[:, :], scalar=0.5, in1=xt, op0=ALU.mult,
                                                   op1=ALU.add).then_inc(s_x, 1)

        @block.scalar
        def _(act):
            n = act.value_load(S["nact"][0:1, 0:1], min_val=1, max_val=CHUNKS)
            with act.Fori(0, n) as c:
                for j in range(CT):
                    t = c * CT + j
                    act.wait_ge(s_o, t + 1)
                    for q in range(4):
                        act.wait_ge(s_t, 4 * t + q + 5)
                        nc.scalar.activation(wT[:, q, :], ps_t[:, q, :], ACT.Copy).then_inc(s_v, 1)

        @block.tensor
        def _(pe):
            n = pe.value_load(S["nact"][0:1, 0:1], min_val=1, max_val=CHUNKS)
            with pe.Fori(0, n) as c:
                for j in range(CT):
                    t = c * CT + j
                    pe.wait_ge(s_w, t + 1)
                    flat = oh[:, 1].rearrange("p e c -> p (e c)")
                    for q in range(4):
                        pe.wait_ge(s_v, 4 * t + q + 1)
                        for s in range(4):
                            last = nc.tensor.transpose(ps_t[:, q, s * P:(s + 1) * P],
                                                       flat[:, (q * 4 + s) * P:(q * 4 + s + 1) * P], ident[:, :])
                        last.then_inc(s_t, 1)
                    pe.wait_ge(s_v, 4 * t + 8)
                    pe.wait_ge(s_x, t + 1)
                    for s in range(ST):
                        last = nc.tensor.matmul(ps_o[:, :], wT[:, s // 4, (s % 4) * P:(s % 4 + 1) * P], ysb[:, s, :],
                                                start=(s == 0), stop=(s == ST - 1))
                    last.then_inc(s_o, 1)


def moe(nc, sems, tag, K, M):
    st = ExitStack()
    with st:
        m = Pool_(nc, st, sems, tag)
        S = {"pos": m.sb("pos", [P, TILES, EX]), "wt": m.sb("wt", [P, TILES, EX]), "y": m.sb("y", [P, ST, D]),
             "nact": m.sb("nact", [P, 1], I32)}
        mid = ExitStack()
        with mid:
            m2 = Pool_(nc, mid, sems, tag + "m")
            S["XT"] = m2.sb("XT", [P, SLOTS_X])
            early = ExitStack()
            with early:
                S["H"] = Pool_(nc, early, sems, tag + "e").sb("H", [P, TILES, D])
                stage_route(nc, sems, tag + "r", K, M, S)
                stage_dispatch(nc, sems, tag + "d", K, S)
            stage_experts(nc, sems, tag + "x", M, S)
        stage_combine(nc, sems, tag + "c", K, S)


LEVELS = [N + 1] + [N >> k for k in range(1, 11)]
SCAN_EPS = 1e-8
LIFT = (3.4445, -4.7750, 2.0315)
POLISH = (1.875, -1.25, 0.375)
LIFTS, POLISHES = 14, 4


def stage_polar(nc, sems, W, K, Q):
    Y = Q["Y"]
    st = ExitStack()
    with st:
        m = Pool_(nc, st, sems, "po")
        X = m.sb("X", [P, 2, P])
        sq = m.sb("sq", [P, 2, P])
        rowsum = m.sb("rowsum", [P, 2])
        norm = m.sb("norm", [P, 2])
        inv = m.sb("inv", [P, 2])
        A = m.sb("A", [P, 2, P])
        TT = m.sb("TT", [P, 2, P])
        C = m.sb("C", [P, 2, P])
        aI = m.sb("aI", [P, 2, P])
        ps_n = m.ps("ps_n", [P, 2])
        ps_a = [m.ps(f"ps_a{w}", [P, P]) for w in range(2)]
        ps_x = [m.ps(f"ps_x{w}", [P, P]) for w in range(2)]
        ps_y = [m.ps(f"ps_y{w}", [P, P]) for w in range(2)]
        s_w = m.sem("s_w")
        s_i = m.sem("s_i")
        s_sq = m.sem("s_sq")
        s_n = m.sem("s_n")
        s_rt = m.sem("s_rt")
        s_iv = m.sem("s_iv")
        s_x0 = m.sem("s_x0")
        s_a = m.sem("s_a")
        s_as = m.sem("s_as")
        s_t = m.sem("s_t")
        s_a2 = m.sem("s_a2")
        s_c = m.sem("s_c")
        s_xy = m.sem("s_xy")
        s_xs = m.sem("s_xs")
        s_ys = m.sem("s_ys")
        block = st.enter_context(nc.Block())

        @block.sync
        def _(sp):
            for w in range(2):
                sp.dma_start(X[:, w, :], W["wp"][w]).then_inc(s_w, 16)
                sp.dma_start(Y[:, w, :], W["wpt"][w]).then_inc(s_w, 16)
            sp.wait_ge(s_w, 64)

        @block.scalar
        def _(act):
            act.wait_ge(s_w, 64)
            for w in range(2):
                nc.scalar.activation(sq[:, w, :], X[:, w, :], ACT.Square,
                                     accum_out=rowsum[:, w:w + 1]).then_inc(s_sq, 1)
            act.wait_ge(s_n, 1)
            nc.scalar.activation(norm[:, :], ps_n[:, :], ACT.Sqrt).then_inc(s_rt, 1)

            def step(n):
                for w in range(2):
                    act.wait_ge(s_a, 2 * n + w + 1)
                    nc.scalar.activation(A[:, w, :], ps_a[w][:, :], ACT.Copy).then_inc(s_as, 1)
                for w in range(2):
                    act.wait_ge(s_xy, 2 * n + w + 1)
                    nc.scalar.activation(X[:, w, :], ps_x[w][:, :], ACT.Copy).then_inc(s_xs, 1)
            with act.Fori(0, LIFTS + POLISHES) as n:
                step(n)

        @block.vector
        def _(dve):
            m.seed(s_c, 2)
            m.seed(s_xs, 2)
            m.seed(s_ys, 2)
            for k, (a, _, _) in enumerate((LIFT, POLISH)):
                nc.vector.tensor_scalar_mul(aI[:, k, :], K["ident"][:, :], a).then_inc(s_i, 1)
            dve.wait_ge(s_rt, 1)
            nc.vector.reciprocal(inv[:, :], norm[:, :]).then_inc(s_iv, 1)
            dve.wait_ge(s_iv, 1)
            for w in range(2):
                for z in (X, Y):
                    nc.vector.tensor_scalar(out=z[:, w, :], in0=z[:, w, :], scalar1=inv[:, w:w + 1], scalar2=None,
                                            op0=ALU.mult).then_inc(s_x0, 1)
            dve.wait_ge(s_i, 2)

            def step(n, k, b, c):
                for w in range(2):
                    dve.wait_ge(s_as, 2 * n + w + 1)
                    nc.vector.scalar_tensor_tensor(out=TT[:, w, :], in0=ps_a[w][:, :], scalar=b,
                                                   in1=aI[:, k, :], op0=ALU.mult, op1=ALU.add).then_inc(s_t, 1)
                for w in range(2):
                    dve.wait_ge(s_t, 2 * n + w + 1)
                    dve.wait_ge(s_a2, 2 * n + w + 1)
                    nc.vector.scalar_tensor_tensor(out=C[:, w, :], in0=ps_a[w][:, :], scalar=c, in1=TT[:, w, :],
                                                   op0=ALU.mult, op1=ALU.add).then_inc(s_c, 1)
                for w in range(2):
                    dve.wait_ge(s_xy, 2 * n + w + 1)
                    nc.vector.tensor_copy(Y[:, w, :], ps_y[w][:, :]).then_inc(s_ys, 1)
            with dve.Fori(0, LIFTS) as n:
                step(n, 0, LIFT[1], LIFT[2])
            with dve.Fori(LIFTS, LIFTS + POLISHES) as n:
                step(n, 1, POLISH[1], POLISH[2])

        @block.tensor
        def _(pe):
            pe.wait_ge(s_sq, 2)
            nc.tensor.matmul(ps_n[:, :], K["ones"][:, :], rowsum[:, :], start=True, stop=True).then_inc(s_n, 1)
            pe.wait_ge(s_x0, 4)
            with pe.Fori(0, LIFTS + POLISHES) as n:
                pe.wait_ge(s_xs, 2 * n + 2)
                pe.wait_ge(s_c, 2 * n + 2)
                for w in range(2):
                    nc.tensor.matmul(ps_a[w][:, :], X[:, w, :], X[:, w, :], start=True, stop=True).then_inc(s_a, 1)
                for w in range(2):
                    pe.wait_ge(s_as, 2 * n + w + 1)
                    pe.wait_ge(s_t, 2 * n + w + 1)
                    nc.tensor.matmul(ps_a[w][:, :], A[:, w, :], A[:, w, :], start=True, stop=True).then_inc(s_a2, 1)
                pe.wait_ge(s_ys, 2 * n + 2)
                for w in range(2):
                    pe.wait_ge(s_c, 2 * n + w + 3)
                    nc.tensor.matmul(ps_x[w][:, :], Y[:, w, :], C[:, w, :], start=True, stop=True)
                    nc.tensor.matmul(ps_y[w][:, :], C[:, w, :], Y[:, w, :], start=True, stop=True).then_inc(s_xy, 1)


def stage_scan_in(nc, sems, W, K, Q):
    X, ident = K["X"], K["ident"]
    E0, vT = Q["E"][0], Q["vT"]
    st = ExitStack()
    with st:
        m = Pool_(nc, st, sems, "si")
        norm = Norm(m, X, ident)
        w = m.sb("w", [P, 2, D])
        idn = m.sb("idn", [P, 1])
        ps_tr = m.ps("ps_tr", [P, CW])
        ps_q = m.ps("ps_q", [P, 2, CW])
        s_w = m.sem("s_w")
        s_p = m.sem("s_p")
        s_e = m.sem("s_e")
        block = st.enter_context(nc.Block())

        @block.sync
        def _(sp):
            sp.dma_start(w[:, :, :], W["wqv"]).then_inc(s_w, 16)
            sp.dma_start(idn[:, :], W["identity"]).then_inc(s_w, 16)
            sp.wait_ge(s_w, 32)

        @block.vector
        def _(dve):
            norm.dve_eps(nc)
            m.seed(s_e, 2)
            norm.dve_stats(nc, 0, 0)
            norm.dve_apply(nc, 0, 0)
            dve.wait_ge(s_w, 32)
            nc.vector.tensor_copy(E0[:, :, 0], bcast(idn[:, 0:1], 1, B)[:, :, 0])

            def chunk(c, u, b, more):
                if more:
                    norm.dve_stats(nc, c + 1, 1 - u)
                    norm.dve_apply(nc, c + 1, 1 - u)
                for r in range(2):
                    dst = E0[:, ds(b, 1), 1 + u * CW:1 + (u + 1) * CW] if r == 0 else vT[:, ds(b, 1), u * CW:(u + 1) * CW]
                    dve.wait_ge(s_p, 2 * c + r + 1)
                    nc.vector.tensor_scalar(out=dst.rearrange("p o n -> p (o n)"), in0=ps_q[:, r, :], scalar1=0.0,
                                            scalar2=None, op0=ALU.add).then_inc(s_e, 1)

            with dve.Fori(0, CHUNKS // 2 - 1) as k:
                for u in range(2):
                    chunk(k * 2 + u, u, k, True)
            chunk(CHUNKS - 2, 0, B - 1, True)
            chunk(CHUNKS - 1, 1, B - 1, False)

        @block.scalar
        def _(act):
            act.wait_ge(norm.s_eps, 1)
            norm.act_std(nc, 0, 0)
            norm.act_hT(nc, 0, 0, ps_tr)
            with act.Fori(0, CHUNKS // 2 - 1) as k:
                for u in range(2):
                    norm.act_std(nc, k * 2 + u + 1, 1 - u)
                    norm.act_hT(nc, k * 2 + u + 1, 1 - u, ps_tr)
            norm.act_std(nc, CHUNKS - 1, 1)
            norm.act_hT(nc, CHUNKS - 1, 1, ps_tr)

        @block.tensor
        def _(pe):
            pe.wait_ge(s_w, 32)
            norm.pe_transpose(nc, 0, 0, ps_tr)

            def chunk(c, u, more):
                pe.wait_ge(norm.s_hT, c + 1)
                for r in range(2):
                    pe.wait_ge(s_e, 2 * c + r + 1)
                    nc.tensor.matmul(ps_q[:, r, :], w[:, r, :], norm.hT[:, u, :], start=True,
                                     stop=True).then_inc(s_p, 1)
                if more:
                    norm.pe_transpose(nc, c + 1, 1 - u, ps_tr)

            with pe.Fori(0, CHUNKS // 2 - 1) as k:
                for u in range(2):
                    chunk(k * 2 + u, u, True)
            chunk(CHUNKS - 2, 0, True)
            chunk(CHUNKS - 1, 1, False)


def scan_combines():
    stages = []
    last = len(LEVELS) - 1
    for l in range(last):
        stages.append(("down", l, LEVELS[l + 1], (l, 0, 2), (l, 1, 2), (l + 1, 0, 1)))
    for l in range(last - 1, -1, -1):
        n = LEVELS[l] // 2 - (LEVELS[l] % 2 == 0)
        stages.append(("up", l, n, (l + 1, 0, 1), (l, 2, 2), (l, 2, 2)))
    out = []
    for kind, l, n, left, right, dst in stages:
        per = max(1, min(B, CW // n)) if n else 0
        out.append((kind, l, [(b, per, n, left, right, dst) for b in range(0, B, per)] if n else []))
    return out


def stage_scan_tree(nc, sems, K, Q):
    E_, Y = Q["E"], Q["Y"]
    st = ExitStack()
    with st:
        m = Pool_(nc, st, sems, "sc")
        sq = m.sb("sq", [P, 2, CW])
        rt = m.sb("rt", [P, 2, CW])
        rc = m.sb("rc", [P, 2, CW])
        eps = m.sb("eps", [P, 1])
        ps_z = m.ps("ps_z", [P, 2, CW])
        ps_m = m.ps("ps_m", [P, 2, CW])
        s_eps = m.sem("s_eps")
        s_z = m.sem("s_z")
        s_sq = m.sem("s_sq")
        s_m = m.sem("s_m")
        s_rt = m.sem("s_rt")
        s_rc = m.sem("s_rc")
        s_o = m.sem("s_o")
        s_cp = m.sem("s_cp")
        block = st.enter_context(nc.Block())
        plan = scan_combines()

        def view(x, b, per, n):
            level, first, step = x
            return E_[level][:, b:b + per, first:first + step * (n - 1) + 1:step]

        def flat(t, v, per, n):
            return t[:, v, 0:per * n].rearrange("p (b n) -> p b n", n=n)

        @block.tensor
        def _(pe):
            g = ups = 0

            def sums(g, per, n):
                pe.wait_ge(s_sq, g + 1)
                nc.tensor.matmul(ps_m[:, g % 2, 0:per * n], K["ones"][:, :], sq[:, g % 2, 0:per * n],
                                 start=True, stop=True).then_inc(s_m, 1)
            for kind, l, combos in plan:
                if g:
                    pe.wait_ge(s_o, g)
                if ups:
                    pe.wait_ge(s_cp, ups)
                for k, (b, per, n, left, right, dst) in enumerate(combos):
                    if k >= 2:
                        pe.wait_ge(s_o, g - 1)
                    z = flat(ps_z, g % 2, per, n)
                    nc.tensor.matmul(z, Y[:, 0, :], view(left, b, per, n), start=True, stop=False)
                    nc.tensor.matmul(z, Y[:, 1, :], view(right, b, per, n), start=False, stop=True).then_inc(s_z, 1)
                    if k:
                        sums(g - 1, per, n)
                    g += 1
                if combos:
                    sums(g - 1, per, n)
                ups += kind == "up"

        @block.scalar
        def _(act):
            act.wait_ge(s_eps, 1)
            g = 0

            def roots(g, per, n):
                act.wait_ge(s_m, g + 1)
                nc.scalar.activation(rt[:, g % 2, 0:per * n], ps_m[:, g % 2, 0:per * n], ACT.Sqrt,
                                     bias=eps[:, 0:1], scale=1.0 / D).then_inc(s_rt, 1)
            for kind, l, combos in plan:
                for k, (b, per, n, *_) in enumerate(combos):
                    act.wait_ge(s_z, g + 1)
                    nc.scalar.activation(sq[:, g % 2, 0:per * n], ps_z[:, g % 2, 0:per * n],
                                         ACT.Square).then_inc(s_sq, 1)
                    if k:
                        roots(g - 1, per, n)
                    g += 1
                if combos:
                    roots(g - 1, per, n)

        @block.gpsimd
        def _(pool):
            g = ups = 0
            for kind, l, combos in plan:
                if kind == "up":
                    if g:
                        pool.wait_ge(s_o, g)
                    if ups:
                        pool.wait_ge(s_cp, ups)
                    n = LEVELS[l] // 2
                    nc.gpsimd.tensor_copy(E_[l][:, :, 1:2 * n:2], E_[l + 1][:, :, 0:n]).then_inc(s_cp, 1)
                    ups += 1
                g += len(combos)

        @block.vector
        def _(dve):
            nc.vector.memset(eps[:, :], SCAN_EPS).then_inc(s_eps, 1)
            g = 0
            for kind, l, combos in plan:
                for b, per, n, left, right, dst in combos:
                    dve.wait_ge(s_rt, g + 1)
                    nc.vector.reciprocal(rc[:, g % 2, 0:per * n], rt[:, g % 2, 0:per * n]).then_inc(s_rc, 1)
                    dve.wait_ge(s_rc, g + 1)
                    nc.vector.tensor_tensor(out=view(dst, b, per, n), in0=flat(ps_z, g % 2, per, n),
                                            in1=flat(rc, g % 2, per, n), op=ALU.mult).then_inc(s_o, 1)
                    g += 1


def stage_scan_out(nc, sems, W, K, Q):
    X = K["X"]
    E0, vT = Q["E"][0], Q["vT"]
    st = ExitStack()
    with st:
        m = Pool_(nc, st, sems, "so")
        w = m.sb("w", [P, D])
        pr = m.sb("pr", [P, 2, CW])
        ps_y = m.ps("ps_y", [P, 2, CT, D])
        s_w = m.sem("s_w")
        s_pr = m.sem("s_pr")
        s_y = m.sem("s_y")
        s_x = m.sem("s_x")
        block = st.enter_context(nc.Block())

        @block.sync
        def _(sp):
            sp.dma_start(w[:, :], W["wc"]).then_inc(s_w, 16)
            sp.wait_ge(s_w, 16)

        @block.vector
        def _(dve):
            m.seed(s_y, 2)
            m.seed(s_x, 2)

            def product(c, u, b):
                dve.wait_ge(s_y, c + 1)
                nc.vector.tensor_tensor(out=pr[:, u, :],
                                        in0=E0[:, ds(b, 1), 1 + u * CW:1 + (u + 1) * CW].rearrange("p o n -> p (o n)"),
                                        in1=vT[:, ds(b, 1), u * CW:(u + 1) * CW].rearrange("p o n -> p (o n)"),
                                        op=ALU.mult).then_inc(s_pr, 1)

            def add(c, u):
                dve.wait_ge(s_y, c + 3)
                xc = X[:, ds(c * CT, CT), :]
                nc.vector.tensor_tensor(out=xc, in0=ps_y[:, u], in1=xc, op=ALU.add).then_inc(s_x, 1)
            product(0, 0, 0)
            with dve.Fori(0, CHUNKS // 2 - 1) as k:
                product(2 * k + 1, 1, k)
                add(2 * k, 0)
                product(2 * k + 2, 0, k + 1)
                add(2 * k + 1, 1)
            product(CHUNKS - 1, 1, B - 1)
            add(CHUNKS - 2, 0)
            add(CHUNKS - 1, 1)

        @block.tensor
        def _(pe):
            pe.wait_ge(s_w, 16)
            with pe.Fori(0, CHUNKS // 2) as k:
                for u in range(2):
                    c = k * 2 + u
                    pe.wait_ge(s_x, c + 1)
                    pe.wait_ge(s_pr, c + 1)
                    for j in range(CT):
                        last = nc.tensor.matmul(ps_y[:, u, j, :], pr[:, u, j * P:(j + 1) * P], w[:, :],
                                                start=True, stop=True)
                    last.then_inc(s_y, 1)


def stage_scan(nc, sems, W, K):
    st = ExitStack()
    with st:
        m = Pool_(nc, st, sems, "s")
        Q = {"Y": m.sb("Y", [P, 2, P]), "vT": m.sb("vT", [P, B, N]),
             "E": [m.sb(f"E{k}", [P, B, n]) for k, n in enumerate(LEVELS)]}
        stage_polar(nc, sems, W, K, Q)
        stage_scan_in(nc, sems, W, K, Q)
        stage_scan_tree(nc, sems, K, Q)
        stage_scan_out(nc, sems, W, K, Q)


def stage_store(nc, sems, K, out):
    st = ExitStack()
    with st:
        m = Pool_(nc, st, sems, "st")
        s_out = m.sem("s_out")
        block = st.enter_context(nc.Block())

        @block.sync
        def _(sp):
            o = out.rearrange("b (n p) d -> p (b n) d", p=P)
            for q in range(4):
                sp.dma_start(o[:, q * 8:q * 8 + 8, :], K["X"][:, q * 8:q * 8 + 8, :]).then_inc(s_out, 16)
            sp.wait_ge(s_out, 64)


def program(nc, W, out, stages="fafmsm"):
    st = ExitStack()
    with st:
        sems = st
        m = Pool_(nc, st, sems, "g")
        K = {"X": m.sb("X", [P, TILES, D]), "ident": m.sb("ident", [P, P]), "ones": m.sb("ones", [P, P]),
             "triu": m.sb("triu", [P, P]), "identb": m.sb("identb", [P, P], BF16),
             "onesb": m.sb("onesb", [P, P], BF16), "triub": m.sb("triub", [P, P], BF16),
             "iota": m.sb("iota", [P, CAP]), "zero": m.sb("zero", [P, 1])}
        stage_load(nc, sems, W, K)
        R = {"w1": m.sb("w1", [P, E + 1, I]), "w3": m.sb("w3", [P, E + 1, I]),
             "w2": m.sb("w2", [P, 3, E + 1, D]), "wr": m.sb("wr", [P, E]), "br": m.sb("br", [1, E]),
             "rev": m.sb("rev", [P, E])}
        K["s_wt_fa"], K["s_wt_fb"] = m.sem("s_wt_fa"), m.sem("s_wt_fb")
        with nc.cleanup_on_exit():
            if stages[0] == "f":
                stage_ffn(nc, sems, "fa", W, K, R, True)
        attn = ExitStack()
        with nc.cleanup_on_exit(), attn:
            ma = Pool_(nc, attn, sems, "a")
            A = {n: ma.sb(n, [P, PAIRS, PT_, 2 * DH]) for n in "qkvo"}
            if stages[1] == "a":
                stage_qkv(nc, sems, W, K, A)
                stage_attention(nc, sems, K, A)
                stage_project(nc, sems, W, K, A)
        if stages[2:] == "...":
            stage_store(nc, sems, K, out)
            return
        M = {"wr": m.sb("xwr", [P, EX]), "wg": m.sb("xwg", [P, EX, HID]), "wu": m.sb("xwu", [P, EX, HID]),
             "wd": m.sb("xwd", [HID, EX, D])}
        with nc.cleanup_on_exit():
            if stages[2] == "f":
                stage_ffn(nc, sems, "fb", W, K, R, stages[0] != "f", M)
            elif stages[3:] != "...":
                stage_moe_weights(nc, sems, W, M)
        with nc.cleanup_on_exit():
            if stages[3] == "m":
                moe(nc, sems, "ma", K, M)
        with nc.cleanup_on_exit():
            if stages[4] == "s":
                stage_scan(nc, sems, W, K)
        with nc.cleanup_on_exit():
            if stages[5] == "m":
                moe(nc, sems, "mb", K, M)
        stage_store(nc, sems, K, out)


def stage_moe_weights(nc, sems, W, M):
    st = ExitStack()
    with st:
        s_w = Pool_(nc, st, sems, "mw").sem("s_w")
        block = st.enter_context(nc.Block())

        @block.sync
        def _(sp):
            for n in ("wr", "wg", "wu", "wd"):
                sp.dma_start(M[n][tuple(slice(None) for _ in M[n].shape)], W["x" + n]).then_inc(s_w, 16)
            sp.wait_ge(s_w, 64)


def host_arrays(i):
    import numpy as np
    c = np.ascontiguousarray
    up = np.arange(P)
    a = {"x": c(i["L0_attn_x"])}
    for n, name in (("w1", "1"), ("w3", "3")):
        e, s = np.asarray(i["L0_ffn_ew" + name]), np.asarray(i["L0_ffn_sw" + name])
        a[n] = c(np.concatenate([e, s[None]]).transpose(2, 0, 1))
    a["w2"] = c(np.concatenate([np.asarray(i["L0_ffn_ew2"]), np.asarray(i["L0_ffn_sw2"])[None]]).transpose(2, 0, 1))
    a["wr"] = c(np.asarray(i["L0_ffn_router_w"]).T)
    a["br"] = c(np.asarray(i["L0_ffn_routing_bias"]).reshape(1, -1))
    a["ident"] = np.eye(P, dtype=np.float32)
    a["ones"] = np.ones((P, P), np.float32)
    a["triu"] = (up[:, None] < up[None, :]).astype(np.float32)
    a["iota"] = np.tile(np.arange(CAP, dtype=np.float32), (P, 1))
    a["xwr"] = c(np.asarray(i["L1_ffn_gate_w"]).T)
    a["xwg"] = c(np.asarray(i["L1_ffn_w_gate"]).transpose(2, 0, 1))
    a["xwu"] = c(np.asarray(i["L1_ffn_w_up"]).transpose(2, 0, 1))
    a["xwd"] = c(np.asarray(i["L1_ffn_w_down"]).transpose(2, 0, 1))
    a["wqv"] = c(np.stack([np.asarray(i["L1_attn_W" + n]).T for n in "qv"], axis=1))
    a["identity"] = c(np.asarray(i["L1_attn_identity"]).reshape(P, 1))
    a["wp"] = c(np.stack([np.asarray(i["L1_attn_Wp1"]), np.asarray(i["L1_attn_Wp2"])]))
    a["wpt"] = c(a["wp"].transpose(0, 2, 1))
    a["wc"] = c(np.asarray(i["L1_attn_Wc"]).T)
    a["rev"] = np.tile(np.arange(E, 0, -1, dtype=np.float32), (P, 1))
    a["wqkv"] = c(np.concatenate([np.asarray(i["L0_attn_W" + n]).T for n in "qkv"], axis=1))
    a["wo"] = c(np.asarray(i["L0_attn_Wo"]).T)
    a["nw"] = c(np.broadcast_to(np.stack([np.asarray(i["L0_attn_qn_w"]), np.asarray(i["L0_attn_kn_w"])]), (P, 2, DH)))
    return a


def kernel(**inputs):
    import numpy as np
    import concourse.bacc as bacc
    from concourse.bass_utils import run_bass_kernel_spmd

    arrays = host_arrays(inputs)
    nc = bacc.Bacc("TRN2", target_bir_lowering=False, num_devices=1)
    W = {n: nc.dram_tensor(n, a.shape, mybir.dt.from_np(a.dtype), kind="ExternalInput").ap() for n, a in arrays.items()}
    out = nc.dram_tensor("out", (B, N, D), F32, kind="ExternalOutput").ap()
    program(nc, W, out)
    r = run_bass_kernel_spmd(nc, [arrays], core_ids=[0])
    return r.results[0]["out"]
```

```python
from contextlib import ExitStack

import concourse.bass as bass
from concourse import mybir

F32 = mybir.dt.float32
BF16 = mybir.dt.bfloat16
I32 = mybir.dt.int32
ALU = mybir.AluOpType
ACT = mybir.ActivationFunctionType
AX = mybir.AxisListType
ds = bass.ds

P = 128
D = 128
B, N = 4, 1024
T = B * N
TILES = T // P
CT = 4
CW = CT * P
CHUNKS = TILES // CT
LN_EPS = 1e-5

I = 352
E = 7
IC = [(0, 128), (128, 128), (256, 96)]
SLOT_TILES = -(-(T // P + E) // 4) * 4
FILL = SLOT_TILES // 4


def bcast(ap, at, n):
    dims = [list(x) for x in ap.ap]
    dims.insert(at, [0, n])
    return bass.AP(ap.tensor, ap.offset, dims)


class Pool_:

    def __init__(self, nc, stack, sems, tag):
        self.nc, self.stack, self.sems, self.tag = nc, stack, sems, tag
        self.seeds = None

    def sb(self, name, shape, dt=F32):
        return self.stack.enter_context(self.nc.sbuf_tensor(f"{self.tag}_{name}", shape, dt))

    def ps(self, name, shape, dt=F32):
        return self.stack.enter_context(self.nc.psum_tensor(f"{self.tag}_{name}", shape, dt))

    def seed(self, sem, n):
        if self.seeds is None:
            self.seeds, self.n = self.sb("seeds", [P, 12]), 0
        self.nc.vector.memset(self.seeds[:, self.n:self.n + 1], 0.0).then_inc(sem, n)
        self.n += 1

    def sem(self, name):
        return self.nc.alloc_semaphore(name=f"{self.tag}_{name}")


class Norm:

    def __init__(self, m, X, ident, transposed=True):
        self.X, self.ident = X, ident
        self.stats = m.sb("stats", [P, 2, CT, 6])
        self.mv = m.sb("mv", [P, 2, CT, 2])
        self.std = m.sb("std", [P, 2, CT])
        self.rstd = m.sb("rstd", [P, 2, CT])
        self.h = m.sb("h", [P, 2, CT, D])
        self.hT = m.sb("hT", [P, 2, CW])
        self.eps = m.sb("eps", [P, 1])
        self.tick = m.sb("tick", [P, 1])
        self.s_stats = m.sem("s_stats")
        self.s_mv = m.sem("s_mv")
        self.s_std = m.sem("s_std")
        self.s_rstd = m.sem("s_rstd")
        self.s_h = m.sem("s_h")
        self.s_tr = m.sem("s_tr")
        self.s_hT = m.sem("s_hT")
        self.s_eps = m.sem("s_eps")

    def dve_eps(self, nc):
        nc.vector.memset(self.eps[:, :], LN_EPS).then_inc(self.s_eps, 1)

    def dve_stats(self, nc, c, u):
        for j in range(CT):
            nc.vector.bn_stats(self.stats[:, u, j, :], self.X[:, ds(c * CT + j, 1), :]).then_inc(self.s_stats, 1)
        nc.vector.wait_ge(self.s_stats, (c + 1) * CT)
        nc.vector.memset(self.tick[:, :], 0.0)
        for j in range(CT):
            nc.vector.bn_aggr(self.mv[:, u, j, :], self.stats[:, u, j, :]).then_inc(self.s_mv, 1)

    def act_std(self, nc, c, u):
        nc.scalar.wait_ge(self.s_mv, (c + 1) * CT)
        nc.scalar.activation(self.std[:, u, :], self.mv[:, u, :, 1], ACT.Sqrt,
                             bias=self.eps[:, 0:1]).then_inc(self.s_std, 1)

    def dve_apply(self, nc, c, u):
        nc.vector.wait_ge(self.s_std, c + 1)
        nc.vector.reciprocal(self.rstd[:, u, :], self.std[:, u, :]).then_inc(self.s_rstd, 1)
        nc.vector.wait_ge(self.s_rstd, c + 1)
        for j in range(CT):
            nc.vector.tensor_scalar(out=self.h[:, u, j, :], in0=self.X[:, ds(c * CT + j, 1), :],
                                    scalar1=self.mv[:, u, j, 0:1], scalar2=self.rstd[:, u, j:j + 1],
                                    op0=ALU.subtract, op1=ALU.mult).then_inc(self.s_h, 1)

    def pe_transpose(self, nc, c, u, tr):
        nc.tensor.wait_ge(self.s_h, (c + 1) * CT)
        for j in range(CT):
            last = nc.tensor.transpose(tr[:, j * P:(j + 1) * P], self.h[:, u, j, :], self.ident[:, :])
        last.then_inc(self.s_tr, 1)

    def act_hT(self, nc, c, u, tr):
        nc.scalar.wait_ge(self.s_tr, c + 1)
        nc.scalar.activation(self.hT[:, u, :], tr[:, :], ACT.Copy).then_inc(self.s_hT, 1)


def stage_load(nc, sems, W, consts):
    st = ExitStack()
    with st:
        m = Pool_(nc, st, sems, "ld")
        s_in = m.sem("s_in")
        block = st.enter_context(nc.Block())

        @block.sync
        def _(sp):
            xin = W["x"].rearrange("b (n p) d -> p (b n) d", p=P)
            for q in range(4):
                sp.dma_start(consts["X"][:, q * 8:q * 8 + 8, :], xin[:, q * 8:q * 8 + 8, :]).then_inc(s_in, 16)
            for name in ("ident", "ones", "triu", "iota"):
                sp.dma_start(consts[name][:, :], W[name]).then_inc(s_in, 16)
            sp.wait_ge(s_in, 16 * 8)

        @block.vector
        def _(dve):
            nc.vector.memset(consts["zero"][:, :], 0.0)
            dve.wait_ge(s_in, 16 * 8)
            for name in ("ident", "ones", "triu"):
                nc.vector.tensor_copy(consts[name + "b"][:, :], consts[name][:, :])


def stage_ffn_route(nc, sems, tag, W, K, R, F, load):
    X, ident = K["X"], K["ident"]
    H, hT = F["H"], F["hT"]
    st = ExitStack()
    with st:
        m = Pool_(nc, st, sems, tag)
        norm = Norm(m, X, ident)
        lg = m.sb("lg", [P, TILES, E])
        pr = m.sb("pr", [P, TILES, E])
        pmax = m.sb("pmax", [P, TILES])
        eq = m.sb("eq", [P, TILES, E])
        smax = m.sb("smax", [P, TILES])
        pc = m.sb("pc", [P, TILES])
        tw = m.sb("tw", [P, TILES])
        mask = m.sb("mask", [P, TILES, E], BF16)
        PAD = TILES // 2
        cum = m.sb("cum", [P, 2, PAD + TILES, E])
        full = m.sb("full", [P, E, TILES])
        tiles_e = m.sb("tiles_e", [P, E])
        PADE = 4
        end = m.sb("end", [P, 2, PADE + E])
        start = m.sb("start", [P, E])
        sl = m.sb("sl", [P, 4, TILES, E])
        slf = m.sb("slf", [P, TILES])
        past = m.sb("past", [P, SLOT_TILES, E - 1])
        tef = m.sb("tef", [P, SLOT_TILES])
        ps_tr = m.ps("ps_tr", [P, CW])
        ps_lg = m.ps("ps_lg", [P, 2, CW])
        ps_pos = m.ps("ps_pos", [P, TILES, E])
        ps_cnt = m.ps("ps_cnt", [P, TILES, E])
        s_w = m.sem("s_w")
        s_wx = m.sem("s_wx")
        s_st = [m.sem("s_st0"), m.sem("s_st1")]
        s_lgm = m.sem("s_lgm")
        s_lg = m.sem("s_lg")
        s_z = m.sem("s_z")
        s_pr = m.sem("s_pr")
        s_r = m.sem("s_r")
        s_mk = m.sem("s_mk")
        s_c = m.sem("s_c")
        if load:
            zb = m.sb("zb", [P, FILL * D])
        block = st.enter_context(nc.Block())

        @block.sync
        def _(sp):
            if load:
                sp.dma_start(R["wr"][:, :], W["wr"]).then_inc(s_w, 16)
                sp.dma_start(R["br"][:, :], W["br"]).then_inc(s_w, 16)
                sp.dma_start(R["rev"][:, :], W["rev"]).then_inc(s_w, 16)
                sp.dma_start(R["steps"][:, :], W["steps"]).then_inc(s_w, 16)
                sp.dma_start(R["w1"][:, :, :], W["w1"]).then_inc(s_wx, 16)
                sp.dma_start(R["w3"][:, :, :], W["w3"]).then_inc(s_wx, 16)
                for j, (i0, n) in enumerate(IC):
                    sp.dma_start(R["w2"][0:n, j, :, :], W["w2"][i0:i0 + n, :, :]).then_inc(s_wx, 16)
                sp.wait_ge(s_z, 4)
                fill = F["Hs"].rearrange("(q p t) d -> q p (t d)", p=P, t=FILL)
                for q in range(SLOT_TILES // FILL):
                    sp.dma_start(fill[q], zb[:, :]).then_inc(s_wx, 16)
            with sp.Fori(0, CHUNKS // 2) as k:
                for u in range(2):
                    c = k * 2 + u
                    sp.wait_ge(norm.s_h, (c + 1) * CT)
                    sp.dma_start(H[:, ds(c * CT, CT), :], norm.h[:, u]).then_inc(s_st[u], 16)
                    sp.wait_ge(norm.s_hT, c + 1)
                    sp.dma_start(hT[:, ds(c * CW, CW)], norm.hT[:, u, :]).then_inc(s_st[u], 16)
            for u in range(2):
                sp.wait_ge(s_st[u], CHUNKS // 2 * 32 + 32)
            if load:
                sp.wait_ge(s_wx, 16 * (5 + SLOT_TILES // FILL))

        @block.vector
        def _(dve):
            norm.dve_eps(nc)
            for u in range(2):
                m.seed(s_st[u], 32)
            m.seed(s_lg, 2)
            nc.vector.memset(cum[:, :, 0:PAD, :], 0.0).then_inc(s_z, 1)
            nc.vector.memset(end[:, :, 0:PADE], 0.0).then_inc(s_z, 1)
            if load:
                nc.vector.memset(zb[:, :], 0.0).then_inc(s_z, 1)
                nc.vector.memset(R["w2"][IC[-1][1]:P, len(IC) - 1, :, :], 0.0).then_inc(s_z, 1)
                dve.wait_ge(s_w, 64)
            norm.dve_stats(nc, 0, 0)
            norm.dve_apply(nc, 0, 0)

            def chunk(k, u, more):
                c = k * 2 + u
                if more:
                    norm.dve_stats(nc, c + 1, 1 - u)
                    dve.wait_ge(s_st[1 - u], (k + u) * 32 + 32)
                    norm.dve_apply(nc, c + 1, 1 - u)
                dve.wait_ge(s_lgm, c + 1)
                nc.vector.tensor_scalar(out=lg[:, ds(c * CT, CT), :].rearrange("p t e -> p (t e)"),
                                        in0=ps_lg[:, u, 0:CT * E], scalar1=-50.0, scalar2=50.0,
                                        op0=ALU.max, op1=ALU.min).then_inc(s_lg, 1)

            with dve.Fori(0, CHUNKS // 2 - 1) as k:
                for u in range(2):
                    chunk(k, u, True)
            chunk(CHUNKS // 2 - 1, 0, True)
            chunk(CHUNKS // 2 - 1, 1, False)

            done = 0

            def step(ins):
                nonlocal done
                done += 1
                ins.then_inc(s_r, 1)
                dve.wait_ge(s_r, done)
            dve.wait_ge(s_pr, 1)
            step(nc.vector.tensor_reduce(out=pmax[:, :], in_=pr[:, :, :], axis=AX.X, op=ALU.max))
            step(nc.vector.tensor_tensor(out=eq[:, :, :], in0=pr[:, :, :], in1=bcast(pmax[:, :], 2, E),
                                         op=ALU.is_equal))
            step(nc.vector.tensor_tensor(out=eq[:, :, :], in0=eq[:, :, :], in1=bcast(R["rev"][:, :], 1, TILES),
                                         op=ALU.mult))
            step(nc.vector.tensor_reduce(out=smax[:, :], in_=eq[:, :, :], axis=AX.X, op=ALU.max))
            nc.vector.tensor_tensor(out=mask[:, :, :], in0=eq[:, :, :], in1=bcast(smax[:, :], 2, E),
                                    op=ALU.is_equal).then_inc(s_mk, 1)
            step(nc.vector.tensor_scalar(out=pc[:, :], in0=pmax[:, :], scalar1=1e-8, scalar2=1.0 - 1e-8,
                                         op0=ALU.max, op1=ALU.min))
            step(nc.vector.tensor_scalar(out=tw[:, :], in0=pc[:, :], scalar1=0.5, scalar2=1e-8,
                                         op0=ALU.add, op1=ALU.add))
            step(nc.vector.tensor_scalar(out=tw[:, :], in0=tw[:, :], scalar1=0.5, scalar2=2.0,
                                         op0=ALU.max, op1=ALU.min))
            step(nc.vector.reciprocal(tw[:, :], tw[:, :]))
            nc.vector.tensor_scalar_mul(F["w_sh"][:, :], tw[:, :], 0.25)
            nc.vector.scalar_tensor_tensor(out=F["w_ex"][:, :], in0=pc[:, :], scalar=0.5, in1=tw[:, :],
                                           op0=ALU.mult, op1=ALU.mult)
            dve.wait_ge(s_c, 1)
            dve.wait_ge(s_z, 2)
            step(nc.vector.tensor_copy(cum[:, 0, PAD:, :], ps_cnt[:, :, :]))
            v, s = 0, 1
            while s < TILES:
                step(nc.vector.tensor_tensor(out=cum[:, 1 - v, PAD:, :], in0=cum[:, v, PAD:, :],
                                             in1=cum[:, v, PAD - s:PAD + TILES - s, :], op=ALU.add))
                v, s = 1 - v, 2 * s
            total = cum[:, v, PAD + TILES - 1, :]
            step(nc.vector.tensor_tensor(out=full[:, :, :], in0=bcast(total, 2, TILES),
                                         in1=bcast(R["steps"][:, SLOT_TILES:], 1, E), op=ALU.is_gt))
            step(nc.vector.tensor_reduce(out=tiles_e[:, :], in_=full[:, :, :], axis=AX.X, op=ALU.add))
            step(nc.vector.tensor_copy(end[:, 0, PADE:], tiles_e[:, :]))
            w = 0
            for s in (1, 2, 4):
                step(nc.vector.tensor_tensor(out=end[:, 1 - w, PADE:], in0=end[:, w, PADE:],
                                             in1=end[:, w, PADE - s:PADE + E - s], op=ALU.add))
                w = 1 - w
            ends = end[:, w, PADE:]
            step(nc.vector.tensor_tensor(out=start[:, :], in0=ends, in1=tiles_e[:, :], op=ALU.subtract))
            step(nc.vector.tensor_tensor(out=sl[:, 0], in0=ps_pos[:, :, :], in1=cum[:, v, PAD:, :], op=ALU.add))
            step(nc.vector.tensor_tensor(out=sl[:, 1], in0=sl[:, 0], in1=ps_cnt[:, :, :], op=ALU.subtract))
            step(nc.vector.scalar_tensor_tensor(out=sl[:, 2], in0=bcast(start[:, :], 1, TILES), scalar=float(P),
                                                in1=sl[:, 1], op0=ALU.mult, op1=ALU.add))
            step(nc.vector.tensor_tensor(out=sl[:, 3], in0=sl[:, 2], in1=mask[:, :, :], op=ALU.mult))
            step(nc.vector.tensor_reduce(out=slf[:, :], in_=sl[:, 3], axis=AX.X, op=ALU.add))
            step(nc.vector.tensor_copy(F["slot"][:, :], slf[:, :]))
            step(nc.vector.tensor_tensor(out=past[:, :, :], in0=bcast(ends[:, 0:E - 1], 1, SLOT_TILES),
                                         in1=bcast(R["steps"][:, 0:SLOT_TILES], 2, E - 1), op=ALU.is_le))
            step(nc.vector.tensor_reduce(out=tef[:, :], in_=past[:, :, :], axis=AX.X, op=ALU.add))
            step(nc.vector.tensor_copy(F["expert"][:, :], tef[:, :]))

        @block.scalar
        def _(act):
            act.wait_ge(norm.s_eps, 1)
            norm.act_std(nc, 0, 0)
            norm.act_hT(nc, 0, 0, ps_tr)
            with act.Fori(0, CHUNKS // 2 - 1) as k:
                for u in range(2):
                    norm.act_std(nc, k * 2 + u + 1, 1 - u)
                    norm.act_hT(nc, k * 2 + u + 1, 1 - u, ps_tr)
            norm.act_std(nc, CHUNKS - 1, 1)
            norm.act_hT(nc, CHUNKS - 1, 1, ps_tr)
            act.wait_ge(s_lg, CHUNKS + 2)
            nc.scalar.activation(pr[:, :, :], lg[:, :, :], ACT.Sigmoid).then_inc(s_pr, 1)

        @block.tensor
        def _(pe):
            if load:
                pe.wait_ge(s_w, 64)
            norm.pe_transpose(nc, 0, 0, ps_tr)

            def chunk(c, u, more):
                pe.wait_ge(norm.s_hT, c + 1)
                pe.wait_ge(s_lg, c + 1)
                for s in range(CT):
                    nc.tensor.matmul(ps_lg[:, u, s * E:(s + 1) * E], norm.hT[:, u, s * P:(s + 1) * P],
                                     R["wr"][:, :], start=True, stop=False)
                    last = nc.tensor.matmul(ps_lg[:, u, s * E:(s + 1) * E], K["ones"][0:1, :], R["br"][0:1, :],
                                            start=False, stop=True)
                last.then_inc(s_lgm, 1)
                if more:
                    norm.pe_transpose(nc, c + 1, 1 - u, ps_tr)

            with pe.Fori(0, CHUNKS // 2 - 1) as k:
                for u in range(2):
                    chunk(k * 2 + u, u, True)
            chunk(CHUNKS - 2, 0, True)
            chunk(CHUNKS - 1, 1, False)
            pe.wait_ge(s_mk, 1)
            nc.tensor.matmul(ps_pos[:, :, :], K["triub"][:, :], mask[:, :, :], start=True, stop=True)
            nc.tensor.matmul(ps_cnt[:, :, :], K["onesb"][:, :], mask[:, :, :], start=True, stop=True).then_inc(s_c, 1)


def stage_ffn_shared(nc, sems, tag, W, K, R, F, c0, chunks, scatter, M=None):
    X, H, hT = K["X"], F["H"], F["hT"]
    w1, w3, w2 = R["w1"], R["w3"], R["w2"]
    st = ExitStack()
    with st:
        m = Pool_(nc, st, sems, tag)
        silu = m.sb("silu", [P, 2, CW])
        gu = m.sb("gu", [P, 2, len(IC), CW])
        yw = m.sb("yw", [P, 2, CT, D])
        ps_a = m.ps("ps_a", [P, 2, CW])
        ps_b = m.ps("ps_b", [P, 2, CW])
        ps_y = m.ps("ps_y", [P, 2, CT, D])
        s_ab = m.sem("s_ab")
        s_silu = m.sem("s_silu")
        s_gu = m.sem("s_gu")
        s_y = m.sem("s_y")
        s_yw = m.sem("s_yw")
        s_x = m.sem("s_x")
        s_sc = m.sem("s_sc")
        s_ga = [m.sem(f"s_ga{c}") for c in range(0 if scatter else CHUNKS)]
        s_gw = m.sem("s_gw")
        s_m = m.sem("s_m")
        block = st.enter_context(nc.Block())
        NJ = len(IC)

        @block.sync
        def _(sp):
            if M is not None:
                sp.dma_start(M["wr"][:, :], W["xwr"]).then_inc(s_m, 16)
                for q in range(4):
                    for n in ("wg", "wu", "wd"):
                        sp.dma_start(M[n][:, q * 16:q * 16 + 16, :], W["x" + n][:, q * 16:q * 16 + 16, :]
                                     ).then_inc(s_m, 16)
                sp.wait_ge(s_m, 16 * 13)

        @block.gpsimd
        def _(pool):
            for t in range(TILES):
                at = bass.IndirectOffsetOnAxis(ap=F["slot"][:, t:t + 1], axis=0)
                if scatter:
                    nc.gpsimd.indirect_dma_start(out=F["Hs"][:, :], out_offset=at, in_=H[:, t, :],
                                                 in_offset=None).then_inc(s_sc, 16)
                else:
                    nc.gpsimd.indirect_dma_start(out=H[:, t, :], out_offset=None, in_=F["Ys"][:, :],
                                                 in_offset=at).then_inc(s_ga[t // CT], 16)
            if scatter:
                pool.wait_ge(s_sc, TILES * 16)

        @block.scalar
        def _(act):
            with act.Fori(0, chunks // 2) as k:
                for u in range(2):
                    for j in range(NJ):
                        g, n = u * NJ + j, IC[j][1]
                        act.wait_ge(s_ab, k * 2 * NJ + g + 1)
                        act.wait_ge(s_gu, k * 2 * NJ + g + 1)
                        nc.scalar.activation(silu[0:n, g % 2, :], ps_a[0:n, g % 2, :],
                                             ACT.Silu).then_inc(s_silu, 1)

        @block.vector
        def _(dve):
            m.seed(s_gu, 2)
            m.seed(s_y, 2)
            m.seed(s_yw, 2)

            def gate(c, u, j):
                g, n = u * NJ + j, IC[j][1]
                dve.wait_ge(s_silu, c * NJ + j + 1)
                if j == 0:
                    dve.wait_ge(s_y, c + 1)
                nc.vector.tensor_tensor(out=gu[0:n, u, j, :], in0=ps_b[0:n, g % 2, :],
                                        in1=silu[0:n, g % 2, :], op=ALU.mult).then_inc(s_gu, 1)

            def add(c, u):
                dve.wait_ge(s_y, c + 3)
                nc.vector.tensor_tensor(out=yw[:, u], in0=ps_y[:, u],
                                        in1=bcast(F["w_sh"][:, ds(c0 + c * CT, CT)], 2, D),
                                        op=ALU.mult).then_inc(s_yw, 1)
                dve.wait_ge(s_yw, c + 3)
                xc = X[:, ds(c0 + c * CT, CT), :]
                nc.vector.tensor_tensor(out=xc, in0=yw[:, u], in1=xc, op=ALU.add).then_inc(s_x, 1)

            def chunk(c, u, before):
                for j in range(NJ):
                    gate(c, u, j)
                if before:
                    add(c - 1, 1 - u)
            chunk(0, 0, False)
            with dve.Fori(0, chunks // 2 - 1) as k:
                chunk(k * 2 + 1, 1, True)
                chunk(k * 2 + 2, 0, True)
            chunk(chunks - 1, 1, True)
            add(chunks - 1, 1)
            if not scatter:
                dve.wait_ge(s_x, chunks)
                for c in range(CHUNKS):
                    dve.wait_ge(s_ga[c], 16 * CT)
                    hc = H[:, c * CT:(c + 1) * CT, :]
                    xc = X[:, c * CT:(c + 1) * CT, :]
                    nc.vector.tensor_tensor(out=hc, in0=hc, in1=bcast(F["w_ex"][:, c * CT:(c + 1) * CT], 2, D),
                                            op=ALU.mult).then_inc(s_gw, 1)
                    dve.wait_ge(s_gw, c + 1)
                    nc.vector.tensor_tensor(out=xc, in0=hc, in1=xc, op=ALU.add)

        @block.tensor
        def _(pe):
            def up(c, u):
                for j, (i0, n) in enumerate(IC):
                    g = u * NJ + j
                    pe.wait_ge(s_gu, c * NJ + j + 1)
                    rhs = hT[:, ds(c0 * P + c * CW, CW)]
                    nc.tensor.matmul(ps_a[0:n, g % 2, :], w1[:, E, i0:i0 + n], rhs, start=True, stop=True)
                    nc.tensor.matmul(ps_b[0:n, g % 2, :], w3[:, E, i0:i0 + n], rhs, start=True,
                                     stop=True).then_inc(s_ab, 1)

            def down(c, u):
                pe.wait_ge(s_gu, c * NJ + NJ + 2)
                pe.wait_ge(s_yw, c + 1)
                for s in range(CT):
                    for j, (_, n) in enumerate(IC):
                        last = nc.tensor.matmul(ps_y[:, u, s, :], gu[0:n, u, j, s * P:(s + 1) * P],
                                                w2[0:n, j, E, :], start=(j == 0), stop=(j == NJ - 1))
                last.then_inc(s_y, 1)
            up(0, 0)
            with pe.Fori(0, chunks // 2 - 1) as k:
                up(k * 2 + 1, 1)
                down(k * 2, 0)
                up(k * 2 + 2, 0)
                down(k * 2 + 1, 1)
            up(chunks - 1, 1)
            down(chunks - 2, 0)
            down(chunks - 1, 1)


def stage_ffn_switched(nc, sems, tag, K, R, F):
    w1, w3, w2 = R["w1"], R["w3"], R["w2"]
    Hs = F["Hs"].rearrange("(t p) d -> p t d", p=P)
    Ys = F["Ys"].rearrange("(t p) d -> p t d", p=P)
    NJ = len(IC)
    st = ExitStack()
    with st:
        m = Pool_(nc, st, sems, tag)
        hs = m.sb("hs", [P, 2, 2, D])
        hsT = m.sb("hsT", [P, 2, P])
        sg = m.sb("sg", [P, 2, I])
        gu = m.sb("gu", [P, 2, NJ * P])
        guT = m.sb("guT", [P, 2, NJ * P])
        ys = m.sb("ys", [P, 2, 2, D])
        ps_a = m.ps("ps_a", [P, 2, CW])
        ps_b = m.ps("ps_b", [P, 2, CW])
        ps_g = m.ps("ps_g", [P, 2, CW])
        ps_t = m.ps("ps_t", [P, P])
        ps_y = m.ps("ps_y", [P, P])
        s_ld = [m.sem("s_ld0"), m.sem("s_ld1")]
        s_st = [m.sem("s_st0"), m.sem("s_st1")]
        s_z = m.sem("s_z")
        s_t = m.sem("s_t")
        s_tc = m.sem("s_tc")
        s_ab = m.sem("s_ab")
        s_s = m.sem("s_s")
        s_gu = m.sem("s_gu")
        s_g = m.sem("s_g")
        s_gc = m.sem("s_gc")
        s_y = m.sem("s_y")
        s_yc = m.sem("s_yc")
        block = st.enter_context(nc.Block())
        N4 = SLOT_TILES // 4

        @block.sync
        def _(sp):
            def load(k, v):
                sp.wait_ge(s_t, k * 4 + 2 * v + 2)
                sp.dma_start(hs[:, v], Hs[:, ds(k * 4 + 2 * v, 2), :]).then_inc(s_ld[v], 16)

            def store(k, v):
                sp.wait_ge(s_yc, k * 4 + 2 * v + 4)
                sp.dma_start(Ys[:, ds(k * 4 + 2 * v, 2), :], ys[:, v]).then_inc(s_st[v], 16)
            load(0, 0)
            load(0, 1)
            with sp.Fori(0, N4 - 1) as k:
                for v in range(2):
                    load(k + 1, v)
                    store(k, v)
            for v in range(2):
                store(N4 - 1, v)
            for v in range(2):
                sp.wait_ge(s_st[v], N4 * 16 + 16)

        @block.scalar
        def _(act):
            def hT(t, w):
                act.wait_ge(s_t, t + 5)
                if not isinstance(t, int) or t >= 2:
                    act.wait_ge(s_ab, t - 1)
                nc.scalar.activation(hsT[:, w, :], ps_t[:, :], ACT.Copy).then_inc(s_tc, 1)

            def tile(t, w, more):
                if more:
                    hT(t + 1, 1 - w)
                act.wait_ge(s_ab, t + 1)
                act.wait_ge(s_gu, t + 1)
                nc.scalar.activation(sg[:, w, :], ps_a[:, w, 0:I], ACT.Silu).then_inc(s_s, 1)
            hT(0, 0)
            tile(0, 0, True)
            tile(1, 1, True)
            with act.Fori(1, SLOT_TILES // 2 - 1) as k:
                for w in range(2):
                    tile(k * 2 + w, w, True)
            tile(SLOT_TILES - 2, 0, True)
            tile(SLOT_TILES - 1, 1, False)

        @block.vector
        def _(dve):
            nc.vector.memset(gu[:, :, I:], 0.0).then_inc(s_z, 1)
            m.seed(s_t, 4)
            for s in (s_tc, s_gu, s_g, s_gc, s_y, s_yc):
                m.seed(s, 2)
            for v in range(2):
                m.seed(s_st[v], 16)
            dve.wait_ge(s_z, 1)

            def gate(t, w):
                dve.wait_ge(s_s, t + 1)
                dve.wait_ge(s_g, t + 1)
                nc.vector.tensor_tensor(out=gu[:, w, 0:I], in0=ps_b[:, w, 0:I], in1=sg[:, w, :],
                                        op=ALU.mult).then_inc(s_gu, 1)

            def gT(t, w):
                dve.wait_ge(s_g, t + 3)
                dve.wait_ge(s_y, t + 1)
                nc.vector.tensor_copy(guT[:, w, :], ps_g[:, w, 0:NJ * P]).then_inc(s_gc, 1)

            def y(t, k, v, w):
                if w == 0:
                    dve.wait_ge(s_st[v], k * 16 + 16)
                dve.wait_ge(s_y, t + 3)
                nc.vector.tensor_copy(ys[:, v, w, :], ps_y[:, :]).then_inc(s_yc, 1)

            def four(k, first):
                for x in range(4):
                    t = k * 4 + x
                    gate(t, x % 2)
                    if x >= 2 or not first:
                        y(t - 2, k - int(x < 2), (x + 2) % 4 // 2, x % 2)
                    if x >= 1 or not first:
                        gT(t - 1, 1 - x % 2)
            four(0, True)
            with dve.Fori(1, N4) as k:
                four(k, False)
            y(SLOT_TILES - 2, N4 - 1, 1, 0)
            gT(SLOT_TILES - 1, 1)
            y(SLOT_TILES - 1, N4 - 1, 1, 1)

        @block.tensor
        def _(pe):
            def tr(t, k, v, w):
                if w == 0:
                    pe.wait_ge(s_ld[v], k * 16 + 16)
                pe.wait_ge(s_tc, t + 2)
                nc.tensor.transpose(ps_t[:, :], hs[:, v, w, :], K["ident"][:, :]).then_inc(s_t, 1)

            def up(t, w, e):
                pe.wait_ge(s_tc, t + 3)
                pe.wait_ge(s_gu, t + 1)
                for ps, wx in ((ps_a, w1), (ps_b, w3)):
                    last = nc.tensor.matmul(ps[:, w, 0:I], hsT[:, w, :], wx[:, ds(e, 1), :].rearrange("p o i -> p (o i)"),
                                            start=True, stop=True)
                last.then_inc(s_ab, 1)

            def gates(t, w):
                pe.wait_ge(s_gu, t + 3)
                pe.wait_ge(s_gc, t + 1)
                for j in range(NJ):
                    last = nc.tensor.transpose(ps_g[:, w, j * P:(j + 1) * P], gu[:, w, j * P:(j + 1) * P],
                                               K["ident"][:, :])
                last.then_inc(s_g, 1)

            def down(t, w):
                e = pe.value_load(F["expert"][0:1, ds(t, 1)], min_val=0, max_val=E - 1)
                pe.wait_ge(s_gc, t + 3)
                pe.wait_ge(s_yc, t + 2)
                for j in range(NJ):
                    last = nc.tensor.matmul(ps_y[:, :], guT[:, w, j * P:(j + 1) * P],
                                            w2[:, j, ds(e, 1), :].rearrange("p o d -> p (o d)"),
                                            start=(j == 0), stop=(j == NJ - 1))
                last.then_inc(s_y, 1)

            def four(k, first, more):
                for x in range(4):
                    t = k * 4 + x
                    if more or x < 3:
                        tr(t + 1, k + int(x == 3), (x + 1) % 4 // 2, 1 - x % 2)
                    e = pe.value_load(F["expert"][0:1, ds(t, 1)], min_val=0, max_val=E - 1)
                    up(t, x % 2, e)
                    if x >= 2 or not first:
                        down(t - 2, x % 2)
                    if x >= 1 or not first:
                        gates(t - 1, 1 - x % 2)
            tr(0, 0, 0, 0)
            four(0, True, True)
            with pe.Fori(1, N4 - 1) as k:
                four(k, False, True)
            four(N4 - 1, False, False)
            down(SLOT_TILES - 2, 0)
            gates(SLOT_TILES - 1, 1)
            down(SLOT_TILES - 1, 1)


def ffn(nc, sems, tag, W, K, R, load, M=None):
    st = ExitStack()
    with st:
        m = Pool_(nc, st, sems, tag)
        F = {"H": m.sb("H", [P, TILES, D]), "hT": m.sb("hT", [P, T]), "w_sh": m.sb("w_sh", [P, TILES]),
             "w_ex": m.sb("w_ex", [P, TILES]), "slot": m.sb("slot", [P, TILES], I32),
             "expert": m.sb("expert", [P, SLOT_TILES], I32),
             "Hs": K["Hs"], "Ys": K["Ys"]}
        stage_ffn_route(nc, sems, tag + "r", W, K, R, F, load)
        stage_ffn_shared(nc, sems, tag + "s", W, K, R, F, 0, CHUNKS // 2, True)
        stage_ffn_switched(nc, sems, tag + "x", K, R, F)
        stage_ffn_shared(nc, sems, tag + "g", W, K, R, F, TILES // 2, CHUNKS // 2, False, M)


H, DH = 16, 8
PAIRS = B * H // 2
PT_ = N // P
SCALE = DH ** -0.5
RMS_EPS = 1.1920928955078125e-07
SLOTS = 6
KR = SLOTS * DH
KM = KR + 3
HR = 64


def stage_qkv(nc, sems, W, K, A):
    X, ident = K["X"], K["ident"]
    qkv = [A["q"], A["k"], A["v"]]
    st = ExitStack()
    with st:
        m = Pool_(nc, st, sems, "qkv")
        norm = Norm(m, X, ident)
        w = m.sb("w", [P, 3 * D])
        nw = m.sb("nw", [P, 2, DH])
        sq = m.sb("sq", [P, 2, 2 * D])
        ms = m.sb("ms", [P, 2, 2 * H])
        rr = m.sb("rr", [P, 2, 2 * H])
        qk = m.sb("qk", [P, 2, 2 * D])
        reps = m.sb("reps", [P, 1])
        ps_tr = m.ps("ps_tr", [P, CW])
        ps_q = m.ps("ps_q", [P, 2, CW])
        s_w = m.sem("s_w")
        s_c = m.sem("s_c")
        s_p = m.sem("s_p")
        s_sq = m.sem("s_sq")
        s_ms = m.sem("s_ms")
        s_rt = m.sem("s_rt")
        s_rc = m.sem("s_rc")
        s_n = m.sem("s_n")
        s_v = m.sem("s_v")
        s_g = m.sem("s_g")
        block = st.enter_context(nc.Block())

        @block.sync
        def _(sp):
            sp.dma_start(w[:, :], W["wqkv"]).then_inc(s_w, 16)
            sp.dma_start(nw[:, :, :], W["nw"]).then_inc(s_w, 16)
            sp.wait_ge(s_w, 32)

        @block.vector
        def _(dve):
            norm.dve_eps(nc)
            nc.vector.memset(reps[:, :], RMS_EPS).then_inc(s_c, 1)
            m.seed(s_sq, 2)
            m.seed(s_ms, 2)
            m.seed(s_n, 2)
            m.seed(s_v, 2)
            m.seed(s_g, 4)
            norm.dve_stats(nc, 0, 0)
            norm.dve_apply(nc, 0, 0)

            def sums(t, v):
                dve.wait_ge(s_sq, t + 3)
                nc.vector.tensor_reduce(out=ms[:, v, :], in_=sq[:, v, :].rearrange("p (h d) -> p h d", d=DH),
                                        axis=AX.X, op=ALU.add).then_inc(s_ms, 1)

            def scale(t, v):
                dve.wait_ge(s_rt, t + 1)
                nc.vector.reciprocal(rr[:, v, :], ms[:, v, :]).then_inc(s_rc, 1)
                dve.wait_ge(s_rc, t + 1)
                dve.wait_ge(s_g, 2 * t + 2)
                nc.vector.tensor_tensor(out=qk[:, v, :].rearrange("p (h d) -> p h d", d=DH),
                                        in0=ps_q[:, v, 0:2 * D].rearrange("p (h d) -> p h d", d=DH),
                                        in1=bcast(rr[:, v, :], 2, DH), op=ALU.mult).then_inc(s_n, 1)

            def chunk(c, u, more):
                for j in range(CT):
                    sums(c * CT + j, j % 2)
                    if more and j == 1:
                        norm.dve_stats(nc, c + 1, 1 - u)
                    if more and j == 2:
                        norm.dve_apply(nc, c + 1, 1 - u)
                    scale(c * CT + j, j % 2)

            with dve.Fori(0, CHUNKS // 2 - 1) as k:
                for u in range(2):
                    chunk(k * 2 + u, u, True)
            chunk(CHUNKS - 2, 0, True)
            chunk(CHUNKS - 1, 1, False)

        @block.scalar
        def _(act):
            act.wait_ge(norm.s_eps, 1)
            norm.act_std(nc, 0, 0)
            norm.act_hT(nc, 0, 0, ps_tr)
            act.wait_ge(s_c, 1)

            def chunk(c, u, more):
                for j in range(CT):
                    t, v = c * CT + j, j % 2
                    act.wait_ge(s_p, t + 1)
                    act.wait_ge(s_ms, t + 1)
                    nc.scalar.activation(sq[:, v, :], ps_q[:, v, 0:2 * D], ACT.Square).then_inc(s_sq, 1)
                    act_v(c, u, j, v)
                    act.wait_ge(s_ms, t + 3)
                    nc.scalar.activation(ms[:, v, :], ms[:, v, :], ACT.Sqrt, bias=reps[:, 0:1],
                                         scale=1.0 / DH).then_inc(s_rt, 1)
                    if more and j == 1:
                        norm.act_std(nc, c + 1, 1 - u)
                    if more and j == 3:
                        norm.act_hT(nc, c + 1, 1 - u, ps_tr)

            def act_v(c, u, j, v):
                b = (c - u) // 2 if isinstance(c, int) else kk[0]
                dst = A["v"][:, ds(b * 8, 8), 4 * u + j, :]
                nc.scalar.activation(dst, ps_q[:, v, 2 * D:3 * D].rearrange("p (h d) -> p h d", d=16),
                                     ACT.Copy).then_inc(s_v, 1)

            kk = [None]
            with act.Fori(0, CHUNKS // 2 - 1) as k:
                kk[0] = k
                for u in range(2):
                    chunk(k * 2 + u, u, True)
            chunk(CHUNKS - 2, 0, True)
            chunk(CHUNKS - 1, 1, False)

        @block.gpsimd
        def _(pool):
            pool.wait_ge(s_w, 32)

            def chunk(c, u, b):
                for j in range(CT):
                    t, v = c * CT + j, j % 2
                    pool.wait_ge(s_n, t + 3)
                    for r, x in enumerate(("q", "k")):
                        dst = A[x][:, ds(b * 8, 8), 4 * u + j, :].rearrange("p h (a d) -> p h a d", d=DH)
                        src = qk[:, v, r * D:(r + 1) * D].rearrange("p (h a d) -> p h a d", a=2, d=DH)
                        nc.gpsimd.tensor_tensor(out=dst, in0=src, in1=bcast(bcast(nw[:, r, :], 1, 2), 1, 8),
                                                op=ALU.mult).then_inc(s_g, 1)

            with pool.Fori(0, CHUNKS // 2) as k:
                for u in range(2):
                    chunk(k * 2 + u, u, k)

        @block.tensor
        def _(pe):
            pe.wait_ge(s_w, 32)
            norm.pe_transpose(nc, 0, 0, ps_tr)

            def chunk(c, u, more):
                pe.wait_ge(norm.s_hT, c + 1)
                for j in range(CT):
                    t, v = c * CT + j, j % 2
                    pe.wait_ge(s_n, t + 1)
                    pe.wait_ge(s_v, t + 1)
                    nc.tensor.matmul(ps_q[:, v, 0:3 * D], norm.hT[:, u, j * P:(j + 1) * P], w[:, :],
                                     start=True, stop=True).then_inc(s_p, 1)
                    if more and j == 2:
                        norm.pe_transpose(nc, c + 1, 1 - u, ps_tr)

            with pe.Fori(0, CHUNKS // 2 - 1) as k:
                for u in range(2):
                    chunk(k * 2 + u, u, True)
            chunk(CHUNKS - 2, 0, True)
            chunk(CHUNKS - 1, 1, False)


def stage_attention(nc, sems, K, A):
    ident, identb, O = K["ident"], K["identb"], A["o"]
    G8 = PT_
    st = ExitStack()
    with st:
        m = Pool_(nc, st, sems, "at")
        raw = m.sb("raw", [P, 2, 3, G8 * 16])
        qx = m.sb("qx", [P, 2, G8, 2, HR], BF16)
        kx = m.sb("kx", [P, 2, G8, 2, HR], BF16)
        vx = m.sb("vx", [P, 2, G8, 2, 32])
        r1 = m.sb("r1", [P, 4, G8 * 2, DH])
        mr = m.sb("mr", [P, 2, G8 * 2])
        qT1 = m.sb("qT1", [P, 2, N], BF16)
        qT2 = m.sb("qT2", [P, 2, N], BF16)
        qm1 = m.sb("qm1", [P, 2, 2, N], BF16)
        qm2 = m.sb("qm2", [P, 2, 2, N], BF16)
        kT1 = m.sb("kT1", [P, 2, N], BF16)
        kT2 = m.sb("kT2", [P, 2, N], BF16)
        negm = m.sb("negm", [P, 2, G8, 2])
        pT = m.sb("pT", [P, 8, CW])
        oT = m.sb("oT", [P, 2, CW])
        ro = m.sb("ro", [P, 2, 4, 4])
        ps_s = m.ps("ps_s", [P, 2, N])
        ps_p = m.ps("ps_p", [P, 2, CW])
        ps_o = m.ps("ps_o", [P, CW])
        ps_t = m.ps("ps_t", [P, CW])
        tb = ps_t[:, :].bitcast(BF16)
        s_raw = [m.sem(f"s_raw{u}") for u in range(2)]
        s_c = m.sem("s_c")
        s_q1 = m.sem("s_q1")
        s_bld = m.sem("s_bld")
        s_vx = m.sem("s_vx")
        s_msp = m.sem("s_msp")
        s_ms1 = m.sem("s_ms1")
        s_tq1 = m.sem("s_tq1")
        s_tk = m.sem("s_tk")
        s_tq2 = m.sem("s_tq2")
        s_to = m.sem("s_to")
        s_eq1 = m.sem("s_eq1")
        s_ek = m.sem("s_ek")
        s_eq2 = m.sem("s_eq2")
        s_eo = m.sem("s_eo")
        s_m1 = [m.sem(f"s_m1{u}") for u in range(2)]
        s_m2 = [m.sem(f"s_m2{u}") for u in range(2)]
        s_z = m.sem("s_z")
        s_k2 = [m.sem(f"s_k2{u}") for u in range(2)]
        s_s = m.sem("s_s")
        s_mx = m.sem("s_mx")
        s_p = m.sem("s_p")
        s_e = m.sem("s_e")
        s_pv = m.sem("s_pv")
        s_oe = m.sem("s_oe")
        s_ro = m.sem("s_ro")
        LEAD = 3
        NQ = 9
        block = st.enter_context(nc.Block())

        @block.sync
        def _(sp):
            def pair(i, u, h):
                if not isinstance(i, int) or i >= 2:
                    sp.wait_ge(s_vx, i - 1)
                for r, x in enumerate(("q", "k", "v")):
                    sp.dma_start(raw[:, u, r, :], A[x][:, ds(i, 1), :, :].rearrange("p o t w -> p (o t w)")
                                 ).then_inc(s_raw[u], 16)

            def copy_k(i, u, h):
                sp.wait_ge(s_ek, i + 1)
                if not isinstance(i, int) or i >= 2:
                    sp.wait_ge(s_p, 32 * i - 32)
                sp.dma_start(kT2[:, u, :], kT1[:, u, :]).then_inc(s_k2[u], 16)

            def copy_q(i, u, src, dst, out, done):
                sp.wait_ge(out, i + 1)
                for h in range(2):
                    r = slice(h * HR, (h + 1) * HR)
                    sp.dma_start(dst[r, u, h, :], src[r, u, :]).then_inc(done[u], 16)

            def copy_q1(i, u):
                copy_q(i, u, qT1, qm1, s_eq1, s_m1)

            def copy_q2(i, u):
                copy_q(i, u, qT2, qm2, s_eq2, s_m2)

            for i in range(2):
                pair(i, i, 0)
            sp.wait_ge(s_z, 2)
            copy_q1(0, 0)
            copy_k(0, 0, 0)
            pair(2, 0, 1)
            copy_q1(1, 1)
            copy_k(1, 1, 0)
            copy_q2(0, 0)
            with sp.Fori(0, PAIRS // 2 - 2) as k:
                for u in range(2):
                    pair(k * 2 + u + 3, 1 - u, k + 1)
                    copy_q1(k * 2 + u + 2, u)
                    copy_q2(k * 2 + u + 1, 1 - u)
                    copy_k(k * 2 + u + 2, u, 1)
            pair(PAIRS - 1, 1, None)
            copy_q1(PAIRS - 2, 0)
            copy_q2(PAIRS - 3, 1)
            copy_k(PAIRS - 2, 0, None)
            copy_q1(PAIRS - 1, 1)
            copy_q2(PAIRS - 2, 0)
            copy_k(PAIRS - 1, 1, None)
            copy_q2(PAIRS - 1, 1)
            for u in range(2):
                sp.wait_ge(s_k2[u], 16 * (PAIRS // 2))

        @block.gpsimd
        def _(pool):
            nc.gpsimd.memset(qx[:, :, :, :, KR:HR], 0.0).then_inc(s_c, 1)
            nc.gpsimd.memset(kx[:, :, :, :, KR:HR], 0.0).then_inc(s_c, 1)
            nc.gpsimd.memset(vx[:, :, :, :, :], 0.0).then_inc(s_c, 1)
            nc.gpsimd.memset(qm1[:, :, :, :], 0.0).then_inc(s_z, 1)
            nc.gpsimd.memset(qm2[:, :, :, :], 0.0).then_inc(s_z, 1)
            pool.wait_ge(s_c, 3)
            nc.gpsimd.memset(kx[:, :, :, :, KR:KM], 1.0).then_inc(s_c, 1)
            nc.gpsimd.memset(vx[:, :, :, :, DH:DH + 1], 1.0).then_inc(s_c, 1)
            pool.wait_ge(s_c, 5)

            def part(dst, src):
                zero = K["zero"][:, 0:1]
                for at, n in enumerate(src.shape[1:]):
                    zero = bcast(zero, at + 1, n)
                zero = bass.AP(zero.tensor, zero.offset, [list(x) for x in zero.ap][:-1])
                return nc.gpsimd.tensor_tensor(out=dst, in0=src, in1=zero, op=ALU.add)

            def build(i, u, h):
                if not isinstance(i, int) or i >= 2:
                    pool.wait_ge(s_tq2, i - 1)
                pool.wait_ge(s_raw[u], 48 * (h + 1))

                def step(k, ins):
                    ins.then_inc(s_q1, 1)
                    pool.wait_ge(s_q1, i * NQ + k)
                q = raw[:, u, 0, :].rearrange("p (g d) -> p g d", d=DH)
                kk = raw[:, u, 1, :].rearrange("p (g d) -> p g d", d=DH)
                qs = qx[:, u].rearrange("p t h (s d) -> p (t h) s d", d=DH)
                ks = kx[:, u].rearrange("p t h (s d) -> p (t h) s d", d=DH)
                step(1, part(qs[:, :, 0:3, :], bcast(q, 2, 3)))
                step(2, part(ks[:, :, 1:6:2, :], bcast(kk, 2, 3)))
                step(3, nc.gpsimd.tensor_tensor(out=r1[:, 0], in0=q, in1=qs[:, :, 0, :], op=ALU.subtract))
                step(4, nc.gpsimd.tensor_tensor(out=r1[:, 1], in0=kk, in1=ks[:, :, 1, :], op=ALU.subtract))
                step(5, part(qs[:, :, 3:5, :], bcast(r1[:, 0], 2, 2)))
                step(6, part(ks[:, :, 2:5:2, :], bcast(r1[:, 1], 2, 2)))
                step(7, nc.gpsimd.tensor_tensor(out=r1[:, 2], in0=r1[:, 0], in1=qs[:, :, 3, :], op=ALU.subtract))
                step(8, nc.gpsimd.tensor_tensor(out=r1[:, 3], in0=r1[:, 1], in1=ks[:, :, 2, :], op=ALU.subtract))
                step(9, part(qs[:, :, 5, :], r1[:, 2]))
                part(ks[:, :, 0, :], r1[:, 3]).then_inc(s_bld, 1)

            def build_v(i, u):
                if not isinstance(i, int) or i >= 2:
                    pool.wait_ge(s_pv, 8 * i - 6)
                part(vx[:, u].rearrange("p t h s -> p (t h) s")[:, :, 0:DH],
                     raw[:, u, 2, :].rearrange("p (g d) -> p g d", d=DH)).then_inc(s_vx, 1)

            def split_max(i, u):
                pool.wait_ge(s_tq1, i + 1)
                pool.wait_ge(s_mx, 16 * i + 18)

                def step(k, ins):
                    ins.then_inc(s_ms1, 1)
                    pool.wait_ge(s_ms1, i * 4 + k)
                n = negm[:, u].rearrange("p t h -> p (t h)")
                x = qx[:, u].rearrange("p t h s -> p (t h) s")
                step(1, part(x[:, :, KR], n))
                step(2, nc.gpsimd.tensor_tensor(out=mr[:, 0, :], in0=n, in1=x[:, :, KR], op=ALU.subtract))
                step(3, part(x[:, :, KR + 1], mr[:, 0, :]))
                step(4, nc.gpsimd.tensor_tensor(out=mr[:, 1, :], in0=mr[:, 0, :], in1=x[:, :, KR + 1],
                                                op=ALU.subtract))
                part(x[:, :, KR + 2], mr[:, 1, :]).then_inc(s_msp, 1)

            build(0, 0, 0)
            build_v(0, 0)
            build(1, 1, 0)
            build_v(1, 1)
            split_max(0, 0)
            with pool.Fori(1, PAIRS // 2) as k:
                for u in range(2):
                    build(k * 2 + u, u, k)
                    split_max(k * 2 + u - 1, 1 - u)
                    build_v(k * 2 + u, u)
            split_max(PAIRS - 1, 1)

        @block.vector
        def _(dve):
            m.seed(s_mx, 2)
            m.seed(s_e, 2)
            m.seed(s_pv, 2)
            m.seed(s_oe, 1)

            def maxima(i, u, t):
                if t == 0 and (not isinstance(i, int) or i >= 2):
                    dve.wait_ge(s_msp, i - 1)
                for h in range(2):
                    dve.wait_ge(s_s, 16 * i + 2 * t + h + 1)
                    nc.vector.tensor_reduce(out=negm[:, u, t, h:h + 1], in_=ps_s[:, h, :], axis=AX.X,
                                            op=ALU.max, negate=True).then_inc(s_mx, 1)

            def output(i, u):
                dve.wait_ge(s_to, i + 1)
                t = ps_t[:, :].rearrange("p (j h a s) -> p j h a s", j=4, h=2, a=2)
                nc.vector.reciprocal(ro[:, u].rearrange("p j (h a) -> p j h a", h=2), t[:, :, :, :, DH]
                                     ).then_inc(s_ro, 1)
                dve.wait_ge(s_ro, i + 1)
                for a in range(2):
                    src = t[:, :, :, a, 0:DH]
                    r = ro[:, u].rearrange("p j (h a) -> p j h a", h=2)[:, :, :, a]
                    o = O[:, ds(i, 1), 4 * a:4 * a + 4, :].rearrange("p o j (h d) -> p (o j) h d", d=DH)
                    nc.vector.tensor_tensor(out=o, in0=src, in1=bcast(r, 3, DH), op=ALU.mult
                                            ).then_inc(s_eo, 1)

            def pair(i, u, nxt, nxt2, prev):
                for s in range(8):
                    if s + LEAD < 8 and nxt:
                        maxima(i + 1, 1 - u, s + LEAD)
                    if s + LEAD >= 8 and nxt2:
                        maxima(i + 2, u, s + LEAD - 8)
                    if s == 1 and prev:
                        output(i - 1, 1 - u)

            for t in range(8):
                maxima(0, 0, t)
            for t in range(LEAD):
                maxima(1, 1, t)
            pair(0, 0, True, True, False)
            pair(1, 1, True, True, True)
            with dve.Fori(1, PAIRS // 2 - 1) as k:
                for u in range(2):
                    pair(k * 2 + u, u, True, True, True)
            pair(PAIRS - 2, 0, True, False, True)
            pair(PAIRS - 1, 1, False, False, True)
            output(PAIRS - 1, 1)

        @block.scalar
        def _(act):
            def evac_q1(i, u, hh=None):
                if hh is not None:
                    act.wait_ge(s_m1[u], 32 * hh)
                act.wait_ge(s_tq1, i + 1)
                nc.scalar.activation(qT1[:, u, :], tb[:, :], ACT.Copy).then_inc(s_eq1, 1)

            def evac_k(i, u, h):
                if h is not None:
                    act.wait_ge(s_k2[u], 16 * h)
                act.wait_ge(s_tk, i + 1)
                nc.scalar.activation(kT1[:, u, :], tb[:, :], ACT.Copy).then_inc(s_ek, 1)

            def evac_q2(i, u, hh=None):
                if hh is not None:
                    act.wait_ge(s_m2[u], 32 * hh)
                act.wait_ge(s_tq2, i + 1)
                nc.scalar.activation(qT2[:, u, :], tb[:, :], ACT.Copy).then_inc(s_eq2, 1)

            def evac_o(i, u):
                act.wait_ge(s_pv, 8 * i + 10)
                nc.scalar.activation(oT[:, u, :], ps_o[:, :], ACT.Copy).then_inc(s_oe, 1)

            def exps(i, u, s):
                if True:
                    act.wait_ge(s_pv, 8 * i + s + 1)
                for n in range(4):
                    h, half = n % 2, n // 2
                    act.wait_ge(s_p, 32 * i + 4 * s + n + 1)
                    nc.scalar.activation(pT[:, (s % 2) * 4 + n, :], ps_p[:, h, :], ACT.Exp,
                                         scale=SCALE).then_inc(s_e, 1)

            def pair(i, u, h, nxt, nxt2):
                for s in range(8):
                    exps(i, u, s)
                    if s == 3 and nxt2:
                        evac_q1(i + 2, u, h + 1)
                    if s == 4 and nxt2:
                        evac_k(i + 2, u, h + 1)
                    if s == 6 and nxt:
                        evac_q2(i + 1, 1 - u, h + u)
                evac_o(i, u)

            evac_q1(0, 0)
            evac_k(0, 0, None)
            evac_q1(1, 1)
            evac_k(1, 1, None)
            evac_q2(0, 0)
            pair(0, 0, 0, True, True)
            pair(1, 1, 0, True, True)
            with act.Fori(1, PAIRS // 2 - 1) as k:
                for u in range(2):
                    pair(k * 2 + u, u, k, True, True)
            pair(PAIRS - 2, 0, PAIRS // 2 - 1, True, False)
            pair(PAIRS - 1, 1, None, False, False)

        @block.tensor
        def _(pe):
            def rows(h, n):
                return slice(h * HR, h * HR + n)

            def transposes(src, u):
                for t in range(G8):
                    last = nc.tensor.transpose(tb[:, t * P:(t + 1) * P],
                                               src[:, u, t].rearrange("p h s -> p (h s)"), identb[:, :])
                return last

            def q1(i, u, before):
                for s, v in before:
                    pe.wait_ge(s, v)
                pe.wait_ge(s_bld, i + 1)
                transposes(qx, u).then_inc(s_tq1, 1)

            def k1(i, u):
                pe.wait_ge(s_eq1, i + 1)
                transposes(kx, u).then_inc(s_tk, 1)

            def q2(i, u, before):
                pe.wait_ge(*before)
                pe.wait_ge(s_msp, i + 1)
                transposes(qx, u).then_inc(s_tq2, 1)

            def o1(i, u, before):
                pe.wait_ge(*before)
                pe.wait_ge(s_oe, i + 2)
                for j in range(4):
                    last = nc.tensor.transpose(ps_t[:, j * P:(j + 1) * P], oT[:, u, j * P:(j + 1) * P], ident[:, :])
                last.then_inc(s_to, 1)

            def by_query(i, u, hh, t):
                if t == 0:
                    pe.wait_ge(s_m1[u], 32 * (hh + 1))
                    pe.wait_ge(s_ek, i + 1)
                for h in range(2):
                    pe.wait_ge(s_mx, 16 * i + 2 * t + h + 1)
                    for half in range(2):
                        mm = nc.tensor.matmul(ps_s[:, h, half * CW:(half + 1) * CW],
                                              qm1[:, u, h, t * P:(t + 1) * P],
                                              kT1[:, u, half * CW:(half + 1) * CW],
                                              start=True, stop=True)
                    mm.then_inc(s_s, 1)

            def by_key(i, u, hh, s, half):
                if s == 0 and half == 0:
                    pe.wait_ge(s_m2[u], 32 * (hh + 1))
                    pe.wait_ge(s_k2[u], 16 * (hh + 1))
                for h in range(2):
                    n = 2 * half + h
                    pe.wait_ge(s_e, 32 * i + 4 * s + n + 1)
                    nc.tensor.matmul(ps_p[:, h, :], kT2[:, u, s * P:(s + 1) * P],
                                     qm2[:, u, h, half * CW:(half + 1) * CW],
                                     start=True, stop=True).then_inc(s_p, 1)

            def values(i, u, s):
                if s == 0:
                    pe.wait_ge(s_vx, i + 1)
                    pe.wait_ge(s_oe, i + 1)
                pe.wait_ge(s_e, 32 * i + 4 * s + 6)
                for n in range(4):
                    h, half = n % 2, n // 2
                    g = 32 * (2 * h + half)
                    last = nc.tensor.matmul(ps_o[g:g + 32, :], vx[:, u, s, h, :], pT[:, (s % 2) * 4 + n, :],
                                            start=(s == 0), stop=(s == 7))
                last.then_inc(s_pv, 1)

            def pair(i, u, hh, nxt, nxt2, prev):
                for s in range(8):
                    by_key(i, u, hh, s, 0)
                    if s + LEAD < 8 and nxt:
                        by_query(i + 1, 1 - u, hh + u, s + LEAD)
                    if s + LEAD >= 8 and nxt2:
                        by_query(i + 2, u, hh + 1, s + LEAD - 8)
                    by_key(i, u, hh, s, 1)
                    if s:
                        values(i, u, s - 1)
                    if s == 1 and prev:
                        o1(i - 1, 1 - u, (s_eq2, i + 1))
                    if s == 3 and nxt2:
                        q1(i + 2, u, [(s_eo, 2 * i)] if prev else [(s_eq2, i + 1)])
                    if s == 4 and nxt2:
                        k1(i + 2, u)
                    if s == 6 and nxt:
                        q2(i + 1, 1 - u, (s_ek, i + 3) if nxt2 else (s_eo, 2 * i))
                values(i, u, 7)

            q1(0, 0, [])
            k1(0, 0)
            for t in range(8):
                by_query(0, 0, 0, t)
            q1(1, 1, [(s_ek, 1)])
            k1(1, 1)
            for t in range(LEAD):
                by_query(1, 1, 0, t)
            q2(0, 0, (s_ek, 2))
            pair(0, 0, 0, True, True, False)
            pair(1, 1, 0, True, True, True)
            with pe.Fori(1, PAIRS // 2 - 1) as k:
                for u in range(2):
                    pair(k * 2 + u, u, k, True, True, True)
            pair(PAIRS - 2, 0, PAIRS // 2 - 1, True, False, True)
            pair(PAIRS - 1, 1, PAIRS // 2 - 1, False, False, True)
            o1(PAIRS - 1, 1, (s_eo, 2 * (PAIRS - 1)))


def stage_project(nc, sems, W, K, A):
    X, ident, O = K["X"], K["ident"], A["o"]
    st = ExitStack()
    with st:
        m = Pool_(nc, st, sems, "wo")
        w = m.sb("w", [P, D])
        oc = m.sb("oc", [P, 2, CT, D])
        oT = m.sb("oT", [P, 2, CW])
        ps_t = m.ps("ps_t", [P, 2, CW])
        ps_y = m.ps("ps_y", [P, 2, CT, D])
        s_w = m.sem("s_w")
        s_oc = m.sem("s_oc")
        s_t = m.sem("s_t")
        s_oT = m.sem("s_oT")
        s_y = m.sem("s_y")
        s_x = m.sem("s_x")
        block = st.enter_context(nc.Block())

        @block.sync
        def _(sp):
            sp.dma_start(w[:, :], W["wo"]).then_inc(s_w, 16)
            sp.wait_ge(s_w, 16)

        @block.gpsimd
        def _(pool):
            with pool.Fori(0, CHUNKS // 2) as k:
                for u in range(2):
                    c = k * 2 + u
                    pool.wait_ge(s_t, c + 1)
                    for j in range(CT):
                        nc.gpsimd.tensor_tensor(out=oc[:, u, j, :].rearrange("p (h w) -> p h w", w=16),
                                                in0=O[:, ds(k * 8, 8), 4 * u + j, :],
                                                in1=bcast(bcast(K["zero"][:, 0:1], 1, 8), 2, 16)[:, :, :, 0],
                                                op=ALU.add).then_inc(s_oc, 1)

        @block.tensor
        def _(pe):
            pe.wait_ge(s_w, 16)
            with pe.Fori(0, CHUNKS // 2) as k:
                for u in range(2):
                    c = k * 2 + u
                    pe.wait_ge(s_oc, 4 * c + 4)
                    pe.wait_ge(s_oT, c + 1)
                    for j in range(CT):
                        last = nc.tensor.transpose(ps_t[:, u, j * P:(j + 1) * P], oc[:, u, j, :], ident[:, :])
                    last.then_inc(s_t, 1)
                    pe.wait_ge(s_oT, c + 3)
                    pe.wait_ge(s_x, c + 1)
                    for j in range(CT):
                        last = nc.tensor.matmul(ps_y[:, u, j, :], oT[:, u, j * P:(j + 1) * P], w[:, :],
                                                start=True, stop=True)
                    last.then_inc(s_y, 1)

        @block.scalar
        def _(act):
            with act.Fori(0, CHUNKS // 2) as k:
                for u in range(2):
                    c = k * 2 + u
                    act.wait_ge(s_y, c + 1)
                    act.wait_ge(s_t, c + 3)
                    nc.scalar.activation(oT[:, u, :], ps_t[:, u, :], ACT.Copy).then_inc(s_oT, 1)

        @block.vector
        def _(dve):
            m.seed(s_t, 2)
            m.seed(s_oT, 2)
            m.seed(s_x, 2)
            m.seed(s_y, 2)
            with dve.Fori(0, CHUNKS // 2) as k:
                for u in range(2):
                    c = k * 2 + u
                    dve.wait_ge(s_y, c + 3)
                    xc = X[:, ds(c * CT, CT), :]
                    nc.vector.tensor_tensor(out=xc, in0=ps_y[:, u], in1=xc, op=ALU.add).then_inc(s_x, 1)




EX, TOPK, HID, CAP = 64, 8, 96, 32
SLOTS_X = EX * CAP
ST = SLOTS_X // P
FAR = 1000.0


def stage_route(nc, sems, tag, K, M, S):
    X, ident = K["X"], K["ident"]
    pos, wt, H, nact = S["pos"], S["wt"], S["H"], S["nact"]
    st = ExitStack()
    with st:
        m = Pool_(nc, st, sems, tag)
        norm = Norm(m, X, ident)
        lmax = m.sb("lmax", [P, CT])
        ls = m.sb("ls", [P, CT, EX])
        ex = m.sb("ex", [P, CT, EX])
        sm = m.sb("sm", [P, CT])
        rs = m.sb("rs", [P, CT])
        pr = m.sb("pr", [P, CT, EX])
        v8 = m.sb("v8", [P, CT, TOPK])
        rest = m.sb("rest", [P, CT, EX])
        mask = m.sb("mask", [P, CT, EX], BF16)
        s8 = m.sb("s8", [P, CT])
        r8 = m.sb("r8", [P, CT])
        pt = m.sb("pt", [P, CT, EX])
        carry = m.sb("carry", [P, EX])
        low = m.sb("low", [P, 1])
        open_ = m.sb("open", [P, 1])
        cnt = m.sb("cnt", [P, 1])
        ps_tr = m.ps("ps_tr", [P, CW])
        ps_lg = m.ps("ps_lg", [P, CT, EX])
        ps_c = m.ps("ps_c", [P, CT, EX])
        ps_n = m.ps("ps_n", [P, EX])
        s_lg = m.sem("s_lg")
        s_d = m.sem("s_d")
        s_ls = m.sem("s_ls")
        s_ex = m.sem("s_ex")
        s_mk = m.sem("s_mk")
        s_c = m.sem("s_c")
        s_h = [m.sem("s_h0"), m.sem("s_h1")]
        block = st.enter_context(nc.Block())
        STEPS = 21

        @block.sync
        def _(sp):
            with sp.Fori(0, CHUNKS // 2) as k:
                for u in range(2):
                    c = k * 2 + u
                    sp.wait_ge(norm.s_h, (c + 1) * CT)
                    sp.dma_start(H[:, ds(c * CT, CT), :], norm.h[:, u]).then_inc(s_h[u], 16)
            sp.wait_ge(s_h[0], CHUNKS // 2 * 16)
            sp.wait_ge(s_h[1], CHUNKS // 2 * 16 + 16)

        @block.vector
        def _(dve):
            norm.dve_eps(nc)
            m.seed(s_h[1], 16)
            nc.vector.memset(carry[:, :], FAR).then_inc(s_d, 1)
            nc.vector.memset(cnt[:, :], 0.0).then_inc(s_d, 1)
            norm.dve_stats(nc, 0, 0)
            norm.dve_apply(nc, 0, 0)

            def chunk(k, u, more):
                c = k * 2 + u
                base = c * STEPS + 2

                def step(i, ins):
                    ins.then_inc(s_d, 1)
                    dve.wait_ge(s_d, base + i)

                def tick():
                    nc.vector.memset(norm.tick[:, :], 0.0)
                dve.wait_ge(s_d, c * STEPS + 2)
                step(1, nc.vector.tensor_reduce(out=low[:, :], in_=carry[:, :], axis=AX.X, op=ALU.min))
                step(2, nc.vector.tensor_scalar(out=open_[:, :], in0=low[:, :], scalar1=FAR + CAP, scalar2=None,
                                                op0=ALU.is_lt))
                step(3, nc.vector.tensor_tensor(out=cnt[:, :], in0=cnt[:, :], in1=open_[:, :], op=ALU.add))
                dve.wait_ge(s_lg, c + 1)
                step(4, nc.vector.tensor_reduce(out=lmax[:, :], in_=ps_lg[:, :, :], axis=AX.X, op=ALU.max))
                nc.vector.tensor_tensor(out=ls[:, :, :], in0=ps_lg[:, :, :], in1=bcast(lmax[:, :], 2, EX),
                                        op=ALU.subtract).then_inc(s_ls, 1)
                if more:
                    norm.dve_stats(nc, c + 1, 1 - u)
                dve.wait_ge(s_ex, c + 1)
                step(5, nc.vector.tensor_reduce(out=sm[:, :], in_=ex[:, :, :], axis=AX.X, op=ALU.add))
                step(6, nc.vector.reciprocal(rs[:, :], sm[:, :]))
                step(7, nc.vector.tensor_tensor(out=pr[:, :, :], in0=ex[:, :, :], in1=bcast(rs[:, :], 2, EX),
                                                op=ALU.mult))
                tick()
                for j in range(CT):
                    nc.vector.max(v8[:, j, :], pr[:, j, :]).then_inc(s_d, 1)
                dve.wait_ge(s_d, base + 11)
                tick()
                for j in range(CT):
                    nc.vector.match_replace(out=rest[:, j, :], in_to_replace=v8[:, j, :], in_values=pr[:, j, :],
                                            imm_value=-1.0).then_inc(s_d, 1)
                dve.wait_ge(s_d, base + 15)
                nc.vector.tensor_scalar(out=mask[:, :, :], in0=rest[:, :, :], scalar1=0.0, scalar2=None,
                                        op0=ALU.is_lt).then_inc(s_mk, 1)
                step(16, nc.vector.tensor_reduce(out=s8[:, :], in_=v8[:, :, :], axis=AX.X, op=ALU.add))
                step(17, nc.vector.reciprocal(r8[:, :], s8[:, :]))
                step(18, nc.vector.tensor_tensor(out=wt[:, ds(c * CT, CT), :], in0=pr[:, :, :],
                                                 in1=bcast(r8[:, :], 2, EX), op=ALU.mult))
                if more:
                    dve.wait_ge(s_h[1 - u], (k + 1) * 16)
                    norm.dve_apply(nc, c + 1, 1 - u)
                dve.wait_ge(s_mk, c + 1)
                dve.wait_ge(s_c, c + 1)
                step(19, nc.vector.scalar_tensor_tensor(out=pt[:, :, :], in0=mask[:, :, :], scalar=-FAR,
                                                        in1=ps_c[:, :, :], op0=ALU.mult, op1=ALU.add))
                step(20, nc.vector.tensor_tensor(out=pos[:, ds(c * CT, CT), :], in0=pt[:, :, :],
                                                 in1=bcast(carry[:, :], 1, CT), op=ALU.add))
                step(21, nc.vector.tensor_tensor(out=carry[:, :], in0=ps_n[:, :], in1=carry[:, :], op=ALU.add))

            with dve.Fori(0, CHUNKS // 2 - 1) as k:
                for u in range(2):
                    chunk(k, u, True)
            chunk(CHUNKS // 2 - 1, 0, True)
            chunk(CHUNKS // 2 - 1, 1, False)
            nc.vector.tensor_copy(nact[:, :], cnt[:, :])

        @block.scalar
        def _(act):
            act.wait_ge(norm.s_eps, 1)
            norm.act_std(nc, 0, 0)
            norm.act_hT(nc, 0, 0, ps_tr)

            def chunk(c, u, more):
                act.wait_ge(s_ls, c + 1)
                nc.scalar.activation(ex[:, :, :], ls[:, :, :], ACT.Exp).then_inc(s_ex, 1)
                if more:
                    norm.act_std(nc, c + 1, 1 - u)
                    norm.act_hT(nc, c + 1, 1 - u, ps_tr)

            with act.Fori(0, CHUNKS // 2 - 1) as k:
                for u in range(2):
                    chunk(k * 2 + u, u, True)
            chunk(CHUNKS - 2, 0, True)
            chunk(CHUNKS - 1, 1, False)

        @block.tensor
        def _(pe):
            norm.pe_transpose(nc, 0, 0, ps_tr)

            def chunk(c, u, more):
                pe.wait_ge(norm.s_hT, c + 1)
                pe.wait_ge(s_d, c * STEPS + 2)
                for s in range(CT):
                    last = nc.tensor.matmul(ps_lg[:, s, :], norm.hT[:, u, s * P:(s + 1) * P], M["wr"][:, :],
                                            start=True, stop=True)
                last.then_inc(s_lg, 1)
                if more:
                    norm.pe_transpose(nc, c + 1, 1 - u, ps_tr)
                pe.wait_ge(s_mk, c + 1)
                nc.tensor.matmul(ps_c[:, :, :], K["triub"][:, :], mask[:, :, :], start=True, stop=False,
                                 skip_group_check=True)
                for j in range(1, CT):
                    nc.tensor.matmul(ps_c[:, j:CT, :], K["onesb"][:, :],
                                     mask[:, 0:CT - j, :], start=False, stop=(j == CT - 1),
                                     skip_group_check=True)
                for j in range(CT):
                    last = nc.tensor.matmul(ps_n[:, :], K["onesb"][:, :], mask[:, j, :], start=(j == 0),
                                            stop=(j == CT - 1))
                last.then_inc(s_c, 1)

            with pe.Fori(0, CHUNKS // 2 - 1) as k:
                for u in range(2):
                    chunk(k * 2 + u, u, True)
            chunk(CHUNKS - 2, 0, True)
            chunk(CHUNKS - 1, 1, False)


def stage_dispatch(nc, sems, tag, K, S):
    pos, H, XT = S["pos"], S["H"], S["XT"]
    st = ExitStack()
    with st:
        m = Pool_(nc, st, sems, tag)
        hc = m.sb("hc", [P, CT * D])
        hp = m.sb("hp", [P, 3, CT * D], BF16)
        r = m.sb("r", [P, 2, CT * D])
        oh = m.sb("oh", [P, CT, EX, CAP], BF16)
        ps_x = m.ps("ps_x", [P, 4, CW])
        s_h = m.sem("s_h")
        s_p = m.sem("s_p")
        s_oh = m.sem("s_oh")
        s_x = m.sem("s_x")
        s_xa = m.sem("s_xa")
        s_z = m.sem("s_z")
        block = st.enter_context(nc.Block())

        @block.sync
        def _(sp):
            n = sp.value_load(S["nact"][0:1, 0:1], min_val=1, max_val=CHUNKS)
            with sp.Fori(0, n) as c:
                sp.wait_ge(s_xa, c * 4 + 4)
                sp.dma_start(hc[:, :], H[:, ds(c * CT, CT), :].rearrange("p t d -> p (t d)")).then_inc(s_h, 16)

        @block.gpsimd
        def _(pool):
            n = pool.value_load(S["nact"][0:1, 0:1], min_val=1, max_val=CHUNKS)
            zero = bcast(K["zero"][:, 0:1], 1, CT * D)[:, :, 0]
            with pool.Fori(0, n) as c:
                def step(k, ins):
                    ins.then_inc(s_p, 1)
                    pool.wait_ge(s_p, c * 5 + k)
                pool.wait_ge(s_h, c * 16 + 16)
                step(1, nc.gpsimd.tensor_tensor(out=hp[:, 0, :], in0=hc[:, :], in1=zero, op=ALU.add))
                step(2, nc.gpsimd.tensor_tensor(out=r[:, 0, :], in0=hc[:, :], in1=hp[:, 0, :], op=ALU.subtract))
                step(3, nc.gpsimd.tensor_tensor(out=hp[:, 1, :], in0=r[:, 0, :], in1=zero, op=ALU.add))
                step(4, nc.gpsimd.tensor_tensor(out=r[:, 1, :], in0=r[:, 0, :], in1=hp[:, 1, :], op=ALU.subtract))
                step(5, nc.gpsimd.tensor_tensor(out=hp[:, 2, :], in0=r[:, 1, :], in1=zero, op=ALU.add))

        @block.vector
        def _(dve):
            nc.vector.memset(XT[:, :], 0.0).then_inc(s_z, 1)
            m.seed(s_xa, 4)
            dve.wait_ge(s_z, 1)
            n = dve.value_load(S["nact"][0:1, 0:1], min_val=1, max_val=CHUNKS)
            with dve.Fori(0, n) as c:
                dve.wait_ge(s_xa, c * 4 + 4)
                for j in range(CT):
                    row = pos[:, ds(c * CT + j, 1), :].rearrange("p o e -> p (o e)")
                    nc.vector.tensor_tensor(out=oh[:, j], in0=bcast(row, 2, CAP),
                                            in1=bcast(K["iota"][:, :], 1, EX), op=ALU.is_equal).then_inc(s_oh, 1)
                for q in range(4):
                    dve.wait_ge(s_x, c * 4 + q + 1)
                    nc.vector.tensor_tensor(out=XT[:, q * CW:(q + 1) * CW], in0=ps_x[:, q, :],
                                            in1=XT[:, q * CW:(q + 1) * CW], op=ALU.add).then_inc(s_xa, 1)

        @block.tensor
        def _(pe):
            n = pe.value_load(S["nact"][0:1, 0:1], min_val=1, max_val=CHUNKS)
            with pe.Fori(0, n) as c:
                pe.wait_ge(s_p, c * 5 + 5)
                pe.wait_ge(s_oh, c * 4 + 4)
                for q in range(4):
                    for j in range(CT):
                        for a in range(3):
                            last = nc.tensor.matmul(
                                ps_x[:, q, :], hp[:, a, j * D:(j + 1) * D],
                                oh[:, j].rearrange("p e c -> p (e c)")[:, q * CW:(q + 1) * CW],
                                start=(j == 0 and a == 0), stop=(j == CT - 1 and a == 2))
                    last.then_inc(s_x, 1)


def stage_experts(nc, sems, tag, M, S):
    XT, ysb = S["XT"], S["y"]
    wg, wu, wd = M["wg"], M["wu"], M["wd"]
    st = ExitStack()
    with st:
        m = Pool_(nc, st, sems, tag)
        sg = m.sb("sg", [HID, 4, CW])
        gu = m.sb("gu", [HID, 4, CW])
        ps_g = m.ps("ps_g", [HID, 2, CW])
        ps_u = m.ps("ps_u", [HID, 2, CW])
        ps_y = m.ps("ps_y", [P, 2, 4, D])
        s_gu = m.sem("s_gup")
        s_s = m.sem("s_s")
        s_g = m.sem("s_g")
        s_y = m.sem("s_y")
        s_ye = m.sem("s_ye")
        block = st.enter_context(nc.Block())

        @block.tensor
        def _(pe):
            def up(q):
                if q >= 2:
                    pe.wait_ge(s_g, q - 1)
                for e in range(16):
                    x = XT[:, q * CW + e * CAP:q * CW + (e + 1) * CAP]
                    nc.tensor.matmul(ps_g[:, q % 2, e * CAP:(e + 1) * CAP], wg[:, q * 16 + e, :], x,
                                     start=True, stop=True)
                    last = nc.tensor.matmul(ps_u[:, q % 2, e * CAP:(e + 1) * CAP], wu[:, q * 16 + e, :], x,
                                            start=True, stop=True)
                last.then_inc(s_gu, 1)

            def down(q):
                pe.wait_ge(s_g, q + 1)
                if q >= 2:
                    pe.wait_ge(s_ye, q - 1)
                for t in range(4):
                    for e in range(4):
                        n = t * 4 + e
                        last = nc.tensor.matmul(ps_y[e * CAP:(e + 1) * CAP, q % 2, t, :],
                                                gu[:, q, n * CAP:(n + 1) * CAP], wd[:, q * 16 + n, :],
                                                start=True, stop=True)
                last.then_inc(s_y, 1)

            for q in range(4):
                up(q)
                if q:
                    down(q - 1)
            down(3)

        @block.scalar
        def _(act):
            for q in range(4):
                act.wait_ge(s_gu, q + 1)
                nc.scalar.activation(sg[:, q, :], ps_g[:, q % 2, :], ACT.Silu).then_inc(s_s, 1)

        @block.vector
        def _(dve):
            for q in range(4):
                dve.wait_ge(s_s, q + 1)
                nc.vector.tensor_tensor(out=gu[:, q, :], in0=ps_u[:, q % 2, :], in1=sg[:, q, :],
                                        op=ALU.mult).then_inc(s_g, 1)
                if q:
                    dve.wait_ge(s_y, q)
                    nc.vector.tensor_copy(ysb[:, 4 * q - 4:4 * q, :], ps_y[:, (q - 1) % 2]).then_inc(s_ye, 1)
            dve.wait_ge(s_y, 4)
            nc.vector.tensor_copy(ysb[:, 12:16, :], ps_y[:, 1]).then_inc(s_ye, 1)


def stage_combine(nc, sems, tag, K, S):
    X, ident = K["X"], K["ident"]
    pos, wt, ysb = S["pos"], S["wt"], S["y"]
    st = ExitStack()
    with st:
        m = Pool_(nc, st, sems, tag)
        oh = m.sb("oh", [P, 2, EX, CAP])
        wT = m.sb("wT", [P, 4, CW])
        ps_t = m.ps("ps_t", [P, 4, CW])
        ps_o = m.ps("ps_o", [P, D])
        s_e = m.sem("s_e")
        s_w = m.sem("s_w")
        s_t = m.sem("s_t")
        s_v = m.sem("s_v")
        s_o = m.sem("s_o")
        s_x = m.sem("s_x")
        block = st.enter_context(nc.Block())

        @block.vector
        def _(dve):
            m.seed(s_t, 4)
            m.seed(s_v, 4)
            m.seed(s_o, 1)
            m.seed(s_x, 1)
            n = dve.value_load(S["nact"][0:1, 0:1], min_val=1, max_val=CHUNKS)
            with dve.Fori(0, n) as c:
                for j in range(CT):
                    t, v = c * CT + j, j % 2
                    row = pos[:, ds(t, 1), :].rearrange("p o e -> p (o e)")
                    w = wt[:, ds(t, 1), :].rearrange("p o e -> p (o e)")
                    dve.wait_ge(s_t, 4 * t + 4)
                    nc.vector.tensor_tensor(out=oh[:, 0], in0=bcast(row, 2, CAP),
                                            in1=bcast(K["iota"][:, :], 1, EX), op=ALU.is_equal).then_inc(s_e, 1)
                    dve.wait_ge(s_e, t + 1)
                    nc.vector.tensor_tensor(out=oh[:, 1], in0=oh[:, 0], in1=bcast(w, 2, CAP),
                                            op=ALU.mult).then_inc(s_w, 1)
                    dve.wait_ge(s_o, t + 2)
                    xt = X[:, ds(t, 1), :].rearrange("p o d -> p (o d)")
                    nc.vector.scalar_tensor_tensor(out=xt, in0=ps_o[:, :], scalar=0.5, in1=xt, op0=ALU.mult,
                                                   op1=ALU.add).then_inc(s_x, 1)

        @block.scalar
        def _(act):
            n = act.value_load(S["nact"][0:1, 0:1], min_val=1, max_val=CHUNKS)
            with act.Fori(0, n) as c:
                for j in range(CT):
                    t = c * CT + j
                    act.wait_ge(s_o, t + 1)
                    for q in range(4):
                        act.wait_ge(s_t, 4 * t + q + 5)
                        nc.scalar.activation(wT[:, q, :], ps_t[:, q, :], ACT.Copy).then_inc(s_v, 1)

        @block.tensor
        def _(pe):
            n = pe.value_load(S["nact"][0:1, 0:1], min_val=1, max_val=CHUNKS)
            with pe.Fori(0, n) as c:
                for j in range(CT):
                    t = c * CT + j
                    pe.wait_ge(s_w, t + 1)
                    flat = oh[:, 1].rearrange("p e c -> p (e c)")
                    for q in range(4):
                        pe.wait_ge(s_v, 4 * t + q + 1)
                        for s in range(4):
                            last = nc.tensor.transpose(ps_t[:, q, s * P:(s + 1) * P],
                                                       flat[:, (q * 4 + s) * P:(q * 4 + s + 1) * P], ident[:, :])
                        last.then_inc(s_t, 1)
                    pe.wait_ge(s_v, 4 * t + 8)
                    pe.wait_ge(s_x, t + 1)
                    for s in range(ST):
                        last = nc.tensor.matmul(ps_o[:, :], wT[:, s // 4, (s % 4) * P:(s % 4 + 1) * P], ysb[:, s, :],
                                                start=(s == 0), stop=(s == ST - 1))
                    last.then_inc(s_o, 1)


def moe(nc, sems, tag, K, M):
    st = ExitStack()
    with st:
        m = Pool_(nc, st, sems, tag)
        S = {"pos": m.sb("pos", [P, TILES, EX]), "wt": m.sb("wt", [P, TILES, EX]), "y": m.sb("y", [P, ST, D]),
             "nact": m.sb("nact", [P, 1], I32)}
        mid = ExitStack()
        with mid:
            m2 = Pool_(nc, mid, sems, tag + "m")
            S["XT"] = m2.sb("XT", [P, SLOTS_X])
            early = ExitStack()
            with early:
                S["H"] = Pool_(nc, early, sems, tag + "e").sb("H", [P, TILES, D])
                stage_route(nc, sems, tag + "r", K, M, S)
                stage_dispatch(nc, sems, tag + "d", K, S)
            stage_experts(nc, sems, tag + "x", M, S)
        stage_combine(nc, sems, tag + "c", K, S)


LEVELS = [N + 1] + [N >> k for k in range(1, 11)]
SCAN_EPS = 1e-8
LIFT = (3.4445, -4.7750, 2.0315)
POLISH = (1.875, -1.25, 0.375)
LIFTS, POLISHES = 14, 4


def stage_polar(nc, sems, W, K, Q):
    Y = Q["Y"]
    st = ExitStack()
    with st:
        m = Pool_(nc, st, sems, "po")
        X = m.sb("X", [P, 2, P])
        sq = m.sb("sq", [P, 2, P])
        rowsum = m.sb("rowsum", [P, 2])
        norm = m.sb("norm", [P, 2])
        inv = m.sb("inv", [P, 2])
        A = m.sb("A", [P, 2, P])
        TT = m.sb("TT", [P, 2, P])
        C = m.sb("C", [P, 2, P])
        aI = m.sb("aI", [P, 2, P])
        ps_n = m.ps("ps_n", [P, 2])
        ps_a = [m.ps(f"ps_a{w}", [P, P]) for w in range(2)]
        ps_x = [m.ps(f"ps_x{w}", [P, P]) for w in range(2)]
        ps_y = [m.ps(f"ps_y{w}", [P, P]) for w in range(2)]
        s_w = m.sem("s_w")
        s_i = m.sem("s_i")
        s_sq = m.sem("s_sq")
        s_n = m.sem("s_n")
        s_rt = m.sem("s_rt")
        s_iv = m.sem("s_iv")
        s_x0 = m.sem("s_x0")
        s_a = m.sem("s_a")
        s_as = m.sem("s_as")
        s_t = m.sem("s_t")
        s_a2 = m.sem("s_a2")
        s_c = m.sem("s_c")
        s_xy = m.sem("s_xy")
        s_xs = m.sem("s_xs")
        s_ys = m.sem("s_ys")
        block = st.enter_context(nc.Block())

        @block.sync
        def _(sp):
            for w in range(2):
                sp.dma_start(X[:, w, :], W["wp"][w]).then_inc(s_w, 16)
                sp.dma_start(Y[:, w, :], W["wpt"][w]).then_inc(s_w, 16)
            sp.wait_ge(s_w, 64)

        @block.scalar
        def _(act):
            act.wait_ge(s_w, 64)
            for w in range(2):
                nc.scalar.activation(sq[:, w, :], X[:, w, :], ACT.Square,
                                     accum_out=rowsum[:, w:w + 1]).then_inc(s_sq, 1)
            act.wait_ge(s_n, 1)
            nc.scalar.activation(norm[:, :], ps_n[:, :], ACT.Sqrt).then_inc(s_rt, 1)

            def step(n):
                for w in range(2):
                    act.wait_ge(s_a, 2 * n + w + 1)
                    nc.scalar.activation(A[:, w, :], ps_a[w][:, :], ACT.Copy).then_inc(s_as, 1)
                for w in range(2):
                    act.wait_ge(s_xy, 2 * n + w + 1)
                    nc.scalar.activation(X[:, w, :], ps_x[w][:, :], ACT.Copy).then_inc(s_xs, 1)
            with act.Fori(0, LIFTS + POLISHES) as n:
                step(n)

        @block.vector
        def _(dve):
            m.seed(s_c, 2)
            m.seed(s_xs, 2)
            m.seed(s_ys, 2)
            for k, (a, _, _) in enumerate((LIFT, POLISH)):
                nc.vector.tensor_scalar_mul(aI[:, k, :], K["ident"][:, :], a).then_inc(s_i, 1)
            dve.wait_ge(s_rt, 1)
            nc.vector.reciprocal(inv[:, :], norm[:, :]).then_inc(s_iv, 1)
            dve.wait_ge(s_iv, 1)
            for w in range(2):
                for z in (X, Y):
                    nc.vector.tensor_scalar(out=z[:, w, :], in0=z[:, w, :], scalar1=inv[:, w:w + 1], scalar2=None,
                                            op0=ALU.mult).then_inc(s_x0, 1)
            dve.wait_ge(s_i, 2)

            def step(n, k, b, c):
                for w in range(2):
                    dve.wait_ge(s_as, 2 * n + w + 1)
                    nc.vector.scalar_tensor_tensor(out=TT[:, w, :], in0=ps_a[w][:, :], scalar=b,
                                                   in1=aI[:, k, :], op0=ALU.mult, op1=ALU.add).then_inc(s_t, 1)
                for w in range(2):
                    dve.wait_ge(s_t, 2 * n + w + 1)
                    dve.wait_ge(s_a2, 2 * n + w + 1)
                    nc.vector.scalar_tensor_tensor(out=C[:, w, :], in0=ps_a[w][:, :], scalar=c, in1=TT[:, w, :],
                                                   op0=ALU.mult, op1=ALU.add).then_inc(s_c, 1)
                for w in range(2):
                    dve.wait_ge(s_xy, 2 * n + w + 1)
                    nc.vector.tensor_copy(Y[:, w, :], ps_y[w][:, :]).then_inc(s_ys, 1)
            with dve.Fori(0, LIFTS) as n:
                step(n, 0, LIFT[1], LIFT[2])
            with dve.Fori(LIFTS, LIFTS + POLISHES) as n:
                step(n, 1, POLISH[1], POLISH[2])

        @block.tensor
        def _(pe):
            pe.wait_ge(s_sq, 2)
            nc.tensor.matmul(ps_n[:, :], K["ones"][:, :], rowsum[:, :], start=True, stop=True).then_inc(s_n, 1)
            pe.wait_ge(s_x0, 4)
            with pe.Fori(0, LIFTS + POLISHES) as n:
                pe.wait_ge(s_xs, 2 * n + 2)
                pe.wait_ge(s_c, 2 * n + 2)
                for w in range(2):
                    nc.tensor.matmul(ps_a[w][:, :], X[:, w, :], X[:, w, :], start=True, stop=True).then_inc(s_a, 1)
                for w in range(2):
                    pe.wait_ge(s_as, 2 * n + w + 1)
                    pe.wait_ge(s_t, 2 * n + w + 1)
                    nc.tensor.matmul(ps_a[w][:, :], A[:, w, :], A[:, w, :], start=True, stop=True).then_inc(s_a2, 1)
                pe.wait_ge(s_ys, 2 * n + 2)
                for w in range(2):
                    pe.wait_ge(s_c, 2 * n + w + 3)
                    nc.tensor.matmul(ps_x[w][:, :], Y[:, w, :], C[:, w, :], start=True, stop=True)
                    nc.tensor.matmul(ps_y[w][:, :], C[:, w, :], Y[:, w, :], start=True, stop=True).then_inc(s_xy, 1)


def stage_scan_in(nc, sems, W, K, Q):
    X, ident = K["X"], K["ident"]
    E0, vT = Q["E"][0], Q["vT"]
    st = ExitStack()
    with st:
        m = Pool_(nc, st, sems, "si")
        norm = Norm(m, X, ident)
        w = m.sb("w", [P, 2, D])
        idn = m.sb("idn", [P, 1])
        ps_tr = m.ps("ps_tr", [P, CW])
        ps_q = m.ps("ps_q", [P, 2, CW])
        s_w = m.sem("s_w")
        s_p = m.sem("s_p")
        s_e = m.sem("s_e")
        block = st.enter_context(nc.Block())

        @block.sync
        def _(sp):
            sp.dma_start(w[:, :, :], W["wqv"]).then_inc(s_w, 16)
            sp.dma_start(idn[:, :], W["identity"]).then_inc(s_w, 16)
            sp.wait_ge(s_w, 32)

        @block.vector
        def _(dve):
            norm.dve_eps(nc)
            m.seed(s_e, 2)
            norm.dve_stats(nc, 0, 0)
            norm.dve_apply(nc, 0, 0)
            dve.wait_ge(s_w, 32)
            nc.vector.tensor_copy(E0[:, :, 0], bcast(idn[:, 0:1], 1, B)[:, :, 0])

            def chunk(c, u, b, more):
                if more:
                    norm.dve_stats(nc, c + 1, 1 - u)
                    norm.dve_apply(nc, c + 1, 1 - u)
                for r in range(2):
                    dst = E0[:, ds(b, 1), 1 + u * CW:1 + (u + 1) * CW] if r == 0 else vT[:, ds(b, 1), u * CW:(u + 1) * CW]
                    dve.wait_ge(s_p, 2 * c + r + 1)
                    nc.vector.tensor_scalar(out=dst.rearrange("p o n -> p (o n)"), in0=ps_q[:, r, :], scalar1=0.0,
                                            scalar2=None, op0=ALU.add).then_inc(s_e, 1)

            with dve.Fori(0, CHUNKS // 2 - 1) as k:
                for u in range(2):
                    chunk(k * 2 + u, u, k, True)
            chunk(CHUNKS - 2, 0, B - 1, True)
            chunk(CHUNKS - 1, 1, B - 1, False)

        @block.scalar
        def _(act):
            act.wait_ge(norm.s_eps, 1)
            norm.act_std(nc, 0, 0)
            norm.act_hT(nc, 0, 0, ps_tr)
            with act.Fori(0, CHUNKS // 2 - 1) as k:
                for u in range(2):
                    norm.act_std(nc, k * 2 + u + 1, 1 - u)
                    norm.act_hT(nc, k * 2 + u + 1, 1 - u, ps_tr)
            norm.act_std(nc, CHUNKS - 1, 1)
            norm.act_hT(nc, CHUNKS - 1, 1, ps_tr)

        @block.tensor
        def _(pe):
            pe.wait_ge(s_w, 32)
            norm.pe_transpose(nc, 0, 0, ps_tr)

            def chunk(c, u, more):
                pe.wait_ge(norm.s_hT, c + 1)
                for r in range(2):
                    pe.wait_ge(s_e, 2 * c + r + 1)
                    nc.tensor.matmul(ps_q[:, r, :], w[:, r, :], norm.hT[:, u, :], start=True,
                                     stop=True).then_inc(s_p, 1)
                if more:
                    norm.pe_transpose(nc, c + 1, 1 - u, ps_tr)

            with pe.Fori(0, CHUNKS // 2 - 1) as k:
                for u in range(2):
                    chunk(k * 2 + u, u, True)
            chunk(CHUNKS - 2, 0, True)
            chunk(CHUNKS - 1, 1, False)


def scan_combines():
    stages = []
    last = len(LEVELS) - 1
    for l in range(last):
        stages.append(("down", l, LEVELS[l + 1], (l, 0, 2), (l, 1, 2), (l + 1, 0, 1)))
    for l in range(last - 1, -1, -1):
        n = LEVELS[l] // 2 - (LEVELS[l] % 2 == 0)
        stages.append(("up", l, n, (l + 1, 0, 1), (l, 2, 2), (l, 2, 2)))
    out = []
    for kind, l, n, left, right, dst in stages:
        per = max(1, min(B, CW // n)) if n else 0
        out.append((kind, l, [(b, per, n, left, right, dst) for b in range(0, B, per)] if n else []))
    return out


def stage_scan_tree(nc, sems, K, Q):
    E_, Y = Q["E"], Q["Y"]
    st = ExitStack()
    with st:
        m = Pool_(nc, st, sems, "sc")
        sq = m.sb("sq", [P, 2, CW])
        rt = m.sb("rt", [P, 2, CW])
        rc = m.sb("rc", [P, 2, CW])
        eps = m.sb("eps", [P, 1])
        ps_z = m.ps("ps_z", [P, 2, CW])
        ps_m = m.ps("ps_m", [P, 2, CW])
        s_eps = m.sem("s_eps")
        s_z = m.sem("s_z")
        s_sq = m.sem("s_sq")
        s_m = m.sem("s_m")
        s_rt = m.sem("s_rt")
        s_rc = m.sem("s_rc")
        s_o = m.sem("s_o")
        s_cp = m.sem("s_cp")
        block = st.enter_context(nc.Block())
        plan = scan_combines()

        def view(x, b, per, n):
            level, first, step = x
            return E_[level][:, b:b + per, first:first + step * (n - 1) + 1:step]

        def flat(t, v, per, n):
            return t[:, v, 0:per * n].rearrange("p (b n) -> p b n", n=n)

        @block.tensor
        def _(pe):
            g = ups = 0

            def sums(g, per, n):
                pe.wait_ge(s_sq, g + 1)
                nc.tensor.matmul(ps_m[:, g % 2, 0:per * n], K["ones"][:, :], sq[:, g % 2, 0:per * n],
                                 start=True, stop=True).then_inc(s_m, 1)
            for kind, l, combos in plan:
                if g:
                    pe.wait_ge(s_o, g)
                if ups:
                    pe.wait_ge(s_cp, ups)
                for k, (b, per, n, left, right, dst) in enumerate(combos):
                    if k >= 2:
                        pe.wait_ge(s_o, g - 1)
                    z = flat(ps_z, g % 2, per, n)
                    nc.tensor.matmul(z, Y[:, 0, :], view(left, b, per, n), start=True, stop=False)
                    nc.tensor.matmul(z, Y[:, 1, :], view(right, b, per, n), start=False, stop=True).then_inc(s_z, 1)
                    if k:
                        sums(g - 1, per, n)
                    g += 1
                if combos:
                    sums(g - 1, per, n)
                ups += kind == "up"

        @block.scalar
        def _(act):
            act.wait_ge(s_eps, 1)
            g = 0

            def roots(g, per, n):
                act.wait_ge(s_m, g + 1)
                nc.scalar.activation(rt[:, g % 2, 0:per * n], ps_m[:, g % 2, 0:per * n], ACT.Sqrt,
                                     bias=eps[:, 0:1], scale=1.0 / D).then_inc(s_rt, 1)
            for kind, l, combos in plan:
                for k, (b, per, n, *_) in enumerate(combos):
                    act.wait_ge(s_z, g + 1)
                    nc.scalar.activation(sq[:, g % 2, 0:per * n], ps_z[:, g % 2, 0:per * n],
                                         ACT.Square).then_inc(s_sq, 1)
                    if k:
                        roots(g - 1, per, n)
                    g += 1
                if combos:
                    roots(g - 1, per, n)

        @block.gpsimd
        def _(pool):
            g = ups = 0
            for kind, l, combos in plan:
                if kind == "up":
                    if g:
                        pool.wait_ge(s_o, g)
                    if ups:
                        pool.wait_ge(s_cp, ups)
                    n = LEVELS[l] // 2
                    nc.gpsimd.tensor_copy(E_[l][:, :, 1:2 * n:2], E_[l + 1][:, :, 0:n]).then_inc(s_cp, 1)
                    ups += 1
                g += len(combos)

        @block.vector
        def _(dve):
            nc.vector.memset(eps[:, :], SCAN_EPS).then_inc(s_eps, 1)
            g = 0
            for kind, l, combos in plan:
                for b, per, n, left, right, dst in combos:
                    dve.wait_ge(s_rt, g + 1)
                    nc.vector.reciprocal(rc[:, g % 2, 0:per * n], rt[:, g % 2, 0:per * n]).then_inc(s_rc, 1)
                    dve.wait_ge(s_rc, g + 1)
                    nc.vector.tensor_tensor(out=view(dst, b, per, n), in0=flat(ps_z, g % 2, per, n),
                                            in1=flat(rc, g % 2, per, n), op=ALU.mult).then_inc(s_o, 1)
                    g += 1


def stage_scan_out(nc, sems, W, K, Q):
    X = K["X"]
    E0, vT = Q["E"][0], Q["vT"]
    st = ExitStack()
    with st:
        m = Pool_(nc, st, sems, "so")
        w = m.sb("w", [P, D])
        pr = m.sb("pr", [P, 2, CW])
        ps_y = m.ps("ps_y", [P, 2, CT, D])
        s_w = m.sem("s_w")
        s_pr = m.sem("s_pr")
        s_y = m.sem("s_y")
        s_x = m.sem("s_x")
        block = st.enter_context(nc.Block())

        @block.sync
        def _(sp):
            sp.dma_start(w[:, :], W["wc"]).then_inc(s_w, 16)
            sp.wait_ge(s_w, 16)

        @block.vector
        def _(dve):
            m.seed(s_y, 2)
            m.seed(s_x, 2)

            def product(c, u, b):
                dve.wait_ge(s_y, c + 1)
                nc.vector.tensor_tensor(out=pr[:, u, :],
                                        in0=E0[:, ds(b, 1), 1 + u * CW:1 + (u + 1) * CW].rearrange("p o n -> p (o n)"),
                                        in1=vT[:, ds(b, 1), u * CW:(u + 1) * CW].rearrange("p o n -> p (o n)"),
                                        op=ALU.mult).then_inc(s_pr, 1)

            def add(c, u):
                dve.wait_ge(s_y, c + 3)
                xc = X[:, ds(c * CT, CT), :]
                nc.vector.tensor_tensor(out=xc, in0=ps_y[:, u], in1=xc, op=ALU.add).then_inc(s_x, 1)
            product(0, 0, 0)
            with dve.Fori(0, CHUNKS // 2 - 1) as k:
                product(2 * k + 1, 1, k)
                add(2 * k, 0)
                product(2 * k + 2, 0, k + 1)
                add(2 * k + 1, 1)
            product(CHUNKS - 1, 1, B - 1)
            add(CHUNKS - 2, 0)
            add(CHUNKS - 1, 1)

        @block.tensor
        def _(pe):
            pe.wait_ge(s_w, 16)
            with pe.Fori(0, CHUNKS // 2) as k:
                for u in range(2):
                    c = k * 2 + u
                    pe.wait_ge(s_x, c + 1)
                    pe.wait_ge(s_pr, c + 1)
                    for j in range(CT):
                        last = nc.tensor.matmul(ps_y[:, u, j, :], pr[:, u, j * P:(j + 1) * P], w[:, :],
                                                start=True, stop=True)
                    last.then_inc(s_y, 1)


def stage_scan(nc, sems, W, K):
    st = ExitStack()
    with st:
        m = Pool_(nc, st, sems, "s")
        Q = {"Y": m.sb("Y", [P, 2, P]), "vT": m.sb("vT", [P, B, N]),
             "E": [m.sb(f"E{k}", [P, B, n]) for k, n in enumerate(LEVELS)]}
        stage_polar(nc, sems, W, K, Q)
        stage_scan_in(nc, sems, W, K, Q)
        stage_scan_tree(nc, sems, K, Q)
        stage_scan_out(nc, sems, W, K, Q)


def stage_store(nc, sems, K, out):
    st = ExitStack()
    with st:
        m = Pool_(nc, st, sems, "st")
        s_out = m.sem("s_out")
        block = st.enter_context(nc.Block())

        @block.sync
        def _(sp):
            o = out.rearrange("b (n p) d -> p (b n) d", p=P)
            for q in range(4):
                sp.dma_start(o[:, q * 8:q * 8 + 8, :], K["X"][:, q * 8:q * 8 + 8, :]).then_inc(s_out, 16)
            sp.wait_ge(s_out, 64)


def program(nc, W, out, stages="fafmsm"):
    st = ExitStack()
    with st:
        sems = st
        m = Pool_(nc, st, sems, "g")
        K = {"X": m.sb("X", [P, TILES, D]), "ident": m.sb("ident", [P, P]), "ones": m.sb("ones", [P, P]),
             "triu": m.sb("triu", [P, P]), "identb": m.sb("identb", [P, P], BF16),
             "onesb": m.sb("onesb", [P, P], BF16), "triub": m.sb("triub", [P, P], BF16),
             "iota": m.sb("iota", [P, CAP]), "zero": m.sb("zero", [P, 1])}
        stage_load(nc, sems, W, K)
        R = {"w1": m.sb("w1", [P, E + 1, I]), "w3": m.sb("w3", [P, E + 1, I]),
             "w2": m.sb("w2", [P, 3, E + 1, D]), "wr": m.sb("wr", [P, E]), "br": m.sb("br", [1, E]),
             "rev": m.sb("rev", [P, E]), "steps": m.sb("steps", [P, SLOT_TILES + TILES])}
        K["Hs"] = nc.dram_tensor("Hs", (SLOT_TILES * P, D), F32, kind="Internal").ap()
        K["Ys"] = nc.dram_tensor("Ys", (SLOT_TILES * P, D), F32, kind="Internal").ap()
        with nc.cleanup_on_exit():
            if stages[0] == "f":
                ffn(nc, sems, "fa", W, K, R, True)
        attn = ExitStack()
        with nc.cleanup_on_exit(), attn:
            ma = Pool_(nc, attn, sems, "a")
            A = {n: ma.sb(n, [P, PAIRS, PT_, 2 * DH]) for n in "qkvo"}
            if stages[1] == "a":
                stage_qkv(nc, sems, W, K, A)
                stage_attention(nc, sems, K, A)
                stage_project(nc, sems, W, K, A)
        if stages[2:] == "...":
            stage_store(nc, sems, K, out)
            return
        M = {"wr": m.sb("xwr", [P, EX]), "wg": m.sb("xwg", [P, EX, HID]), "wu": m.sb("xwu", [P, EX, HID]),
             "wd": m.sb("xwd", [HID, EX, D])}
        with nc.cleanup_on_exit():
            if stages[2] == "f":
                ffn(nc, sems, "fb", W, K, R, stages[0] != "f", M)
            elif stages[3:] != "...":
                stage_moe_weights(nc, sems, W, M)
        with nc.cleanup_on_exit():
            if stages[3] == "m":
                moe(nc, sems, "ma", K, M)
        with nc.cleanup_on_exit():
            if stages[4] == "s":
                stage_scan(nc, sems, W, K)
        with nc.cleanup_on_exit():
            if stages[5] == "m":
                moe(nc, sems, "mb", K, M)
        stage_store(nc, sems, K, out)


def stage_moe_weights(nc, sems, W, M):
    st = ExitStack()
    with st:
        s_w = Pool_(nc, st, sems, "mw").sem("s_w")
        block = st.enter_context(nc.Block())

        @block.sync
        def _(sp):
            for n in ("wr", "wg", "wu", "wd"):
                sp.dma_start(M[n][tuple(slice(None) for _ in M[n].shape)], W["x" + n]).then_inc(s_w, 16)
            sp.wait_ge(s_w, 64)


def host_arrays(i):
    import numpy as np
    c = np.ascontiguousarray
    up = np.arange(P)
    a = {"x": c(i["L0_attn_x"])}
    for n, name in (("w1", "1"), ("w3", "3")):
        e, s = np.asarray(i["L0_ffn_ew" + name]), np.asarray(i["L0_ffn_sw" + name])
        a[n] = c(np.concatenate([e, s[None]]).transpose(2, 0, 1))
    a["w2"] = c(np.concatenate([np.asarray(i["L0_ffn_ew2"]), np.asarray(i["L0_ffn_sw2"])[None]]).transpose(2, 0, 1))
    a["wr"] = c(np.asarray(i["L0_ffn_router_w"]).T)
    a["br"] = c(np.asarray(i["L0_ffn_routing_bias"]).reshape(1, -1))
    a["ident"] = np.eye(P, dtype=np.float32)
    a["ones"] = np.ones((P, P), np.float32)
    a["triu"] = (up[:, None] < up[None, :]).astype(np.float32)
    a["iota"] = np.tile(np.arange(CAP, dtype=np.float32), (P, 1))
    a["xwr"] = c(np.asarray(i["L1_ffn_gate_w"]).T)
    a["xwg"] = c(np.asarray(i["L1_ffn_w_gate"]).transpose(2, 0, 1))
    a["xwu"] = c(np.asarray(i["L1_ffn_w_up"]).transpose(2, 0, 1))
    a["xwd"] = c(np.asarray(i["L1_ffn_w_down"]).transpose(2, 0, 1))
    a["wqv"] = c(np.stack([np.asarray(i["L1_attn_W" + n]).T for n in "qv"], axis=1))
    a["identity"] = c(np.asarray(i["L1_attn_identity"]).reshape(P, 1))
    a["wp"] = c(np.stack([np.asarray(i["L1_attn_Wp1"]), np.asarray(i["L1_attn_Wp2"])]))
    a["wpt"] = c(a["wp"].transpose(0, 2, 1))
    a["wc"] = c(np.asarray(i["L1_attn_Wc"]).T)
    a["steps"] = np.tile(np.concatenate([np.arange(SLOT_TILES), P * np.arange(TILES)]).astype(np.float32), (P, 1))
    a["rev"] = np.tile(np.arange(E, 0, -1, dtype=np.float32), (P, 1))
    a["wqkv"] = c(np.concatenate([np.asarray(i["L0_attn_W" + n]).T for n in "qkv"], axis=1))
    a["wo"] = c(np.asarray(i["L0_attn_Wo"]).T)
    a["nw"] = c(np.broadcast_to(np.stack([np.asarray(i["L0_attn_qn_w"]), np.asarray(i["L0_attn_kn_w"])]), (P, 2, DH)))
    return a


def kernel(**inputs):
    import numpy as np
    import concourse.bacc as bacc
    from concourse.bass_utils import run_bass_kernel_spmd

    arrays = host_arrays(inputs)
    nc = bacc.Bacc("TRN2", target_bir_lowering=False, num_devices=1)
    W = {n: nc.dram_tensor(n, a.shape, mybir.dt.from_np(a.dtype), kind="ExternalInput").ap() for n, a in arrays.items()}
    out = nc.dram_tensor("out", (B, N, D), F32, kind="ExternalOutput").ap()
    program(nc, W, out)
    r = run_bass_kernel_spmd(nc, [arrays], core_ids=[0])
    return r.results[0]["out"]
```

```python
from contextlib import ExitStack

import concourse.bass as bass
from concourse import mybir

F32 = mybir.dt.float32
BF16 = mybir.dt.bfloat16
I32 = mybir.dt.int32
ALU = mybir.AluOpType
ACT = mybir.ActivationFunctionType
AX = mybir.AxisListType
ds = bass.ds

P = 128
D = 128
B, N = 4, 1024
T = B * N
TILES = T // P
CT = 4
CW = CT * P
CHUNKS = TILES // CT
LN_EPS = 1e-5

I = 352
E = 7
IC = [(0, 128), (128, 128), (256, 96)]
SLOT_TILES = -(-(T // P + E) // 4) * 4
FILL = SLOT_TILES // 4


def bcast(ap, at, n):
    dims = [list(x) for x in ap.ap]
    dims.insert(at, [0, n])
    return bass.AP(ap.tensor, ap.offset, dims)


class Pool_:

    def __init__(self, nc, stack, sems, tag):
        self.nc, self.stack, self.sems, self.tag = nc, stack, sems, tag
        self.seeds = None

    def sb(self, name, shape, dt=F32):
        return self.stack.enter_context(self.nc.sbuf_tensor(f"{self.tag}_{name}", shape, dt))

    def ps(self, name, shape, dt=F32):
        return self.stack.enter_context(self.nc.psum_tensor(f"{self.tag}_{name}", shape, dt))

    def seed(self, sem, n):
        if self.seeds is None:
            self.seeds, self.n = self.sb("seeds", [P, 12]), 0
        self.nc.vector.memset(self.seeds[:, self.n:self.n + 1], 0.0).then_inc(sem, n)
        self.n += 1

    def sem(self, name):
        return self.nc.alloc_semaphore(name=f"{self.tag}_{name}")


class Stats:

    def __init__(self, m, K):
        self.X, self.mv = K["X"], K["mv"]
        self.stats = m.sb("stats", [P, TILES, 6])
        self.s_stats = m.sem("s_stats")
        self.s_mv = m.sem("s_mv")
        self.done = 0

    def dve(self, nc, t, n):
        for i in range(t, t + n):
            nc.vector.bn_stats(self.stats[:, i, :], self.X[:, i, :]).then_inc(self.s_stats, 1)
        self.done += n
        nc.vector.wait_ge(self.s_stats, self.done)
        for i in range(t, t + n):
            nc.vector.bn_aggr(self.mv[:, i, :], self.stats[:, i, :]).then_inc(self.s_mv, 1)


class Norm:

    def __init__(self, m, K, H=None, hT_all=None, stats=False):
        self.X, self.ident, self.H, self.hT_all = K["X"], K["ident"], H, hT_all
        self.mv = K["mv"]
        self.own = Stats(m, K) if stats else None
        self.ps_tr = m.ps("ps_tr", [P, 2, CW])
        self.std = m.sb("std", [P, TILES])
        self.rstd = m.sb("rstd", [P, TILES])
        self.h = m.sb("h", [P, 2, CT, D])
        self.hT = m.sb("hT", [P, 2, CW])
        self.eps = m.sb("eps", [P, 1])
        self.tick = m.sb("tick", [P, 2])
        self.s_std = m.sem("s_std")
        self.s_rstd = m.sem("s_rstd")
        self.s_h = m.sem("s_h")
        self.s_tr = m.sem("s_tr")
        self.s_hT = m.sem("s_hT")
        self.s_eps = m.sem("s_eps")
        if H is not None:
            self.s_H = m.sem("s_H")

    def dve_all(self, nc):
        nc.vector.memset(self.eps[:, :], LN_EPS).then_inc(self.s_eps, 1)
        nc.vector.memset(self.tick[:, 0:1], 0.0).then_inc(self.s_tr, 2)
        if self.H is not None:
            nc.vector.memset(self.tick[:, 1:2], 0.0).then_inc(self.s_H, 2)
        if self.own:
            self.own.dve(nc, 0, TILES)
        nc.vector.wait_ge(self.s_std, 1)
        nc.vector.reciprocal(self.rstd[:, :], self.std[:, :]).then_inc(self.s_rstd, 1)
        nc.vector.wait_ge(self.s_rstd, 1)

    def act_all(self, nc):
        nc.scalar.wait_ge(self.s_eps, 1)
        if self.own:
            nc.scalar.wait_ge(self.own.s_mv, TILES)
        nc.scalar.activation(self.std[:, :], self.mv[:, :, 1], ACT.Sqrt,
                             bias=self.eps[:, 0:1]).then_inc(self.s_std, 1)

    def dve_apply(self, nc, c, u):
        nc.vector.wait_ge(self.s_tr, c + 1)
        if self.H is not None:
            nc.vector.wait_ge(self.s_H, c + 1)
        for j in range(CT):
            t = ds(c * CT + j, 1)
            nc.vector.tensor_scalar(out=self.h[:, u, j, :], in0=self.X[:, t, :],
                                    scalar1=self.mv[:, t, 0], scalar2=self.rstd[:, t],
                                    op0=ALU.subtract, op1=ALU.mult).then_inc(self.s_h, 1)

    def pe_transpose(self, nc, c, u):
        nc.tensor.wait_ge(self.s_h, (c + 1) * CT)
        for j in range(CT):
            last = nc.tensor.transpose(self.ps_tr[:, u, j * P:(j + 1) * P], self.h[:, u, j, :], self.ident[:, :])
        last.then_inc(self.s_tr, 1)

    def act_hT(self, nc, c, u):
        nc.scalar.wait_ge(self.s_tr, c + 3)
        out = nc.scalar.activation(self.hT[:, u, :], self.ps_tr[:, u, :], ACT.Copy)
        if self.hT_all is not None:
            out = nc.scalar.activation(self.hT_all[:, ds(c * CW, CW)], self.ps_tr[:, u, :], ACT.Copy)
        out.then_inc(self.s_hT, 1)
        if self.H is not None:
            nc.scalar.activation(self.H[:, ds(c * CT, CT), :], self.h[:, u], ACT.Copy).then_inc(self.s_H, 1)


LIFT = (3.4445, -4.7750, 2.0315)
POLISH = (1.875, -1.25, 0.375)
LIFTS, POLISHES = 14, 4


class Polar:
    FIRST = 9

    def __init__(self, m, XY):
        self.XY = XY
        self.rowsum = m.sb("rowsum", [P, 2])
        self.norm = m.sb("norm", [P, 2])
        self.A = m.sb("A", [P, 2, P])
        self.TT = m.sb("TT", [P, 2, P])
        self.C = m.sb("C", [P, 2, P])
        self.aI = m.sb("aI", [P, 2, P])
        self.s_w = m.sem("s_w")
        self.s_i = m.sem("s_i")
        self.s_sq = m.sem("s_sq")
        self.s_n = m.sem("s_n")
        self.s_rt = m.sem("s_rt")
        self.s_iv = m.sem("s_iv")
        self.s_a = [m.sem(f"s_a{w}") for w in range(2)]
        self.s_as = [m.sem(f"s_as{w}") for w in range(2)]
        self.s_t = [m.sem(f"s_t{w}") for w in range(2)]
        self.s_c = [m.sem(f"s_c{w}") for w in range(2)]
        self.s_xy = [m.sem(f"s_xy{w}") for w in range(2)]
        self.s_x = [m.sem(f"s_x{w}") for w in range(2)]

    def sp_load(self, nc, W):
        for w in range(2):
            nc.sync.dma_start(self.XY[:, w, 0, :], W["wp"][w]).then_inc(self.s_w, 16)
            nc.sync.dma_start(self.XY[:, w, 1, :], W["wpt"][w]).then_inc(self.s_w, 16)

    def act_start(self, nc, ps_n):
        nc.scalar.wait_ge(self.s_w, 64)
        for w in range(2):
            nc.scalar.activation(self.A[:, w, :], self.XY[:, w, 0, :], ACT.Square,
                                 accum_out=self.rowsum[:, w:w + 1]).then_inc(self.s_sq, 1)
        nc.scalar.wait_ge(self.s_n, 1)
        nc.scalar.activation(self.norm[:, :], ps_n[:, :], ACT.Sqrt).then_inc(self.s_rt, 1)

    def pe_start(self, nc, ones, ps_n):
        nc.tensor.wait_ge(self.s_sq, 2)
        nc.tensor.matmul(ps_n[:, :], ones[:, :], self.rowsum[:, :], start=True, stop=True).then_inc(self.s_n, 1)

    def dve_start(self, nc, ident):
        for k, (a, _, _) in enumerate((LIFT, POLISH)):
            nc.vector.tensor_scalar_mul(self.aI[:, k, :], ident[:, :], a).then_inc(self.s_i, 1)
        nc.vector.wait_ge(self.s_rt, 1)
        nc.vector.reciprocal(self.norm[:, :], self.norm[:, :]).then_inc(self.s_iv, 1)
        nc.vector.wait_ge(self.s_iv, 1)
        for w in range(2):
            nc.vector.tensor_scalar(out=self.XY[:, w], in0=self.XY[:, w], scalar1=self.norm[:, w:w + 1], scalar2=None,
                                    op0=ALU.mult).then_inc(self.s_x[w], 1)
        nc.vector.wait_ge(self.s_i, 2)

    def pe(self, nc, n, piece, ps):
        for w in range(2):
            if piece == 0:
                X = self.XY[:, w, 0, :]
                nc.tensor.wait_ge(self.s_x[w], n + 1)
                nc.tensor.matmul(ps[:, w, 0:P], X, X, start=True, stop=True).then_inc(self.s_a[w], 1)
            if piece == 1:
                nc.tensor.wait_ge(self.s_as[w], n + 1)
                nc.tensor.matmul(ps[:, w, 0:P], self.A[:, w, :], self.A[:, w, :], start=True, stop=True
                                 ).then_inc(self.s_a[w], 1)
            if piece == 2:
                X, Y, C = self.XY[:, w, 0, :], self.XY[:, w, 1, :], self.C[:, w, :]
                nc.tensor.wait_ge(self.s_c[w], n + 1)
                nc.tensor.matmul(ps[:, w, 0:P], Y, C, start=True, stop=True)
                nc.tensor.matmul(ps[:, w, P:2 * P], C, Y, start=True, stop=True).then_inc(self.s_xy[w], 1)

    def act(self, nc, n, piece, ps):
        for w in range(2):
            if piece == 0:
                nc.scalar.wait_ge(self.s_a[w], 2 * n + 1)
                nc.scalar.activation(self.A[:, w, :], ps[:, w, 0:P], ACT.Copy).then_inc(self.s_as[w], 1)
            if piece == 1:
                nc.scalar.wait_ge(self.s_xy[w], n + 1)
                nc.scalar.activation(self.XY[:, w].rearrange("p z d -> p (z d)"), ps[:, w, 0:2 * P],
                                     ACT.Copy).then_inc(self.s_x[w], 1)

    def dve(self, nc, n, piece, k, ps):
        _, b, c = (LIFT, POLISH)[k]
        for w in range(2):
            if piece == 0:
                nc.vector.wait_ge(self.s_as[w], n + 1)
                nc.vector.scalar_tensor_tensor(out=self.TT[:, w, :], in0=self.A[:, w, :], scalar=b,
                                               in1=self.aI[:, k, :], op0=ALU.mult, op1=ALU.add
                                               ).then_inc(self.s_t[w], 1)
            if piece == 1:
                nc.vector.wait_ge(self.s_t[w], n + 1)
                nc.vector.wait_ge(self.s_a[w], 2 * n + 2)
                nc.vector.scalar_tensor_tensor(out=self.C[:, w, :], in0=ps[:, w, 0:P], scalar=c,
                                               in1=self.TT[:, w, :], op0=ALU.mult, op1=ALU.add
                                               ).then_inc(self.s_c[w], 1)


def stage_load(nc, sems, W, consts):
    st = ExitStack()
    with st:
        m = Pool_(nc, st, sems, "ld")
        stats = Stats(m, consts)
        s_x = [m.sem(f"s_x{q}") for q in range(4)]
        s_in = m.sem("s_in")
        block = st.enter_context(nc.Block())
        names = ("ident", "ones", "triu", "iota", "own")

        @block.sync
        def _(sp):
            xin = W["x"].rearrange("b (n p) d -> p (b n) d", p=P)
            for q in range(4):
                sp.dma_start(consts["X"][:, q * 8:q * 8 + 8, :], xin[:, q * 8:q * 8 + 8, :]).then_inc(s_x[q], 16)
            for name in names:
                sp.dma_start(consts[name][:, :], W[name]).then_inc(s_in, 16)

        @block.vector
        def _(dve):
            nc.vector.memset(consts["zero"][:, :], 0.0)
            for q in range(4):
                dve.wait_ge(s_x[q], 16)
                stats.dve(nc, q * 8, 8)
            dve.wait_ge(s_in, 16 * len(names))
            for name in ("ident", "ones", "triu"):
                nc.vector.tensor_copy(consts[name + "b"][:, :], consts[name][:, :])


def stage_ffn_route(nc, sems, tag, W, K, R, F, load, M=None, polar=None):
    X, ident = K["X"], K["ident"]
    H, hT = F["H"], F["hT"]
    st = ExitStack()
    with st:
        m = Pool_(nc, st, sems, tag)
        norm = Norm(m, K, H, hT)
        lg = m.sb("lg", [P, TILES, E])
        pr = m.sb("pr", [P, TILES, E])
        pmax = m.sb("pmax", [P, TILES])
        eq = m.sb("eq", [P, TILES, E])
        smax = m.sb("smax", [P, TILES])
        pc = m.sb("pc", [P, TILES])
        tw = m.sb("tw", [P, TILES])
        mask = m.sb("mask", [P, TILES, E], BF16)
        PAD = TILES // 2
        cum = m.sb("cum", [P, 2, PAD + TILES, E])
        full = m.sb("full", [P, E, TILES])
        tiles_e = m.sb("tiles_e", [P, E])
        PADE = 4
        end = m.sb("end", [P, 2, PADE + E])
        start = m.sb("start", [P, E])
        sl = m.sb("sl", [P, 4, TILES, E])
        slf = m.sb("slf", [P, TILES])
        past = m.sb("past", [P, SLOT_TILES, E - 1])
        tef = m.sb("tef", [P, SLOT_TILES])
        some = m.sb("some", [P, SLOT_TILES // 4])
        fours = m.sb("fours", [P, 2])
        ps_lg = m.ps("ps_lg", [P, 2, CW])
        ps_pos = m.ps("ps_pos", [P, TILES, E])
        ps_cnt = m.ps("ps_cnt", [P, TILES, E])
        if polar:
            ps_n = m.ps("ps_n", [P, 2])
        s_w = m.sem("s_w")
        s_wx = m.sem("s_wx")
        s_lgm = m.sem("s_lgm")
        s_lg = m.sem("s_lg")
        s_cl = m.sem("s_cl")
        s_z = m.sem("s_z")
        s_pr = m.sem("s_pr")
        s_r = m.sem("s_r")
        s_mk = m.sem("s_mk")
        s_c = m.sem("s_c")
        if load:
            zb = m.sb("zb", [P, FILL * D])
        block = st.enter_context(nc.Block())

        @block.sync
        def _(sp):
            if polar:
                polar.sp_load(nc, W)
                sp.wait_ge(polar.s_w, 64)
            if M is not None:
                sp.dma_start(M["wr"][:, :], W["xwr"]).then_inc(M["s_m"], 16)
                for q in range(4):
                    for n in ("wgu", "wd"):
                        sp.dma_start(M[n][:, q * 16:q * 16 + 16, :], W["x" + n][:, q * 16:q * 16 + 16, :]
                                     ).then_inc(M["s_m"], 16)
            if load:
                sp.dma_start(R["wr"][:, :], W["wr"]).then_inc(s_w, 16)
                sp.dma_start(R["br"][:, :], W["br"]).then_inc(s_w, 16)
                sp.dma_start(R["rev"][:, :], W["rev"]).then_inc(s_w, 16)
                sp.dma_start(R["steps"][:, :], W["steps"]).then_inc(s_w, 16)
                sp.dma_start(R["w1"][:, :, :], W["w1"]).then_inc(s_wx, 16)
                sp.dma_start(R["w3"][:, :, :], W["w3"]).then_inc(s_wx, 16)
                for j, (i0, n) in enumerate(IC):
                    sp.dma_start(R["w2"][0:n, j, :, :], W["w2"][i0:i0 + n, :, :]).then_inc(s_wx, 16)
                sp.wait_ge(s_z, 4)
                for slots in (F["Hs"], F["Ys"]):
                    fill = slots.rearrange("(q p t) d -> q p (t d)", p=P, t=FILL)
                    for q in range(SLOT_TILES // FILL):
                        sp.dma_start(fill[q], zb[:, :]).then_inc(s_wx, 16)
                sp.wait_ge(s_wx, 16 * (5 + 2 * SLOT_TILES // FILL))

        @block.vector
        def _(dve):
            m.seed(s_lg, 2)
            nc.vector.memset(cum[:, :, 0:PAD, :], 0.0).then_inc(s_z, 1)
            nc.vector.memset(end[:, :, 0:PADE], 0.0).then_inc(s_z, 1)
            if load:
                nc.vector.memset(zb[:, :], 0.0).then_inc(s_z, 1)
                nc.vector.memset(R["w2"][IC[-1][1]:P, len(IC) - 1, :, :], 0.0).then_inc(s_z, 1)
                dve.wait_ge(s_w, 64)
            norm.dve_all(nc)
            if polar:
                polar.dve_start(nc, ident)
            norm.dve_apply(nc, 0, 0)
            norm.dve_apply(nc, 1, 1)

            def chunk(k, u, more):
                c = k * 2 + u
                if more:
                    norm.dve_apply(nc, c + 2, u)
                dve.wait_ge(s_lgm, c + 1)
                nc.vector.tensor_tensor(out=lg[:, ds(c * CT, CT), :],
                                        in0=ps_lg[:, u, 0:CT * E].rearrange("p (t e) -> p t e", e=E),
                                        in1=bcast(R["br"][:, :], 1, CT), op=ALU.add).then_inc(s_lg, 1)

            with dve.Fori(0, CHUNKS // 2 - 1) as k:
                for u in range(2):
                    chunk(k, u, True)
            chunk(CHUNKS // 2 - 1, 0, False)
            chunk(CHUNKS // 2 - 1, 1, False)

            done = 0

            def step(ins):
                nonlocal done
                done += 1
                ins.then_inc(s_r, 1)
                dve.wait_ge(s_r, done)
            dve.wait_ge(s_lg, CHUNKS + 2)
            nc.vector.tensor_scalar(out=lg[:, :, :], in0=lg[:, :, :], scalar1=-50.0, scalar2=50.0,
                                    op0=ALU.max, op1=ALU.min).then_inc(s_cl, 1)
            dve.wait_ge(s_pr, 1)
            step(nc.vector.tensor_reduce(out=pmax[:, :], in_=pr[:, :, :], axis=AX.X, op=ALU.max))
            step(nc.vector.tensor_tensor(out=eq[:, :, :], in0=pr[:, :, :], in1=bcast(pmax[:, :], 2, E),
                                         op=ALU.is_equal))
            step(nc.vector.tensor_tensor(out=eq[:, :, :], in0=eq[:, :, :], in1=bcast(R["rev"][:, :], 1, TILES),
                                         op=ALU.mult))
            step(nc.vector.tensor_reduce(out=smax[:, :], in_=eq[:, :, :], axis=AX.X, op=ALU.max))
            nc.vector.tensor_tensor(out=mask[:, :, :], in0=eq[:, :, :], in1=bcast(smax[:, :], 2, E),
                                    op=ALU.is_equal).then_inc(s_mk, 1)
            step(nc.vector.tensor_scalar(out=pc[:, :], in0=pmax[:, :], scalar1=1e-8, scalar2=1.0 - 1e-8,
                                         op0=ALU.max, op1=ALU.min))
            step(nc.vector.tensor_scalar(out=tw[:, :], in0=pc[:, :], scalar1=0.5, scalar2=1e-8,
                                         op0=ALU.add, op1=ALU.add))
            step(nc.vector.tensor_scalar(out=tw[:, :], in0=tw[:, :], scalar1=0.5, scalar2=2.0,
                                         op0=ALU.max, op1=ALU.min))
            step(nc.vector.reciprocal(tw[:, :], tw[:, :]))
            nc.vector.tensor_scalar_mul(F["w_sh"][:, :], tw[:, :], 0.25)
            nc.vector.scalar_tensor_tensor(out=F["w_ex"][:, :], in0=pc[:, :], scalar=0.5, in1=tw[:, :],
                                           op0=ALU.mult, op1=ALU.mult)
            dve.wait_ge(s_c, 1)
            dve.wait_ge(s_z, 2)
            step(nc.vector.tensor_copy(cum[:, 0, PAD:, :], ps_cnt[:, :, :]))
            v, s = 0, 1
            while s < TILES:
                step(nc.vector.tensor_tensor(out=cum[:, 1 - v, PAD:, :], in0=cum[:, v, PAD:, :],
                                             in1=cum[:, v, PAD - s:PAD + TILES - s, :], op=ALU.add))
                v, s = 1 - v, 2 * s
            total = cum[:, v, PAD + TILES - 1, :]
            step(nc.vector.tensor_tensor(out=full[:, :, :], in0=bcast(total, 2, TILES),
                                         in1=bcast(R["steps"][:, SLOT_TILES:], 1, E), op=ALU.is_gt))
            step(nc.vector.tensor_reduce(out=tiles_e[:, :], in_=full[:, :, :], axis=AX.X, op=ALU.add))
            step(nc.vector.tensor_copy(end[:, 0, PADE:], tiles_e[:, :]))
            w = 0
            for s in (1, 2, 4):
                step(nc.vector.tensor_tensor(out=end[:, 1 - w, PADE:], in0=end[:, w, PADE:],
                                             in1=end[:, w, PADE - s:PADE + E - s], op=ALU.add))
                w = 1 - w
            ends = end[:, w, PADE:]
            step(nc.vector.tensor_tensor(out=start[:, :], in0=ends, in1=tiles_e[:, :], op=ALU.subtract))
            step(nc.vector.tensor_tensor(out=sl[:, 0], in0=ps_pos[:, :, :], in1=cum[:, v, PAD:, :], op=ALU.add))
            step(nc.vector.tensor_tensor(out=sl[:, 1], in0=sl[:, 0], in1=ps_cnt[:, :, :], op=ALU.subtract))
            step(nc.vector.scalar_tensor_tensor(out=sl[:, 2], in0=bcast(start[:, :], 1, TILES), scalar=float(P),
                                                in1=sl[:, 1], op0=ALU.mult, op1=ALU.add))
            step(nc.vector.tensor_tensor(out=sl[:, 3], in0=sl[:, 2], in1=mask[:, :, :], op=ALU.mult))
            step(nc.vector.tensor_reduce(out=slf[:, :], in_=sl[:, 3], axis=AX.X, op=ALU.add))
            step(nc.vector.tensor_copy(F["slot"][:, :], slf[:, :]))
            step(nc.vector.tensor_tensor(out=past[:, :, :], in0=bcast(ends[:, 0:E - 1], 1, SLOT_TILES),
                                         in1=bcast(R["steps"][:, 0:SLOT_TILES], 2, E - 1), op=ALU.is_le))
            step(nc.vector.tensor_reduce(out=tef[:, :], in_=past[:, :, :], axis=AX.X, op=ALU.add))
            step(nc.vector.tensor_copy(F["expert"][:, :], tef[:, :]))
            step(nc.vector.tensor_scalar_mul(fours[:, 0:1], ends[:, E - 1:E], P / 4))
            step(nc.vector.tensor_tensor(out=some[:, :], in0=bcast(fours[:, 0:1], 1, SLOT_TILES // 4)[:, :, 0],
                                         in1=R["steps"][:, SLOT_TILES:SLOT_TILES + SLOT_TILES // 4], op=ALU.is_gt))
            step(nc.vector.tensor_reduce(out=fours[:, 1:2], in_=some[:, :], axis=AX.X, op=ALU.add))
            nc.vector.tensor_scalar(out=F["last"][:, :], in0=fours[:, 1:2], scalar1=-1.0, scalar2=None, op0=ALU.add)

        @block.scalar
        def _(act):
            if polar:
                polar.act_start(nc, ps_n)
            norm.act_all(nc)
            norm.act_hT(nc, 0, 0)
            with act.Fori(0, CHUNKS // 2 - 1) as k:
                for u in range(2):
                    norm.act_hT(nc, k * 2 + u + 1, 1 - u)
            norm.act_hT(nc, CHUNKS - 1, 1)
            act.wait_ge(s_cl, 1)
            nc.scalar.activation(pr[:, :, :], lg[:, :, :], ACT.Sigmoid).then_inc(s_pr, 1)

        @block.tensor
        def _(pe):
            if load:
                pe.wait_ge(s_w, 64)
            if polar:
                polar.pe_start(nc, K["ones"], ps_n)
            norm.pe_transpose(nc, 0, 0)

            def chunk(c, u, more):
                if more:
                    norm.pe_transpose(nc, c + 1, 1 - u)
                pe.wait_ge(norm.s_hT, c + 1)
                pe.wait_ge(s_lg, c + 1)
                for s in range(CT):
                    last = nc.tensor.matmul(ps_lg[:, u, s * E:(s + 1) * E], norm.hT[:, u, s * P:(s + 1) * P],
                                            R["wr"][:, :], start=True, stop=True)
                last.then_inc(s_lgm, 1)

            with pe.Fori(0, CHUNKS // 2 - 1) as k:
                for u in range(2):
                    chunk(k * 2 + u, u, True)
            chunk(CHUNKS - 2, 0, True)
            chunk(CHUNKS - 1, 1, False)
            pe.wait_ge(s_mk, 1)
            nc.tensor.matmul(ps_pos[:, :, :], K["triub"][:, :], mask[:, :, :], start=True, stop=True)
            nc.tensor.matmul(ps_cnt[:, :, :], K["onesb"][:, :], mask[:, :, :], start=True, stop=True).then_inc(s_c, 1)


GATHERED = [[0], [1, 2], [3, 4], [5], [6, 7]]


def stage_ffn_shared(nc, sems, tag, W, K, R, F, c0, chunks, scatter, M=None, polar=None):
    X, H, hT = K["X"], F["H"], F["hT"]
    w1, w3, w2 = R["w1"], R["w3"], R["w2"]
    st = ExitStack()
    with st:
        m = Pool_(nc, st, sems, tag)
        silu = m.sb("silu", [P, 2, CW])
        gu = m.sb("gu", [P, 2, len(IC), CW])
        yw = m.sb("yw", [P, 2, CT, D])
        ps_a = m.ps("ps_a", [P, 2, CW])
        ps_b = m.ps("ps_b", [P, 2, CW])
        ps_y = m.ps("ps_y", [P, 2, CT, D])
        ps_p = m.ps("ps_p", [P, 2, CW]) if polar else None
        n0 = 0 if scatter else Polar.FIRST
        s_ab = m.sem("s_ab")
        s_silu = m.sem("s_silu")
        s_gu = m.sem("s_gu")
        s_y = m.sem("s_y")
        s_yw = m.sem("s_yw")
        s_x = m.sem("s_x")
        s_sc = m.sem("s_sc")
        s_ga = [m.sem(f"s_ga{c}") for c in range(0 if scatter else CHUNKS)]
        s_gw = m.sem("s_gw")
        block = st.enter_context(nc.Block())
        NJ = len(IC)

        @block.sync
        def _(sp):
            if M is not None and scatter:
                sp.wait_ge(M["s_m"], 16 * 9)

        @block.gpsimd
        def _(pool):
            for t in range(TILES):
                at = bass.IndirectOffsetOnAxis(ap=F["slot"][:, t:t + 1], axis=0)
                if scatter:
                    nc.gpsimd.indirect_dma_start(out=F["Hs"][:, :], out_offset=at, in_=H[:, t, :],
                                                 in_offset=None).then_inc(s_sc, 16)
                else:
                    nc.gpsimd.indirect_dma_start(out=H[:, t, :], out_offset=None, in_=F["Ys"][:, :],
                                                 in_offset=at).then_inc(s_ga[t // CT], 16)
            if scatter:
                pool.wait_ge(s_sc, TILES * 16)

        @block.scalar
        def _(act):
            def weight(c):
                act.wait_ge(s_ga[c], 16 * CT)
                for t in range(c * CT, (c + 1) * CT):
                    nc.scalar.activation(H[:, t, :], H[:, t, :], ACT.Copy, scale=F["w_ex"][:, t:t + 1]
                                         ).then_inc(s_gw, 1)

            for c in range(chunks):
                step = 2 * c + n0
                for j in range(NJ):
                    g, n = (c * NJ + j) % 2, IC[j][1]
                    act.wait_ge(s_ab, c * NJ + j + 1)
                    act.wait_ge(s_gu, c * NJ + j + 1)
                    nc.scalar.activation(silu[0:n, g, :], ps_a[0:n, g, :], ACT.Silu).then_inc(s_silu, 1)
                    if polar and j == 0:
                        polar.act(nc, step, 0, ps_p)
                if polar:
                    polar.act(nc, step, 1, ps_p)
                    polar.act(nc, step + 1, 0, ps_p)
                    polar.act(nc, step + 1, 1, ps_p)
                if not scatter:
                    for g in GATHERED[c]:
                        weight(g)
            if polar:
                for piece in range(2):
                    polar.act(nc, n0 + 2 * chunks, piece, ps_p)
            if not scatter:
                for g in GATHERED[chunks]:
                    weight(g)

        @block.vector
        def _(dve):
            m.seed(s_gu, 2)
            m.seed(s_y, 2)
            m.seed(s_yw, 2)

            def gate(c, u, j):
                g, n = u * NJ + j, IC[j][1]
                dve.wait_ge(s_silu, c * NJ + j + 1)
                if j == 0:
                    dve.wait_ge(s_y, c + 1)
                nc.vector.tensor_tensor(out=gu[0:n, u, j, :], in0=ps_b[0:n, g % 2, :],
                                        in1=silu[0:n, g % 2, :], op=ALU.mult).then_inc(s_gu, 1)

            def add(c, u):
                dve.wait_ge(s_y, c + 3)
                nc.vector.tensor_tensor(out=yw[:, u], in0=ps_y[:, u],
                                        in1=bcast(F["w_sh"][:, ds(c0 + c * CT, CT)], 2, D),
                                        op=ALU.mult).then_inc(s_yw, 1)
                dve.wait_ge(s_yw, c + 3)
                xc = X[:, ds(c0 + c * CT, CT), :]
                nc.vector.tensor_tensor(out=xc, in0=yw[:, u], in1=xc, op=ALU.add).then_inc(s_x, 1)

            def kind(n):
                return int(n >= LIFTS)

            def chunk(c, u, before):
                n = 2 * c + n0
                for j in range(NJ):
                    gate(c, u, j)
                    if polar and j < 2:
                        polar.dve(nc, n, j, kind(n), ps_p)
                if polar:
                    for piece in range(2):
                        polar.dve(nc, n + 1, piece, kind(n + 1), ps_p)
                if before:
                    add(c - 1, 1 - u)
            stats = None if scatter else Stats(m, K)

            def gathered(c, before):
                dve.wait_ge(s_gw, (c + 1) * CT)
                if before:
                    dve.wait_ge(s_x, before)
                xc = X[:, c * CT:(c + 1) * CT, :]
                nc.vector.tensor_tensor(out=xc, in0=H[:, c * CT:(c + 1) * CT, :], in1=xc, op=ALU.add).then_inc(s_x, 1)
                dve.wait_ge(s_x, before + 1)
                stats.dve(nc, c * CT, CT)

            for c in range(chunks):
                chunk(c, c % 2, c > 0)
                if not scatter:
                    for g in GATHERED[c]:
                        gathered(g, c + g)
            if polar:
                for piece in range(2):
                    polar.dve(nc, n0 + 2 * chunks, piece, kind(n0 + 2 * chunks), ps_p)
            add(chunks - 1, 1)
            if not scatter:
                for g in GATHERED[chunks]:
                    gathered(g, chunks + g)

        @block.tensor
        def _(pe):
            def up(c, u):
                for j, (i0, n) in enumerate(IC):
                    g = u * NJ + j
                    pe.wait_ge(s_gu, c * NJ + j + 1)
                    rhs = hT[:, ds(c0 * P + c * CW, CW)]
                    nc.tensor.matmul(ps_a[0:n, g % 2, :], w1[:, E, i0:i0 + n], rhs, start=True, stop=True)
                    nc.tensor.matmul(ps_b[0:n, g % 2, :], w3[:, E, i0:i0 + n], rhs, start=True,
                                     stop=True).then_inc(s_ab, 1)
                    if polar:
                        polar.pe(nc, 2 * c + n0, j, ps_p)
                if polar:
                    polar.pe(nc, 2 * c + n0 + 1, 0, ps_p)

            def down(c, u, step):
                pe.wait_ge(s_gu, c * NJ + NJ + 2)
                pe.wait_ge(s_yw, c + 1)
                for s in range(CT):
                    for j, (_, n) in enumerate(IC):
                        last = nc.tensor.matmul(ps_y[:, u, s, :], gu[0:n, u, j, s * P:(s + 1) * P],
                                                w2[0:n, j, E, :], start=(j == 0), stop=(j == NJ - 1))
                    if polar and s in (1, 3):
                        if s == 3:
                            last.then_inc(s_y, 1)
                        polar.pe(nc, step, 1 + s // 2, ps_p)
                if not polar:
                    last.then_inc(s_y, 1)
            up(0, 0)
            if polar:
                polar.pe(nc, n0 + 1, 1, ps_p)
                polar.pe(nc, n0 + 1, 2, ps_p)
            with pe.Fori(0, chunks // 2 - 1) as k:
                up(k * 2 + 1, 1)
                down(k * 2, 0, k * 4 + n0 + 3)
                up(k * 2 + 2, 0)
                down(k * 2 + 1, 1, k * 4 + n0 + 5)
            up(chunks - 1, 1)
            down(chunks - 2, 0, 2 * chunks + n0 - 1)
            if polar:
                polar.pe(nc, 2 * chunks + n0, 0, ps_p)
            down(chunks - 1, 1, 2 * chunks + n0)


def stage_ffn_switched(nc, sems, tag, K, R, F):
    w1, w3, w2 = R["w1"], R["w3"], R["w2"]
    Hs = F["Hs"].rearrange("(t p) d -> p t d", p=P)
    Ys = F["Ys"].rearrange("(t p) d -> p t d", p=P)
    NJ = len(IC)
    st = ExitStack()
    with st:
        m = Pool_(nc, st, sems, tag)
        hs = m.sb("hs", [P, 2, 2, D])
        hsT = m.sb("hsT", [P, 2, P])
        sg = m.sb("sg", [P, 2, I])
        gu = m.sb("gu", [P, 2, NJ * P])
        guT = m.sb("guT", [P, 2, NJ * P])
        ys = m.sb("ys", [P, 2, 2, D])
        ps_a = m.ps("ps_a", [P, 2, CW])
        ps_b = m.ps("ps_b", [P, 2, CW])
        ps_g = m.ps("ps_g", [P, 2, CW])
        ps_t = m.ps("ps_t", [P, P])
        ps_y = m.ps("ps_y", [P, P])
        s_ld = [m.sem("s_ld0"), m.sem("s_ld1")]
        s_st = m.sem("s_st")
        s_yf = m.sem("s_yf")
        tick = m.sb("tick", [P, 2])
        s_z = m.sem("s_z")
        s_t = m.sem("s_t")
        s_tc = m.sem("s_tc")
        s_ab = m.sem("s_ab")
        s_s = m.sem("s_s")
        s_gu = m.sem("s_gu")
        s_g = m.sem("s_g")
        s_gc = m.sem("s_gc")
        s_y = m.sem("s_y")
        s_yc = m.sem("s_yc")
        block = st.enter_context(nc.Block())

        def last_four(engine):
            return engine.value_load(F["last"][0:1, 0:1], min_val=T // P // 4 - 1, max_val=SLOT_TILES // 4 - 1)

        @block.sync
        def _(sp):
            def load(k, v):
                sp.wait_ge(s_t, k * 4 + 2 * v + 2)
                sp.dma_start(hs[:, v], Hs[:, ds(k * 4 + 2 * v, 2), :]).then_inc(s_ld[v], 16)

            load(0, 0)
            load(0, 1)
            end = last_four(sp)
            with sp.Fori(1, end + 1) as k:
                for v in range(2):
                    load(k, v)

        @block.gpsimd
        def _(pool):
            end = last_four(pool)
            with pool.Fori(0, end + 1) as k:
                for v in range(2):
                    pool.wait_ge(s_yc, k * 4 + 2 * v + 4)
                    pool.dma_start(Ys[:, ds(k * 4 + 2 * v, 2), :], ys[:, v]).then_inc(s_st, 16)
                    pool.wait_ge(s_yf, k * 2 + v + 2)
                    pool.wait_ge(s_st, k * 32 + v * 16 + 16)
                    nc.gpsimd.tensor_tensor(out=tick[:, v:v + 1], in0=K["zero"][:, :], in1=K["zero"][:, :], op=ALU.add
                                            ).then_inc(s_yf, 1)

        @block.scalar
        def _(act):
            def hT(t, w):
                act.wait_ge(s_t, t + 5)
                if not isinstance(t, int) or t >= 2:
                    act.wait_ge(s_ab, t - 1)
                nc.scalar.activation(hsT[:, w, :], ps_t[:, :], ACT.Copy).then_inc(s_tc, 1)

            def tile(t, w, more):
                if more:
                    hT(t + 1, 1 - w)
                act.wait_ge(s_ab, t + 1)
                act.wait_ge(s_gu, t + 1)
                nc.scalar.activation(sg[:, w, :], ps_a[:, w, 0:I], ACT.Silu).then_inc(s_s, 1)
            hT(0, 0)
            tile(0, 0, True)
            tile(1, 1, True)
            tile(2, 0, True)
            tile(3, 1, True)
            end = last_four(act)
            with act.Fori(1, end) as k:
                for x in range(4):
                    tile(k * 4 + x, x % 2, True)
            for x in range(4):
                tile(end * 4 + x, x % 2, x < 3)

        @block.vector
        def _(dve):
            nc.vector.memset(gu[:, :, I:], 0.0).then_inc(s_z, 1)
            m.seed(s_t, 4)
            for s in (s_tc, s_gu, s_g, s_gc, s_y, s_yc, s_yf):
                m.seed(s, 2)
            dve.wait_ge(s_z, 1)

            def gate(t, w):
                dve.wait_ge(s_s, t + 1)
                dve.wait_ge(s_g, t + 1)
                nc.vector.tensor_tensor(out=gu[:, w, 0:I], in0=ps_b[:, w, 0:I], in1=sg[:, w, :],
                                        op=ALU.mult).then_inc(s_gu, 1)

            def gT(t, w):
                dve.wait_ge(s_g, t + 3)
                dve.wait_ge(s_y, t + 1)
                nc.vector.tensor_copy(guT[:, w, :], ps_g[:, w, 0:NJ * P]).then_inc(s_gc, 1)

            def y(t, k, v, w):
                if w == 0:
                    dve.wait_ge(s_yf, k * 2 + v + 1)
                dve.wait_ge(s_y, t + 3)
                nc.vector.tensor_copy(ys[:, v, w, :], ps_y[:, :]).then_inc(s_yc, 1)

            def four(k, first):
                for x in range(4):
                    t = k * 4 + x
                    gate(t, x % 2)
                    if x >= 2 or not first:
                        y(t - 2, k - int(x < 2), (x + 2) % 4 // 2, x % 2)
                    if x >= 1 or not first:
                        gT(t - 1, 1 - x % 2)
            four(0, True)
            end = last_four(dve)
            with dve.Fori(1, end + 1) as k:
                four(k, False)
            y(end * 4 + 2, end, 1, 0)
            gT(end * 4 + 3, 1)
            y(end * 4 + 3, end, 1, 1)

        @block.tensor
        def _(pe):
            def tr(t, k, v, w):
                if w == 0:
                    pe.wait_ge(s_ld[v], k * 16 + 16)
                pe.wait_ge(s_tc, t + 2)
                nc.tensor.transpose(ps_t[:, :], hs[:, v, w, :], K["ident"][:, :]).then_inc(s_t, 1)

            def up(t, w, e):
                pe.wait_ge(s_tc, t + 3)
                pe.wait_ge(s_gu, t + 1)
                for ps, wx in ((ps_a, w1), (ps_b, w3)):
                    last = nc.tensor.matmul(ps[:, w, 0:I], hsT[:, w, :], wx[:, ds(e, 1), :].rearrange("p o i -> p (o i)"),
                                            start=True, stop=True)
                last.then_inc(s_ab, 1)

            def gates(t, w):
                pe.wait_ge(s_gu, t + 3)
                pe.wait_ge(s_gc, t + 1)
                for j in range(NJ):
                    last = nc.tensor.transpose(ps_g[:, w, j * P:(j + 1) * P], gu[:, w, j * P:(j + 1) * P],
                                               K["ident"][:, :])
                last.then_inc(s_g, 1)

            def down(t, w):
                e = pe.value_load(F["expert"][0:1, ds(t, 1)], min_val=0, max_val=E - 1)
                pe.wait_ge(s_gc, t + 3)
                pe.wait_ge(s_yc, t + 2)
                for j in range(NJ):
                    last = nc.tensor.matmul(ps_y[:, :], guT[:, w, j * P:(j + 1) * P],
                                            w2[:, j, ds(e, 1), :].rearrange("p o d -> p (o d)"),
                                            start=(j == 0), stop=(j == NJ - 1))
                last.then_inc(s_y, 1)

            def four(k, first, more):
                for x in range(4):
                    t = k * 4 + x
                    if more or x < 3:
                        tr(t + 1, k + int(x == 3), (x + 1) % 4 // 2, 1 - x % 2)
                    e = pe.value_load(F["expert"][0:1, ds(t, 1)], min_val=0, max_val=E - 1)
                    up(t, x % 2, e)
                    if x >= 2 or not first:
                        down(t - 2, x % 2)
                    if x >= 1 or not first:
                        gates(t - 1, 1 - x % 2)
            tr(0, 0, 0, 0)
            four(0, True, True)
            end = last_four(pe)
            with pe.Fori(1, end) as k:
                four(k, False, True)
            four(end, False, False)
            down(end * 4 + 2, 0)
            gates(end * 4 + 3, 1)
            down(end * 4 + 3, 1)


def ffn(nc, sems, tag, W, K, R, load, M=None, XY=None):
    st = ExitStack()
    with st:
        m = Pool_(nc, st, sems, tag)
        F = {"H": m.sb("H", [P, TILES, D]), "hT": m.sb("hT", [P, T]), "w_sh": m.sb("w_sh", [P, TILES]),
             "w_ex": m.sb("w_ex", [P, TILES]), "slot": m.sb("slot", [P, TILES], I32),
             "expert": m.sb("expert", [P, SLOT_TILES], I32), "last": m.sb("last", [P, 1], I32),
             "Hs": K["Hs"], "Ys": K["Ys"]}
        polar = Polar(m, XY) if XY is not None else None
        if M is not None:
            M["s_m"] = m.sem("s_m")
        stage_ffn_route(nc, sems, tag + "r", W, K, R, F, load, M, polar)
        stage_ffn_shared(nc, sems, tag + "s", W, K, R, F, 0, CHUNKS // 2, True, M, polar)
        stage_ffn_switched(nc, sems, tag + "x", K, R, F)
        stage_ffn_shared(nc, sems, tag + "g", W, K, R, F, TILES // 2, CHUNKS // 2, False, None, polar)


H, DH = 16, 8
PAIRS = B * H // 2
PT_ = N // P
SCALE = DH ** -0.5
RMS_EPS = 1.1920928955078125e-07
SLOTS = 6
KR = SLOTS * DH
KM = KR + 3
HR = 64


def stage_qkv(nc, sems, W, K, A):
    X, ident = K["X"], K["ident"]
    qkv = [A["q"], A["k"], A["v"]]
    st = ExitStack()
    with st:
        m = Pool_(nc, st, sems, "qkv")
        norm = Norm(m, K)
        w = m.sb("w", [P, 3 * D])
        nw = m.sb("nw", [P, 2, DH])
        sq = m.sb("sq", [P, 2, 2, 2 * D])
        ms = m.sb("ms", [P, 2, 2, 2 * H])
        rr = m.sb("rr", [P, 2, 2, 2 * H])
        qk = m.sb("qk", [P, 2, 2, 2 * D])
        reps = m.sb("reps", [P, 1])
        ps_q = m.ps("ps_q", [P, 2, 2, CW])
        s_w = m.sem("s_w")
        s_c = m.sem("s_c")
        s_p = m.sem("s_p")
        s_sq = m.sem("s_sq")
        s_ms = m.sem("s_ms")
        s_rt = m.sem("s_rt")
        s_rc = m.sem("s_rc")
        s_n = m.sem("s_n")
        s_v = m.sem("s_v")
        s_g = m.sem("s_g")
        block = st.enter_context(nc.Block())

        @block.sync
        def _(sp):
            sp.dma_start(w[:, :], W["wqkv"]).then_inc(s_w, 16)
            sp.dma_start(nw[:, :, :], W["nw"]).then_inc(s_w, 16)
            sp.wait_ge(s_w, 32)

        @block.vector
        def _(dve):
            nc.vector.memset(reps[:, :], RMS_EPS).then_inc(s_c, 1)
            m.seed(s_sq, 2)
            m.seed(s_ms, 2)
            m.seed(s_n, 2)
            m.seed(s_v, 4)
            m.seed(s_g, 8)
            norm.dve_all(nc)
            norm.dve_apply(nc, 0, 0)
            norm.dve_apply(nc, 1, 1)

            def sums(g, v):
                dve.wait_ge(s_sq, g + 3)
                nc.vector.tensor_reduce(out=ms[:, v], in_=sq[:, v].rearrange("p t (h d) -> p t h d", d=DH),
                                        axis=AX.X, op=ALU.add).then_inc(s_ms, 1)

            def scale(g, v):
                dve.wait_ge(s_rt, g + 1)
                nc.vector.reciprocal(rr[:, v], ms[:, v]).then_inc(s_rc, 1)
                dve.wait_ge(s_rc, g + 1)
                dve.wait_ge(s_g, 4 * g + 4)
                nc.vector.tensor_tensor(out=qk[:, v].rearrange("p t (h d) -> p t h d", d=DH),
                                        in0=ps_q[:, v, :, 0:2 * D].rearrange("p t (h d) -> p t h d", d=DH),
                                        in1=bcast(rr[:, v], 3, DH), op=ALU.mult).then_inc(s_n, 1)

            def chunk(c, u, more):
                for v in range(2):
                    sums(c * 2 + v, v)
                    if more and v == 0:
                        norm.dve_apply(nc, c + 2, u)
                    scale(c * 2 + v, v)

            with dve.Fori(0, CHUNKS // 2 - 1) as k:
                for u in range(2):
                    chunk(k * 2 + u, u, True)
            chunk(CHUNKS - 2, 0, False)
            chunk(CHUNKS - 1, 1, False)

        @block.scalar
        def _(act):
            norm.act_all(nc)
            norm.act_hT(nc, 0, 0)
            act.wait_ge(s_c, 1)

            def chunk(c, u, more):
                for v in range(2):
                    g = c * 2 + v
                    act.wait_ge(s_p, g + 1)
                    act.wait_ge(s_ms, g + 1)
                    nc.scalar.activation(sq[:, v], ps_q[:, v, :, 0:2 * D], ACT.Square).then_inc(s_sq, 1)
                    for j in range(2):
                        act_v(c, u, v, j)
                    if more and v == 0:
                        norm.act_hT(nc, c + 1, 1 - u)
                    act.wait_ge(s_ms, g + 3)
                    nc.scalar.activation(ms[:, v], ms[:, v], ACT.Sqrt, bias=reps[:, 0:1],
                                         scale=1.0 / DH).then_inc(s_rt, 1)

            def act_v(c, u, v, j):
                b = c // 2 if isinstance(c, int) else batch[0]
                dst = A["v"][:, ds(b * 8, 8), 4 * u + 2 * v + j, :]
                nc.scalar.activation(dst, ps_q[:, v, j, 2 * D:3 * D].rearrange("p (h d) -> p h d", d=16),
                                     ACT.Copy).then_inc(s_v, 1)

            batch = [None]
            with act.Fori(0, CHUNKS // 2 - 1) as k:
                batch[0] = k
                for u in range(2):
                    chunk(k * 2 + u, u, True)
            chunk(CHUNKS - 2, 0, True)
            chunk(CHUNKS - 1, 1, False)

        @block.gpsimd
        def _(pool):
            pool.wait_ge(s_w, 32)

            def chunk(c, u, b):
                for v in range(2):
                    pool.wait_ge(s_n, c * 2 + v + 3)
                    for j in range(2):
                        for r, x in enumerate(("q", "k")):
                            dst = A[x][:, ds(b * 8, 8), 4 * u + 2 * v + j, :].rearrange("p h (a d) -> p h a d", d=DH)
                            src = qk[:, v, j, r * D:(r + 1) * D].rearrange("p (h a d) -> p h a d", a=2, d=DH)
                            nc.gpsimd.tensor_tensor(out=dst, in0=src, in1=bcast(bcast(nw[:, r, :], 1, 2), 1, 8),
                                                    op=ALU.mult).then_inc(s_g, 1)

            with pool.Fori(0, CHUNKS // 2) as k:
                for u in range(2):
                    chunk(k * 2 + u, u, k)

        @block.tensor
        def _(pe):
            pe.wait_ge(s_w, 32)
            norm.pe_transpose(nc, 0, 0)

            def chunk(c, u, more):
                if more:
                    norm.pe_transpose(nc, c + 1, 1 - u)
                pe.wait_ge(norm.s_hT, c + 1)
                for v in range(2):
                    pe.wait_ge(s_n, c * 2 + v + 1)
                    pe.wait_ge(s_v, (c * 2 + v) * 2 + 2)
                    for j in range(2):
                        last = nc.tensor.matmul(ps_q[:, v, j, 0:3 * D],
                                                norm.hT[:, u, (2 * v + j) * P:(2 * v + j + 1) * P], w[:, :],
                                                start=True, stop=True)
                    last.then_inc(s_p, 1)

            with pe.Fori(0, CHUNKS // 2 - 1) as k:
                for u in range(2):
                    chunk(k * 2 + u, u, True)
            chunk(CHUNKS - 2, 0, True)
            chunk(CHUNKS - 1, 1, False)


def stage_attention(nc, sems, K, A):
    ident, identb, O = K["ident"], K["identb"], A["o"]
    G8 = PT_
    st = ExitStack()
    with st:
        m = Pool_(nc, st, sems, "at")
        raw = m.sb("raw", [P, 2, 3, G8 * 16])
        qx = m.sb("qx", [P, 2, G8, 2, HR], BF16)
        kx = m.sb("kx", [P, 2, G8, 2, HR], BF16)
        vx = m.sb("vx", [P, 2, G8, 2, 32])
        r1 = m.sb("r1", [P, 4, G8 * 2, DH])
        mr = m.sb("mr", [P, 2, G8 * 2])
        qT1 = m.sb("qT1", [P, 2, N], BF16)
        qm1 = m.sb("qm1", [P, 2, 2, N], BF16)
        qm2 = m.sb("qm2", [P, 2, 2, N], BF16)
        mp = m.sb("mp", [P, 2, P], BF16)
        mT = m.sb("mT", [HR, 2, P], BF16)
        kT1 = m.sb("kT1", [P, 2, N], BF16)
        kT2 = m.sb("kT2", [P, 2, N], BF16)
        negm = m.sb("negm", [P, 2, G8, 2])
        pT = m.sb("pT", [P, 8, CW])
        oT = m.sb("oT", [P, 2, CW])
        ro = m.sb("ro", [P, 2, 4, 4])
        ps_s = m.ps("ps_s", [P, 2, N])
        ps_p = m.ps("ps_p", [P, 2, CW])
        ps_o = m.ps("ps_o", [P, CW])
        ps_t = m.ps("ps_t", [P, CW])
        tb = ps_t[:, :].bitcast(BF16)
        s_raw = [m.sem(f"s_raw{u}") for u in range(2)]
        s_rv = [m.sem(f"s_rv{u}") for u in range(2)]
        s_c = m.sem("s_c")
        s_cv = m.sem("s_cv")
        s_q1 = m.sem("s_q1")
        s_bld = m.sem("s_bld")
        s_vx = m.sem("s_vx")
        s_msp = m.sem("s_msp")
        s_ms1 = m.sem("s_ms1")
        s_tq1 = m.sem("s_tq1")
        s_tk = m.sem("s_tk")
        s_tm = m.sem("s_tm")
        s_to = m.sem("s_to")
        s_eq1 = m.sem("s_eq1")
        s_ek = m.sem("s_ek")
        s_em = m.sem("s_em")
        s_eo = m.sem("s_eo")
        s_m1 = [m.sem(f"s_m1{u}") for u in range(2)]
        s_m2 = [m.sem(f"s_m2{u}") for u in range(2)]
        s_mm = [m.sem(f"s_mm{u}") for u in range(2)]
        s_z = m.sem("s_z")
        s_k2 = [m.sem(f"s_k2{u}") for u in range(2)]
        s_s = m.sem("s_s")
        s_mx = m.sem("s_mx")
        s_p = m.sem("s_p")
        s_e = m.sem("s_e")
        s_pv = m.sem("s_pv")
        s_oe = m.sem("s_oe")
        s_ro = m.sem("s_ro")
        LEAD = 3
        NQ = 9
        block = st.enter_context(nc.Block())

        @block.sync
        def _(sp):
            def load_qk(i, u):
                if not isinstance(i, int) or i >= 2:
                    sp.wait_ge(s_bld, i - 1)
                for r, x in enumerate(("q", "k")):
                    sp.dma_start(raw[:, u, r, :], A[x][:, ds(i, 1), :, :].rearrange("p o t w -> p (o t w)")
                                 ).then_inc(s_raw[u], 16)

            def load_v(i, u):
                if not isinstance(i, int) or i >= 2:
                    sp.wait_ge(s_vx, i - 1)
                sp.dma_start(raw[:, u, 2, :], A["v"][:, ds(i, 1), :, :].rearrange("p o t w -> p (o t w)")
                             ).then_inc(s_rv[u], 16)

            def copy_q1(i, u):
                sp.wait_ge(s_eq1, 2 * i + 2)
                for h in range(2):
                    r = slice(h * HR, (h + 1) * HR)
                    sp.dma_start(qm1[r, u, h, :], qT1[r, u, :]).then_inc(s_m1[u], 16)

            def copy_2(i, u):
                sp.wait_ge(s_ek, 2 * i + 2)
                if not isinstance(i, int) or i >= 2:
                    sp.wait_ge(s_p, 32 * i - 32)
                sp.dma_start(kT2[:, u, :], kT1[:, u, :]).then_inc(s_k2[u], 16)
                for h in range(2):
                    r = slice(h * HR, h * HR + KR)
                    sp.dma_start(qm2[r, u, h, :], qT1[r, u, :]).then_inc(s_m2[u], 16)

            def copy_m(i, u):
                sp.wait_ge(s_em, i + 1)
                for h in range(2):
                    for a in range(3):
                        row, src = h * HR + KR + a, (h * 3 + a) * G8
                        sp.dma_start(qm2[row:row + 1, u, h, :].rearrange("p (t n) -> p t n", n=P),
                                     mT[src:src + G8, u, :]).then_inc(s_mm[u], 16)

            def pair(i, u, left):
                if left >= 4:
                    load_qk(i + 4, u)
                if left >= 2:
                    load_v(i + 2, u)
                if left >= 1:
                    copy_2(i + 1, 1 - u)
                if left >= 2:
                    copy_q1(i + 2, u)
                if left >= 1:
                    copy_m(i + 1, 1 - u)

            for i in range(2):
                load_qk(i, i)
            for i in range(2):
                load_v(i, i)
            sp.wait_ge(s_z, 2)
            copy_q1(0, 0)
            load_qk(2, 0)
            copy_q1(1, 1)
            load_qk(3, 1)
            copy_2(0, 0)
            copy_m(0, 0)
            with sp.Fori(0, PAIRS // 2 - 2) as k:
                for u in range(2):
                    pair(k * 2 + u, u, 4)
            for i in range(PAIRS - 4, PAIRS):
                pair(i, i % 2, PAIRS - 1 - i)
            for u in range(2):
                sp.wait_ge(s_k2[u], 16 * (PAIRS // 2))

        @block.gpsimd
        def _(pool):
            def part(dst, src):
                zero = K["zero"][:, 0:1]
                for at, n in enumerate(src.shape[1:]):
                    zero = bcast(zero, at + 1, n)
                zero = bass.AP(zero.tensor, zero.offset, [list(x) for x in zero.ap][:-1])
                return nc.gpsimd.tensor_tensor(out=dst, in0=src, in1=zero, op=ALU.add)

            def build(i, u, h):
                if not isinstance(i, int) or i >= 2:
                    pool.wait_ge(s_tk, i - 1)
                pool.wait_ge(s_raw[u], 32 * (h + 1))

                def step(k, ins):
                    ins.then_inc(s_q1, 1)
                    pool.wait_ge(s_q1, i * NQ + k)
                q = raw[:, u, 0, :].rearrange("p (g d) -> p g d", d=DH)
                kk = raw[:, u, 1, :].rearrange("p (g d) -> p g d", d=DH)
                qs = qx[:, u].rearrange("p t h (s d) -> p (t h) s d", d=DH)
                ks = kx[:, u].rearrange("p t h (s d) -> p (t h) s d", d=DH)
                step(1, part(qs[:, :, 0:3, :], bcast(q, 2, 3)))
                step(2, part(ks[:, :, 1:6:2, :], bcast(kk, 2, 3)))
                step(3, nc.gpsimd.tensor_tensor(out=r1[:, 0], in0=q, in1=qs[:, :, 0, :], op=ALU.subtract))
                step(4, nc.gpsimd.tensor_tensor(out=r1[:, 1], in0=kk, in1=ks[:, :, 1, :], op=ALU.subtract))
                step(5, part(qs[:, :, 3:5, :], bcast(r1[:, 0], 2, 2)))
                step(6, part(ks[:, :, 2:5:2, :], bcast(r1[:, 1], 2, 2)))
                step(7, nc.gpsimd.tensor_tensor(out=r1[:, 2], in0=r1[:, 0], in1=qs[:, :, 3, :], op=ALU.subtract))
                step(8, nc.gpsimd.tensor_tensor(out=r1[:, 3], in0=r1[:, 1], in1=ks[:, :, 2, :], op=ALU.subtract))
                step(9, part(qs[:, :, 5, :], r1[:, 2]))
                part(ks[:, :, 0, :], r1[:, 3]).then_inc(s_bld, 1)

            def build_v(i, u, h):
                if not isinstance(i, int) or i >= 2:
                    pool.wait_ge(s_pv, 8 * i - 6)
                pool.wait_ge(s_rv[u], 16 * (h + 1))
                part(vx[:, u].rearrange("p t h s -> p (t h) s")[:, :, 0:DH],
                     raw[:, u, 2, :].rearrange("p (g d) -> p g d", d=DH)).then_inc(s_vx, 1)

            def split_max(i, u):
                if not isinstance(i, int) or i >= 2:
                    pool.wait_ge(s_tm, i - 1)
                pool.wait_ge(s_mx, 16 * i + 18)

                def step(k, ins):
                    ins.then_inc(s_ms1, 1)
                    pool.wait_ge(s_ms1, i * 4 + k)
                n = negm[:, u].rearrange("p t h -> p h t")
                x = mp[:, u, 0:6 * G8].rearrange("p (h a t) -> p h a t", h=2, a=3)
                r = mr[:, :, :].rearrange("p a (h t) -> p a h t", h=2)
                step(1, part(x[:, :, 0, :], n))
                step(2, nc.gpsimd.tensor_tensor(out=r[:, 0], in0=n, in1=x[:, :, 0, :], op=ALU.subtract))
                step(3, part(x[:, :, 1, :], r[:, 0]))
                step(4, nc.gpsimd.tensor_tensor(out=r[:, 1], in0=r[:, 0], in1=x[:, :, 1, :], op=ALU.subtract))
                part(x[:, :, 2, :], r[:, 1]).then_inc(s_msp, 1)

            def pair(i, u, h, left):
                if left >= 1:
                    build_v(i + 1, 1 - u, h + u)
                if left >= 3:
                    build(i + 3, 1 - u, h + 1 + u)
                if left >= 1:
                    split_max(i + 1, 1 - u)

            build(0, 0, 0)
            build(1, 1, 0)
            pool.wait_ge(s_cv, 3)
            build_v(0, 0, 0)
            build(2, 0, 1)
            split_max(0, 0)
            pair(0, 0, 0, 4)
            pair(1, 1, 0, 4)
            with pool.Fori(1, PAIRS // 2 - 2) as k:
                for u in range(2):
                    pair(k * 2 + u, u, k, 4)
            for i in range(PAIRS - 4, PAIRS):
                pair(i, i % 2, i // 2, PAIRS - 1 - i)

        @block.vector
        def _(dve):
            m.seed(s_mx, 2)
            m.seed(s_e, 2)
            m.seed(s_pv, 2)
            m.seed(s_oe, 1)
            nc.vector.memset(qx[:, :, :, :, KR:HR], 0.0).then_inc(s_c, 1)
            nc.vector.memset(kx[:, :, :, :, KR:HR], 0.0).then_inc(s_c, 1)
            dve.wait_ge(s_c, 2)
            nc.vector.memset(kx[:, :, :, :, KR:KM], 1.0).then_inc(s_c, 1)
            nc.vector.memset(vx[:, :, :, :, :], 0.0).then_inc(s_cv, 1)
            dve.wait_ge(s_cv, 1)
            nc.vector.memset(vx[:, :, :, :, DH:DH + 1], 1.0).then_inc(s_cv, 1)
            nc.vector.memset(mp[:, :, :], 0.0).then_inc(s_cv, 1)
            nc.vector.memset(qm1[:, :, :, :], 0.0).then_inc(s_z, 1)
            nc.vector.memset(qm2[:, :, :, :], 0.0).then_inc(s_z, 1)

            def maxima(i, u, t):
                if t == 0 and (not isinstance(i, int) or i >= 2):
                    dve.wait_ge(s_msp, i - 1)
                for h in range(2):
                    dve.wait_ge(s_s, 16 * i + 2 * t + h + 1)
                    nc.vector.tensor_reduce(out=negm[:, u, t, h:h + 1], in_=ps_s[:, h, :], axis=AX.X,
                                            op=ALU.max, negate=True).then_inc(s_mx, 1)

            def output(i, u):
                dve.wait_ge(s_to, i + 1)
                t = ps_t[:, :].rearrange("p (j h a s) -> p j h a s", j=4, h=2, a=2)
                nc.vector.reciprocal(ro[:, u].rearrange("p j (h a) -> p j h a", h=2), t[:, :, :, :, DH]
                                     ).then_inc(s_ro, 1)
                dve.wait_ge(s_ro, i + 1)
                for a in range(2):
                    src = t[:, :, :, a, 0:DH]
                    r = ro[:, u].rearrange("p j (h a) -> p j h a", h=2)[:, :, :, a]
                    o = O[:, ds(i, 1), 4 * a:4 * a + 4, :].rearrange("p o j (h d) -> p (o j) h d", d=DH)
                    nc.vector.tensor_tensor(out=o, in0=src, in1=bcast(r, 3, DH), op=ALU.mult
                                            ).then_inc(s_eo, 1)

            def pair(i, u, nxt, nxt2, prev):
                for s in range(8):
                    if s + LEAD < 8 and nxt:
                        maxima(i + 1, 1 - u, s + LEAD)
                    if s + LEAD >= 8 and nxt2:
                        maxima(i + 2, u, s + LEAD - 8)
                    if s == 6 and prev:
                        output(i - 1, 1 - u)

            for t in range(8):
                maxima(0, 0, t)
            for t in range(LEAD):
                maxima(1, 1, t)
            pair(0, 0, True, True, False)
            pair(1, 1, True, True, True)
            with dve.Fori(1, PAIRS // 2 - 1) as k:
                for u in range(2):
                    pair(k * 2 + u, u, True, True, True)
            pair(PAIRS - 2, 0, True, False, True)
            pair(PAIRS - 1, 1, False, False, True)
            output(PAIRS - 1, 1)

        @block.scalar
        def _(act):
            def evac_q1(i, u, half, hh=None):
                if hh is not None and half == 0:
                    act.wait_ge(s_m1[u], 32 * hh)
                    act.wait_ge(s_m2[u], 32 * hh)
                if half == 0:
                    act.wait_ge(s_tq1, i + 1)
                r = slice(half * CW, (half + 1) * CW)
                nc.scalar.activation(qT1[:, u, r], tb[:, r], ACT.Copy).then_inc(s_eq1, 1)

            def evac_k(i, u, half, hh=None):
                if hh is not None and half == 0:
                    act.wait_ge(s_k2[u], 16 * hh)
                if half == 0:
                    act.wait_ge(s_tk, i + 1)
                r = slice(half * CW, (half + 1) * CW)
                nc.scalar.activation(kT1[:, u, r], tb[:, r], ACT.Copy).then_inc(s_ek, 1)

            def evac_m(i, u, hh=None):
                if hh is not None:
                    act.wait_ge(s_mm[u], 96 * hh)
                act.wait_ge(s_tm, i + 1)
                nc.scalar.activation(mT[:, u, :], tb[0:HR, 0:P], ACT.Copy).then_inc(s_em, 1)

            def evac_o(i, u):
                act.wait_ge(s_pv, 8 * i + 10)
                nc.scalar.activation(oT[:, u, :], ps_o[:, :], ACT.Copy).then_inc(s_oe, 1)

            def exps(i, u, s):
                act.wait_ge(s_pv, 8 * i + s + 1)
                for n in range(4):
                    h, half = n % 2, n // 2
                    act.wait_ge(s_p, 32 * i + 4 * s + n + 1)
                    nc.scalar.activation(pT[:, (s % 2) * 4 + n, :], ps_p[:, h, :], ACT.Exp,
                                         scale=SCALE).then_inc(s_e, 1)

            def pair(i, u, h, nxt, nxt2, first=False):
                for s in range(8):
                    exps(i, u, s)
                    if s in (1, 2) and nxt2:
                        evac_q1(i + 2, u, s - 1, h + 1)
                    if s in (3, 4) and nxt2:
                        evac_k(i + 2, u, s - 3, h + 1)
                    if s == 5 and nxt:
                        evac_m(i + 1, 1 - u, None if first else h + u)
                evac_o(i, u)

            for i in range(2):
                for half in range(2):
                    evac_q1(i, i, half)
                for half in range(2):
                    evac_k(i, i, half)
            evac_m(0, 0)
            pair(0, 0, 0, True, True, True)
            pair(1, 1, 0, True, True)
            with act.Fori(1, PAIRS // 2 - 1) as k:
                for u in range(2):
                    pair(k * 2 + u, u, k, True, True)
            pair(PAIRS - 2, 0, PAIRS // 2 - 1, True, False)
            pair(PAIRS - 1, 1, None, False, False)

        @block.tensor
        def _(pe):
            def rows(h, n):
                return slice(h * HR, h * HR + n)

            def transposes(src, u):
                for t in range(G8):
                    last = nc.tensor.transpose(tb[:, t * P:(t + 1) * P],
                                               src[:, u, t].rearrange("p h s -> p (h s)"), identb[:, :])
                return last

            def q1(i, u, before):
                for s, v in before:
                    pe.wait_ge(s, v)
                pe.wait_ge(s_bld, i + 1)
                transposes(qx, u).then_inc(s_tq1, 1)

            def k1(i, u):
                pe.wait_ge(s_eq1, 2 * i + 2)
                transposes(kx, u).then_inc(s_tk, 1)

            def maxT(i, u, before):
                pe.wait_ge(*before)
                pe.wait_ge(s_msp, i + 1)
                nc.tensor.transpose(tb[:, 0:P], mp[:, u, :], identb[:, :]).then_inc(s_tm, 1)

            def o1(i, u, before):
                pe.wait_ge(*before)
                pe.wait_ge(s_oe, i + 2)
                for j in range(4):
                    last = nc.tensor.transpose(ps_t[:, j * P:(j + 1) * P], oT[:, u, j * P:(j + 1) * P], ident[:, :])
                last.then_inc(s_to, 1)

            def by_query(i, u, hh, t):
                if t == 0:
                    pe.wait_ge(s_m1[u], 32 * (hh + 1))
                    pe.wait_ge(s_ek, 2 * i + 2)
                for h in range(2):
                    pe.wait_ge(s_mx, 16 * i + 2 * t + h + 1)
                    for half in range(2):
                        mm = nc.tensor.matmul(ps_s[:, h, half * CW:(half + 1) * CW],
                                              qm1[:, u, h, t * P:(t + 1) * P],
                                              kT1[:, u, half * CW:(half + 1) * CW],
                                              start=True, stop=True)
                    mm.then_inc(s_s, 1)

            def by_key(i, u, hh, s, half):
                if s == 0 and half == 0:
                    pe.wait_ge(s_m2[u], 32 * (hh + 1))
                    pe.wait_ge(s_mm[u], 96 * (hh + 1))
                    pe.wait_ge(s_k2[u], 16 * (hh + 1))
                for h in range(2):
                    n = 2 * half + h
                    pe.wait_ge(s_e, 32 * i + 4 * s + n + 1)
                    nc.tensor.matmul(ps_p[:, h, :], kT2[:, u, s * P:(s + 1) * P],
                                     qm2[:, u, h, half * CW:(half + 1) * CW],
                                     start=True, stop=True).then_inc(s_p, 1)

            def values(i, u, s):
                if s == 0:
                    pe.wait_ge(s_vx, i + 1)
                    pe.wait_ge(s_oe, i + 1)
                pe.wait_ge(s_e, 32 * i + 4 * s + 6)
                for n in range(4):
                    h, half = n % 2, n // 2
                    g = 32 * (2 * h + half)
                    last = nc.tensor.matmul(ps_o[g:g + 32, :], vx[:, u, s, h, :], pT[:, (s % 2) * 4 + n, :],
                                            start=(s == 0), stop=(s == 7))
                last.then_inc(s_pv, 1)

            def pair(i, u, hh, nxt, nxt2, prev):
                for s in range(8):
                    by_key(i, u, hh, s, 0)
                    if s + LEAD < 8 and nxt:
                        by_query(i + 1, 1 - u, hh + u, s + LEAD)
                    if s + LEAD >= 8 and nxt2:
                        by_query(i + 2, u, hh + 1, s + LEAD - 8)
                    by_key(i, u, hh, s, 1)
                    if s == 1 and nxt2:
                        q1(i + 2, u, [(s_em, i + 1) if isinstance(i, int) and i < 2 else (s_eo, 2 * i - 2)])
                    if s == 3 and nxt2:
                        k1(i + 2, u)
                    if s == 5 and nxt:
                        maxT(i + 1, 1 - u, (s_ek, 2 * i + 6) if nxt2 else (s_eo, 2 * i - 2))
                    if s == 6 and prev:
                        o1(i - 1, 1 - u, (s_em, i + 2) if nxt else (s_eo, 2 * i - 2))
                    if s:
                        values(i, u, s - 1)
                values(i, u, 7)

            pe.wait_ge(s_c, 3)
            q1(0, 0, [])
            k1(0, 0)
            for t in range(8):
                by_query(0, 0, 0, t)
            q1(1, 1, [(s_ek, 2)])
            k1(1, 1)
            for t in range(LEAD):
                by_query(1, 1, 0, t)
            maxT(0, 0, (s_ek, 4))
            pair(0, 0, 0, True, True, False)
            pair(1, 1, 0, True, True, True)
            with pe.Fori(1, PAIRS // 2 - 1) as k:
                for u in range(2):
                    pair(k * 2 + u, u, k, True, True, True)
            pair(PAIRS - 2, 0, PAIRS // 2 - 1, True, False, True)
            pair(PAIRS - 1, 1, PAIRS // 2 - 1, False, False, True)
            o1(PAIRS - 1, 1, (s_eo, 2 * (PAIRS - 1)))


def stage_project(nc, sems, W, K, A):
    X, ident, O = K["X"], K["ident"], A["o"]
    st = ExitStack()
    with st:
        m = Pool_(nc, st, sems, "wo")
        w = m.sb("w", [P, D])
        oc = m.sb("oc", [P, 2, CT, D])
        oT = m.sb("oT", [P, 2, CW])
        ps_t = m.ps("ps_t", [P, 2, CW])
        ps_y = m.ps("ps_y", [P, 2, CT, D])
        s_w = m.sem("s_w")
        s_oc = m.sem("s_oc")
        s_t = m.sem("s_t")
        s_oT = m.sem("s_oT")
        s_y = m.sem("s_y")
        s_x = m.sem("s_x")
        block = st.enter_context(nc.Block())

        @block.sync
        def _(sp):
            sp.dma_start(w[:, :], W["wo"]).then_inc(s_w, 16)
            sp.wait_ge(s_w, 16)

        @block.gpsimd
        def _(pool):
            with pool.Fori(0, CHUNKS // 2) as k:
                for u in range(2):
                    c = k * 2 + u
                    pool.wait_ge(s_t, c + 1)
                    for j in range(CT):
                        nc.gpsimd.tensor_tensor(out=oc[:, u, j, :].rearrange("p (h w) -> p h w", w=16),
                                                in0=O[:, ds(k * 8, 8), 4 * u + j, :],
                                                in1=bcast(bcast(K["zero"][:, 0:1], 1, 8), 2, 16)[:, :, :, 0],
                                                op=ALU.add).then_inc(s_oc, 1)

        @block.tensor
        def _(pe):
            pe.wait_ge(s_w, 16)
            with pe.Fori(0, CHUNKS // 2) as k:
                for u in range(2):
                    c = k * 2 + u
                    pe.wait_ge(s_oc, 4 * c + 4)
                    pe.wait_ge(s_oT, c + 1)
                    for j in range(CT):
                        last = nc.tensor.transpose(ps_t[:, u, j * P:(j + 1) * P], oc[:, u, j, :], ident[:, :])
                    last.then_inc(s_t, 1)
                    pe.wait_ge(s_oT, c + 3)
                    pe.wait_ge(s_x, c + 1)
                    for j in range(CT):
                        last = nc.tensor.matmul(ps_y[:, u, j, :], oT[:, u, j * P:(j + 1) * P], w[:, :],
                                                start=True, stop=True)
                    last.then_inc(s_y, 1)

        @block.scalar
        def _(act):
            with act.Fori(0, CHUNKS // 2) as k:
                for u in range(2):
                    c = k * 2 + u
                    act.wait_ge(s_y, c + 1)
                    act.wait_ge(s_t, c + 3)
                    nc.scalar.activation(oT[:, u, :], ps_t[:, u, :], ACT.Copy).then_inc(s_oT, 1)

        @block.vector
        def _(dve):
            m.seed(s_t, 2)
            m.seed(s_oT, 2)
            m.seed(s_x, 2)
            m.seed(s_y, 2)
            stats = Stats(m, K)
            for c in range(CHUNKS):
                dve.wait_ge(s_y, c + 3)
                xc = X[:, c * CT:(c + 1) * CT, :]
                nc.vector.tensor_tensor(out=xc, in0=ps_y[:, c % 2], in1=xc, op=ALU.add).then_inc(s_x, 1)
                if c:
                    dve.wait_ge(s_x, c + 2)
                    stats.dve(nc, (c - 1) * CT, CT)
            dve.wait_ge(s_x, CHUNKS + 2)
            stats.dve(nc, TILES - CT, CT)




EX, TOPK, HID, CAP = 64, 8, 96, 32
SLOTS_X = EX * CAP
ST = SLOTS_X // P
FAR = 1000.0


def stage_route(nc, sems, tag, K, M, S):
    X, ident = K["X"], K["ident"]
    pos, wt, H, nact = S["pos"], S["wt"], S["H"], S["nact"]
    st = ExitStack()
    with st:
        m = Pool_(nc, st, sems, tag)
        norm = Norm(m, K, H)
        row = m.sb("row", [P, TILES])
        v8 = m.sb("v8", [P, TILES, TOPK])
        r8 = m.sb("r8", [P, TILES])
        mask = m.sb("mask", [P, TILES, EX], BF16)
        PAD = CHUNKS // 2
        cum = m.sb("cum", [P, 2, PAD + CHUNKS, EX])
        low = m.sb("low", [P, CHUNKS])
        open_ = m.sb("open", [P, CHUNKS])
        cnt = m.sb("cnt", [P, 1])
        ps_lg = m.ps("ps_lg", [P, CT * EX])
        ps_c = m.ps("ps_c", [P, TILES, EX])
        ps_n = m.ps("ps_n", [P, CHUNKS, EX])
        s_lg = m.sem("s_lg")
        s_l = m.sem("s_l")
        s_z = m.sem("s_z")
        s_d = m.sem("s_d")
        s_ls = m.sem("s_ls")
        s_ex = m.sem("s_ex")
        s_mk = m.sem("s_mk")
        s_r8 = m.sem("s_r8")
        s_n = m.sem("s_n")
        s_c = m.sem("s_c")
        block = st.enter_context(nc.Block())

        @block.vector
        def _(dve):
            m.seed(s_l, 1)
            nc.vector.memset(cum[:, :, 0:PAD, :], 0.0).then_inc(s_z, 1)
            norm.dve_all(nc)
            norm.dve_apply(nc, 0, 0)
            norm.dve_apply(nc, 1, 1)

            def chunk(k, u, more):
                c = k * 2 + u
                if more:
                    norm.dve_apply(nc, c + 2, u)
                dve.wait_ge(s_lg, c + 1)
                nc.vector.tensor_scalar(out=wt[:, ds(c * CT, CT), :].rearrange("p t e -> p (t e)"),
                                        in0=ps_lg[:, :], scalar1=0.0, scalar2=None,
                                        op0=ALU.add).then_inc(s_l, 1)

            with dve.Fori(0, CHUNKS // 2 - 1) as k:
                for u in range(2):
                    chunk(k, u, True)
            chunk(CHUNKS // 2 - 1, 0, False)
            chunk(CHUNKS // 2 - 1, 1, False)

            done = 0

            def step(ins, wait=True):
                nonlocal done
                done += 1
                ins.then_inc(s_d, 1)
                if wait:
                    dve.wait_ge(s_d, done)
            halves = [slice(0, TILES // 2), slice(TILES // 2, TILES)]
            dve.wait_ge(s_l, CHUNKS + 1)
            step(nc.vector.tensor_reduce(out=row[:, :], in_=wt[:, :, :], axis=AX.X, op=ALU.max))
            for a in halves:
                nc.vector.tensor_tensor(out=wt[:, a, :], in0=wt[:, a, :], in1=bcast(row[:, a], 2, EX),
                                        op=ALU.subtract).then_inc(s_ls, 1)
            dve.wait_ge(s_ls, 2)
            for n, a in enumerate(halves):
                dve.wait_ge(s_ex, n + 1)
                step(nc.vector.tensor_reduce(out=row[:, a], in_=wt[:, a, :], axis=AX.X, op=ALU.add))
            step(nc.vector.reciprocal(row[:, :], row[:, :]))
            step(nc.vector.tensor_tensor(out=wt[:, :, :], in0=wt[:, :, :], in1=bcast(row[:, :], 2, EX),
                                         op=ALU.mult))
            for t in range(TILES):
                step(nc.vector.max(v8[:, t, :], wt[:, t, :]), False)
            dve.wait_ge(s_d, done)
            rest = pos
            for t in range(TILES):
                step(nc.vector.match_replace(out=rest[:, t, :], in_to_replace=v8[:, t, :], in_values=wt[:, t, :],
                                             imm_value=-1.0), False)
            dve.wait_ge(s_d, done)
            for a in halves:
                nc.vector.tensor_scalar(out=mask[:, a, :], in0=rest[:, a, :], scalar1=0.0, scalar2=None,
                                        op0=ALU.is_lt).then_inc(s_mk, 1)
            step(nc.vector.tensor_reduce(out=row[:, :], in_=v8[:, :, :], axis=AX.X, op=ALU.add))
            step(nc.vector.reciprocal(row[:, :], row[:, :]))
            nc.vector.tensor_copy(r8[:, :], row[:, :]).then_inc(s_r8, 1)
            dve.wait_ge(s_n, 1)
            dve.wait_ge(s_z, 1)
            step(nc.vector.tensor_copy(cum[:, 0, PAD:, :], ps_n[:, :, :]))
            v, s = 0, 1
            while s < CHUNKS:
                step(nc.vector.tensor_tensor(out=cum[:, 1 - v, PAD:, :], in0=cum[:, v, PAD:, :],
                                             in1=cum[:, v, PAD - s:PAD + CHUNKS - s, :], op=ALU.add))
                v, s = 1 - v, 2 * s
            before = cum[:, v, PAD - 1:PAD - 1 + CHUNKS, :]
            dve.wait_ge(s_mk, 2)
            dve.wait_ge(s_c, 1)
            step(nc.vector.scalar_tensor_tensor(out=pos[:, :, :], in0=mask[:, :, :], scalar=-FAR,
                                                in1=ps_c[:, :, :], op0=ALU.mult, op1=ALU.add), False)
            step(nc.vector.tensor_reduce(out=low[:, :], in_=before, axis=AX.X, op=ALU.min))
            step(nc.vector.tensor_scalar(out=open_[:, :], in0=low[:, :], scalar1=float(CAP), scalar2=None,
                                         op0=ALU.is_lt))
            step(nc.vector.tensor_reduce(out=cnt[:, :], in_=open_[:, :], axis=AX.X, op=ALU.add))
            nc.vector.tensor_copy(nact[:, :], cnt[:, :])
            for c in range(CHUNKS):
                pc = pos[:, c * CT:(c + 1) * CT, :]
                nc.vector.scalar_tensor_tensor(out=pc, in0=pc, scalar=FAR, in1=bcast(before[:, c, :], 1, CT),
                                               op0=ALU.add, op1=ALU.add)

        @block.gpsimd
        def _(pool):
            pool.wait_ge(s_r8, 1)
            nc.gpsimd.tensor_tensor(out=wt[:, :, :], in0=wt[:, :, :], in1=bcast(r8[:, :], 2, EX), op=ALU.mult)

        @block.scalar
        def _(act):
            norm.act_all(nc)
            norm.act_hT(nc, 0, 0)
            with act.Fori(0, CHUNKS // 2 - 1) as k:
                for u in range(2):
                    norm.act_hT(nc, k * 2 + u + 1, 1 - u)
            norm.act_hT(nc, CHUNKS - 1, 1)
            for n in range(2):
                act.wait_ge(s_ls, n + 1)
                a = wt[:, n * TILES // 2:(n + 1) * TILES // 2, :]
                nc.scalar.activation(a, a, ACT.Exp).then_inc(s_ex, 1)

        @block.tensor
        def _(pe):
            norm.pe_transpose(nc, 0, 0)

            def chunk(c, u, more):
                if more:
                    norm.pe_transpose(nc, c + 1, 1 - u)
                pe.wait_ge(norm.s_hT, c + 1)
                pe.wait_ge(s_l, c + 1)
                for s in range(CT):
                    last = nc.tensor.matmul(ps_lg[:, s * EX:(s + 1) * EX], norm.hT[:, u, s * P:(s + 1) * P],
                                            M["wr"][:, :], start=True, stop=True)
                last.then_inc(s_lg, 1)

            with pe.Fori(0, CHUNKS // 2 - 1) as k:
                for u in range(2):
                    chunk(k * 2 + u, u, True)
            chunk(CHUNKS - 2, 0, True)
            chunk(CHUNKS - 1, 1, False)
            pe.wait_ge(s_mk, 2)
            for t in range(TILES):
                last = nc.tensor.matmul(ps_n[:, t // CT, :], K["onesb"][:, :], mask[:, t, :],
                                        start=(t % CT == 0), stop=(t % CT == CT - 1))
            last.then_inc(s_n, 1)
            for c in range(CHUNKS):
                t = c * CT
                nc.tensor.matmul(ps_c[:, t:t + CT, :], K["triub"][:, :], mask[:, t:t + CT, :], start=True,
                                 stop=False, skip_group_check=True)
                for j in range(1, CT):
                    last = nc.tensor.matmul(ps_c[:, t + j:t + CT, :], K["onesb"][:, :], mask[:, t:t + CT - j, :],
                                            start=False, stop=(j == CT - 1), skip_group_check=True)
            last.then_inc(s_c, 1)


def stage_dispatch(nc, sems, tag, K, S):
    pos, wt, H, XT, w_slot = S["pos"], S["wt"], S["H"], S["XT"], S["w_slot"]
    NP = 3 * P // CAP
    st = ExitStack()
    with st:
        m = Pool_(nc, st, sems, tag)
        hc = m.sb("hc", [P, CT, D])
        hp = m.sb("hp", [P, 3, CT, D], BF16)
        r = m.sb("r", [P, 2, D])
        wc = m.sb("wc", [P, CT, EX])
        wp = m.sb("wp", [P, 3, CT, EX], BF16)
        wr = m.sb("wr", [P, 2, CT, EX])
        wo = m.sb("wo", [P, CT, ST, NP])
        ws = m.sb("ws", [P, CT, ST])
        wa = m.sb("wa", [P, ST])
        oh = m.sb("oh", [P, 2, EX, CAP], BF16)
        ps_x = m.ps("ps_x", [P, 4, CW])
        ps_w = m.ps("ps_w", [P, CT, CW // 2])
        s_h = m.sem("s_h")
        s_r = m.sem("s_r")
        s_w = m.sem("s_w")
        s_oh = m.sem("s_oh")
        s_t = m.sem("s_t")
        s_xa = m.sem("s_xa")
        s_ws = m.sem("s_ws")
        s_z = m.sem("s_z")
        block = st.enter_context(nc.Block())

        @block.sync
        def _(sp):
            n = sp.value_load(S["nact"][0:1, 0:1], min_val=1, max_val=CHUNKS)
            with sp.Fori(0, n) as c:
                sp.wait_ge(s_xa, c * 5 + 5)
                sp.dma_start(hc[:, :, :], H[:, ds(c * CT, CT), :]).then_inc(s_h, 16)
                sp.dma_start(wc[:, :, :], wt[:, ds(c * CT, CT), :]).then_inc(s_h, 16)

        @block.gpsimd
        def _(pool):
            n = pool.value_load(S["nact"][0:1, 0:1], min_val=1, max_val=CHUNKS)
            zero = bcast(K["zero"][:, 0:1], 1, D)[:, :, 0]
            with pool.Fori(0, n) as c:
                pool.wait_ge(s_h, c * 32 + 32)
                for j in range(CT):
                    def step(k, ins):
                        ins.then_inc(s_r, 1)
                        pool.wait_ge(s_r, c * 5 * CT + j * 5 + k)
                    step(1, nc.gpsimd.tensor_tensor(out=hp[:, 0, j], in0=hc[:, j], in1=zero, op=ALU.add))
                    step(2, nc.gpsimd.tensor_tensor(out=r[:, 0], in0=hc[:, j], in1=hp[:, 0, j], op=ALU.subtract))
                    step(3, nc.gpsimd.tensor_tensor(out=hp[:, 1, j], in0=r[:, 0], in1=zero, op=ALU.add))
                    step(4, nc.gpsimd.tensor_tensor(out=r[:, 1], in0=r[:, 0], in1=hp[:, 1, j], op=ALU.subtract))
                    step(5, nc.gpsimd.tensor_tensor(out=hp[:, 2, j], in0=r[:, 1], in1=zero, op=ALU.add))

        @block.vector
        def _(dve):
            m.seed(s_xa, 5)
            m.seed(s_t, 2)
            nc.vector.memset(w_slot[:, :], 0.0).then_inc(s_z, 1)
            nc.vector.memset(XT[:, :], 0.0).then_inc(s_z, 1)
            n = dve.value_load(S["nact"][0:1, 0:1], min_val=1, max_val=CHUNKS)
            with dve.Fori(0, n) as c:
                def wstep(k, ins):
                    ins.then_inc(s_w, 1)
                    dve.wait_ge(s_w, c * 5 + k)
                for j in range(CT):
                    dve.wait_ge(s_t, c * CT + j + 1)
                    row = pos[:, ds(c * CT + j, 1), :].rearrange("p o e -> p (o e)")
                    nc.vector.tensor_tensor(out=oh[:, j % 2], in0=bcast(row, 2, CAP),
                                            in1=bcast(K["iota"][:, :], 1, EX), op=ALU.is_equal).then_inc(s_oh, 1)
                    if j == 0:
                        dve.wait_ge(s_h, c * 32 + 32)
                        wstep(1, nc.vector.tensor_copy(wp[:, 0], wc[:, :, :]))
                        wstep(2, nc.vector.tensor_tensor(out=wr[:, 0], in0=wc[:, :, :], in1=wp[:, 0],
                                                         op=ALU.subtract))
                        wstep(3, nc.vector.tensor_copy(wp[:, 1], wr[:, 0]))
                        wstep(4, nc.vector.tensor_tensor(out=wr[:, 1], in0=wr[:, 0], in1=wp[:, 1],
                                                         op=ALU.subtract))
                        wstep(5, nc.vector.tensor_copy(wp[:, 2], wr[:, 1]))
                dve.wait_ge(s_z, 2)
                dve.wait_ge(s_xa, c * 5 + 5)
                dve.wait_ge(s_t, c * CT + CT + 2)
                for q in range(4):
                    nc.vector.tensor_tensor(out=XT[:, q * CW:(q + 1) * CW], in0=ps_x[:, q, :],
                                            in1=XT[:, q * CW:(q + 1) * CW], op=ALU.add).then_inc(s_xa, 1)
                nc.vector.tensor_tensor(out=wo[:, :, :, :],
                                        in0=ps_w[:, :, 0:ST * NP].rearrange("p t (s k) -> p t s k", k=NP),
                                        in1=bcast(bcast(K["own"][:, :], 1, ST), 1, CT), op=ALU.mult).then_inc(s_ws, 1)
                dve.wait_ge(s_ws, c * 3 + 1)
                nc.vector.tensor_reduce(out=ws[:, :, :], in_=wo[:, :, :, :], axis=AX.X, op=ALU.add).then_inc(s_ws, 1)
                dve.wait_ge(s_ws, c * 3 + 2)
                nc.vector.tensor_reduce(out=wa[:, :], in_=ws[:, :, :].rearrange("p t s -> p s t"), axis=AX.X,
                                        op=ALU.add).then_inc(s_ws, 1)
                dve.wait_ge(s_ws, c * 3 + 3)
                nc.vector.tensor_tensor(out=w_slot[:, :], in0=w_slot[:, :], in1=wa[:, :], op=ALU.add
                                        ).then_inc(s_xa, 1)

        @block.tensor
        def _(pe):
            n = pe.value_load(S["nact"][0:1, 0:1], min_val=1, max_val=CHUNKS)
            with pe.Fori(0, n) as c:
                pe.wait_ge(s_xa, c * 5 + 5)
                for j in range(CT):
                    pe.wait_ge(s_r, (c * CT + j) * 5 + 5)
                    pe.wait_ge(s_oh, c * CT + j + 1)
                    flat = oh[:, j % 2].rearrange("p e c -> p (e c)")
                    for a in range(3):
                        for q in range(4):
                            nc.tensor.matmul(ps_x[:, q, :], hp[:, a, j], flat[:, q * CW:(q + 1) * CW],
                                             start=(j == 0 and a == 0), stop=(j == CT - 1 and a == 2))
                    if j == 0:
                        pe.wait_ge(s_w, c * 5 + 5)
                    for s in range(ST):
                        last = nc.tensor.matmul(ps_w[:, j, s * NP:(s + 1) * NP].rearrange("p (a e) -> p a e", a=3),
                                                flat[:, s * P:(s + 1) * P], wp[:, :, j, s * 4:s * 4 + 4],
                                                start=True, stop=True)
                    last.then_inc(s_t, 1)


def stage_experts(nc, sems, tag, K, M, S):
    XT, ysb, w_slot = S["XT"], S["y"], S["w_slot"]
    wgu, wd = M["wgu"], M["wd"]
    st = ExitStack()
    with st:
        m = Pool_(nc, st, sems, tag)
        sg = m.sb("sg", [P, 2, 4, HID])
        gu = m.sb("gu", [P, 2, 4, HID])
        guT = m.sb("guT", [HID, 2, CW])
        ps_a = m.ps("ps_a", [P, 2, 4, CW // 2])
        ps_t = m.ps("ps_t", [HID, CW])
        ps_y = m.ps("ps_y", [P, 2, 4, D])
        s_up = m.sem("s_up")
        s_s = m.sem("s_s")
        s_g = m.sem("s_g")
        s_t = m.sem("s_t")
        s_tc = m.sem("s_tc")
        s_y = m.sem("s_y")
        s_ye = m.sem("s_ye")
        block = st.enter_context(nc.Block())
        Q = ST // 4

        @block.tensor
        def _(pe):
            def up(q):
                if q >= 2:
                    pe.wait_ge(s_g, q - 1)
                for t in range(4):
                    for e in range(4):
                        n = q * 16 + t * 4 + e
                        last = nc.tensor.matmul(ps_a[e * CAP:(e + 1) * CAP, q % 2, t, 0:2 * HID],
                                                XT[:, n * CAP:(n + 1) * CAP], wgu[:, n, :], start=True, stop=True)
                last.then_inc(s_up, 1)

            def tr(q):
                pe.wait_ge(s_g, q + 1)
                if q >= 1:
                    pe.wait_ge(s_tc, q)
                for t in range(4):
                    last = nc.tensor.transpose(ps_t[:, t * P:(t + 1) * P], gu[:, q % 2, t, :], K["ident"][:, :])
                last.then_inc(s_t, 1)

            def down(q):
                pe.wait_ge(s_tc, q + 1)
                if q >= 2:
                    pe.wait_ge(s_ye, q - 1)
                for t in range(4):
                    for e in range(4):
                        n = t * 4 + e
                        last = nc.tensor.matmul(ps_y[e * CAP:(e + 1) * CAP, q % 2, t, :],
                                                guT[:, q % 2, n * CAP:(n + 1) * CAP], wd[:, q * 16 + n, :],
                                                start=True, stop=True)
                last.then_inc(s_y, 1)

            up(0)
            for q in range(Q):
                if q + 1 < Q:
                    up(q + 1)
                tr(q)
                if q:
                    down(q - 1)
            down(Q - 1)

        @block.scalar
        def _(act):
            for q in range(Q):
                act.wait_ge(s_up, q + 1)
                if q >= 2:
                    act.wait_ge(s_g, q - 1)
                nc.scalar.activation(sg[:, q % 2], ps_a[:, q % 2, :, 0:HID], ACT.Silu).then_inc(s_s, 1)
                act.wait_ge(s_t, q + 1)
                if q >= 2:
                    act.wait_ge(s_y, q - 1)
                nc.scalar.activation(guT[:, q % 2, :], ps_t[:, :], ACT.Copy).then_inc(s_tc, 1)

        @block.vector
        def _(dve):
            def out(q):
                dve.wait_ge(s_y, q + 1)
                nc.vector.tensor_tensor(out=ysb[:, 4 * q:4 * q + 4, :], in0=ps_y[:, q % 2],
                                        in1=bcast(w_slot[:, 4 * q:4 * q + 4], 2, D), op=ALU.mult
                                        ).then_inc(s_ye, 1)
            for q in range(Q):
                dve.wait_ge(s_s, q + 1)
                if q >= 2:
                    dve.wait_ge(s_t, q - 1)
                nc.vector.tensor_tensor(out=gu[:, q % 2], in0=ps_a[:, q % 2, :, HID:2 * HID], in1=sg[:, q % 2],
                                        op=ALU.mult).then_inc(s_g, 1)
                if q:
                    out(q - 1)
            out(Q - 1)


def stage_combine(nc, sems, tag, K, S):
    X, identb = K["X"], K["identb"]
    pos, ysb = S["pos"], S["y"]
    st = ExitStack()
    with st:
        m = Pool_(nc, st, sems, tag)
        oh = m.sb("oh", [P, 2, EX, CAP], BF16)
        ohT = m.sb("ohT", [P, 2, ST, P])
        ps_t = m.ps("ps_t", [P, 2, CW])
        ps_o = m.ps("ps_o", [P, D])
        tb = ps_t[:, :, :].bitcast(BF16)
        s_e = m.sem("s_e")
        s_t = m.sem("s_t")
        s_v = m.sem("s_v")
        s_o = m.sem("s_o")
        s_x = m.sem("s_x")
        block = st.enter_context(nc.Block())

        @block.vector
        def _(dve):
            m.seed(s_t, 4)
            m.seed(s_v, 2)
            m.seed(s_o, 2)
            m.seed(s_x, 1)
            n = dve.value_load(S["nact"][0:1, 0:1], min_val=1, max_val=CHUNKS)

            def rows(t, v):
                row = pos[:, ds(t, 1), :].rearrange("p o e -> p (o e)")
                dve.wait_ge(s_t, 2 * t + 2)
                nc.vector.tensor_tensor(out=oh[:, v], in0=bcast(row, 2, CAP),
                                        in1=bcast(K["iota"][:, :], 1, EX), op=ALU.is_equal).then_inc(s_e, 1)

            def add(t):
                dve.wait_ge(s_o, t + 3)
                xt = X[:, ds(t, 1), :].rearrange("p o d -> p (o d)")
                nc.vector.scalar_tensor_tensor(out=xt, in0=ps_o[:, :], scalar=0.5, in1=xt, op0=ALU.mult,
                                               op1=ALU.add).then_inc(s_x, 1)
            with dve.Fori(0, n) as c:
                for j in range(CT):
                    rows(c * CT + j, j % 2)
                    if j >= 2:
                        add(c * CT + j - 2)
                for j in range(CT - 2, CT):
                    add(c * CT + j)

        @block.scalar
        def _(act):
            n = act.value_load(S["nact"][0:1, 0:1], min_val=1, max_val=CHUNKS)
            with act.Fori(0, n) as c:
                for j in range(CT):
                    t = c * CT + j
                    act.wait_ge(s_o, t + 1)
                    for q in range(2):
                        act.wait_ge(s_t, 2 * t + q + 5)
                        nc.scalar.activation(ohT[:, j % 2, q * 8:q * 8 + 8, :].rearrange("p s n -> p (s n)"),
                                             tb[:, q, :], ACT.Copy).then_inc(s_v, 1)

        @block.tensor
        def _(pe):
            n = pe.value_load(S["nact"][0:1, 0:1], min_val=1, max_val=CHUNKS)

            def tr(t, v):
                pe.wait_ge(s_e, t + 1)
                flat = oh[:, v].rearrange("p e c -> p (e c)")
                for q in range(2):
                    pe.wait_ge(s_v, 2 * t + q + 1)
                    for s in range(8):
                        last = nc.tensor.transpose(tb[:, q, s * P:(s + 1) * P],
                                                   flat[:, (q * 8 + s) * P:(q * 8 + s + 1) * P], identb[:, :])
                    last.then_inc(s_t, 1)

            def sums(t, v):
                pe.wait_ge(s_v, 2 * t + 4)
                pe.wait_ge(s_x, t + 1)
                for s in range(ST):
                    last = nc.tensor.matmul(ps_o[:, :], ohT[:, v, s, :], ysb[:, s, :],
                                            start=(s == 0), stop=(s == ST - 1))
                last.then_inc(s_o, 1)

            with pe.Fori(0, n) as c:
                tr(c * CT, 0)
                for j in range(CT):
                    if j + 1 < CT:
                        tr(c * CT + j + 1, (j + 1) % 2)
                    sums(c * CT + j, j % 2)


def moe(nc, sems, tag, K, M):
    st = ExitStack()
    with st:
        m = Pool_(nc, st, sems, tag)
        S = {"pos": m.sb("pos", [P, TILES, EX]), "wt": m.sb("wt", [P, TILES, EX]), "y": m.sb("y", [P, ST, D]),
             "nact": m.sb("nact", [P, 1], I32), "w_slot": m.sb("w_slot", [P, ST])}
        mid = ExitStack()
        with mid:
            m2 = Pool_(nc, mid, sems, tag + "m")
            S["XT"] = m2.sb("XT", [P, SLOTS_X])
            early = ExitStack()
            with early:
                S["H"] = Pool_(nc, early, sems, tag + "e").sb("H", [P, TILES, D])
                stage_route(nc, sems, tag + "r", K, M, S)
                stage_dispatch(nc, sems, tag + "d", K, S)
            stage_experts(nc, sems, tag + "x", K, M, S)
        stage_combine(nc, sems, tag + "c", K, S)


LEVELS = [N + 1] + [N >> k for k in range(1, 11)]
SCAN_EPS = 1e-8


def stage_scan_in(nc, sems, W, K, Q):
    X, ident = K["X"], K["ident"]
    E0, vT = Q["E"][0], Q["vT"]
    st = ExitStack()
    with st:
        m = Pool_(nc, st, sems, "si")
        norm = Norm(m, K, stats=True)
        w = m.sb("w", [P, 2, D])
        idn = m.sb("idn", [P, 1])
        ps_q = m.ps("ps_q", [P, 2, CW])
        s_w = m.sem("s_w")
        s_p = m.sem("s_p")
        s_e = m.sem("s_e")
        block = st.enter_context(nc.Block())

        @block.sync
        def _(sp):
            sp.dma_start(w[:, :, :], W["wqv"]).then_inc(s_w, 16)
            sp.dma_start(idn[:, :], W["identity"]).then_inc(s_w, 16)
            sp.wait_ge(s_w, 32)

        @block.vector
        def _(dve):
            m.seed(s_e, 2)
            norm.dve_all(nc)
            norm.dve_apply(nc, 0, 0)
            norm.dve_apply(nc, 1, 1)
            dve.wait_ge(s_w, 32)
            nc.vector.tensor_copy(E0[:, :, 0], bcast(idn[:, 0:1], 1, B)[:, :, 0])

            def chunk(c, u, b, more):
                if more:
                    norm.dve_apply(nc, c + 2, u)
                for r in range(2):
                    dst = E0[:, ds(b, 1), 1 + u * CW:1 + (u + 1) * CW] if r == 0 else vT[:, ds(b, 1), u * CW:(u + 1) * CW]
                    dve.wait_ge(s_p, 2 * c + r + 1)
                    nc.vector.tensor_scalar(out=dst.rearrange("p o n -> p (o n)"), in0=ps_q[:, r, :], scalar1=0.0,
                                            scalar2=None, op0=ALU.add).then_inc(s_e, 1)

            with dve.Fori(0, CHUNKS // 2 - 1) as k:
                for u in range(2):
                    chunk(k * 2 + u, u, k, True)
            chunk(CHUNKS - 2, 0, B - 1, False)
            chunk(CHUNKS - 1, 1, B - 1, False)

        @block.scalar
        def _(act):
            norm.act_all(nc)
            norm.act_hT(nc, 0, 0)
            with act.Fori(0, CHUNKS // 2 - 1) as k:
                for u in range(2):
                    norm.act_hT(nc, k * 2 + u + 1, 1 - u)
            norm.act_hT(nc, CHUNKS - 1, 1)

        @block.tensor
        def _(pe):
            pe.wait_ge(s_w, 32)
            norm.pe_transpose(nc, 0, 0)

            def chunk(c, u, more):
                if more:
                    norm.pe_transpose(nc, c + 1, 1 - u)
                pe.wait_ge(norm.s_hT, c + 1)
                for r in range(2):
                    pe.wait_ge(s_e, 2 * c + r + 1)
                    nc.tensor.matmul(ps_q[:, r, :], w[:, r, :], norm.hT[:, u, :], start=True,
                                     stop=True).then_inc(s_p, 1)

            with pe.Fori(0, CHUNKS // 2 - 1) as k:
                for u in range(2):
                    chunk(k * 2 + u, u, True)
            chunk(CHUNKS - 2, 0, True)
            chunk(CHUNKS - 1, 1, False)


def scan_combines():
    stages = []
    last = len(LEVELS) - 1
    for l in range(last):
        stages.append((LEVELS[l + 1], (l, 0, 2), (l, 1, 2), (l + 1, 0, 1), 0))
    for l in range(last - 1, -1, -1):
        n = LEVELS[l] // 2 - (LEVELS[l] % 2 == 0)
        stages.append((n, (l + 1, 0, 1), (l, 2, 2), (l, 2, 2), last - 1 - l))
    combines, copies = [], []
    before = []
    for k, (n, left, right, dst, ups) in enumerate(stages):
        if k >= last:
            copies.append((right[0], len(combines)))
        mine = []
        per = max(1, min(B, CW // n)) if n else 0
        for b in (range(0, B, per) if n else ()):
            need = max([i + 1 for i, b0, p0 in before if b0 < b + per and b < b0 + p0], default=0)
            mine.append((len(combines), b, per))
            combines.append((b, per, n, left, right, dst, need, ups))
        before = mine or before
    return combines, copies


def stage_scan_tree(nc, sems, K, Q):
    E_, Y = Q["E"], Q["Y"]
    RING = 4
    st = ExitStack()
    with st:
        m = Pool_(nc, st, sems, "sc")
        sq = m.sb("sq", [P, RING, CW])
        eps = m.sb("eps", [P, 1])
        ps_z = m.ps("ps_z", [P, RING, CW])
        ps_m = m.ps("ps_m", [P, RING, CW])
        s_eps = m.sem("s_eps")
        s_z = m.sem("s_z")
        s_sq = m.sem("s_sq")
        s_m = m.sem("s_m")
        s_rt = m.sem("s_rt")
        s_rc = m.sem("s_rc")
        s_o = m.sem("s_o")
        s_cp = m.sem("s_cp")
        block = st.enter_context(nc.Block())
        combines, copies = scan_combines()

        def view(x, b, per, n):
            level, first, step = x
            return E_[level][:, b:b + per, first:first + step * (n - 1) + 1:step]

        def flat(t, g):
            _, per, n = combines[g][:3]
            return t[:, g % RING, 0:per * n].rearrange("p (b n) -> p b n", n=n)

        def cols(t, g):
            _, per, n = combines[g][:3]
            return t[:, g % RING, 0:per * n]

        def pipeline(first, second):
            for g, (*_, need, _) in enumerate(combines):
                if g and need == g:
                    second(g - 1)
                first(g)
                if g and need < g:
                    second(g - 1)
            second(len(combines) - 1)

        @block.tensor
        def _(pe):
            def z(g):
                b, per, n, left, right, _, need, ups = combines[g]
                if max(need, g + 1 - RING) > 0:
                    pe.wait_ge(s_o, max(need, g + 1 - RING))
                if ups:
                    pe.wait_ge(s_cp, ups)
                nc.tensor.matmul(flat(ps_z, g), Y[:, 0, :], view(left, b, per, n), start=True, stop=False)
                nc.tensor.matmul(flat(ps_z, g), Y[:, 1, :], view(right, b, per, n), start=False,
                                 stop=True).then_inc(s_z, 1)

            def sums(g):
                pe.wait_ge(s_sq, g + 1)
                nc.tensor.matmul(cols(ps_m, g), K["ones"][:, :], cols(sq, g), start=True, stop=True
                                 ).then_inc(s_m, 1)
            pipeline(z, sums)

        @block.scalar
        def _(act):
            act.wait_ge(s_eps, 1)

            def squares(g):
                act.wait_ge(s_z, g + 1)
                nc.scalar.activation(cols(sq, g), cols(ps_z, g), ACT.Square).then_inc(s_sq, 1)

            def roots(g):
                act.wait_ge(s_m, g + 1)
                nc.scalar.activation(cols(sq, g), cols(ps_m, g), ACT.Sqrt, bias=eps[:, 0:1],
                                     scale=1.0 / D).then_inc(s_rt, 1)
            pipeline(squares, roots)

        @block.gpsimd
        def _(pool):
            for k, (l, g) in enumerate(copies):
                pool.wait_ge(s_o, g)
                if k:
                    pool.wait_ge(s_cp, k)
                n = LEVELS[l] // 2
                nc.gpsimd.tensor_copy(E_[l][:, :, 1:2 * n:2], E_[l + 1][:, :, 0:n]).then_inc(s_cp, 1)

        @block.vector
        def _(dve):
            nc.vector.memset(eps[:, :], SCAN_EPS).then_inc(s_eps, 1)
            for g, (b, per, n, _, _, dst, _, _) in enumerate(combines):
                dve.wait_ge(s_rt, g + 1)
                nc.vector.reciprocal(cols(sq, g), cols(sq, g)).then_inc(s_rc, 1)
                dve.wait_ge(s_rc, g + 1)
                nc.vector.tensor_tensor(out=view(dst, b, per, n), in0=flat(ps_z, g), in1=flat(sq, g),
                                        op=ALU.mult).then_inc(s_o, 1)


def stage_scan_out(nc, sems, W, K, Q):
    X = K["X"]
    E0, vT = Q["E"][0], Q["vT"]
    st = ExitStack()
    with st:
        m = Pool_(nc, st, sems, "so")
        w = m.sb("w", [P, D])
        pr = m.sb("pr", [P, 2, CW])
        ps_y = m.ps("ps_y", [P, 2, CT, D])
        s_w = m.sem("s_w")
        s_pr = m.sem("s_pr")
        s_y = m.sem("s_y")
        s_x = m.sem("s_x")
        block = st.enter_context(nc.Block())

        @block.sync
        def _(sp):
            sp.dma_start(w[:, :], W["wc"]).then_inc(s_w, 16)
            sp.wait_ge(s_w, 16)

        @block.vector
        def _(dve):
            m.seed(s_y, 2)
            m.seed(s_x, 2)

            stats = Stats(m, K)

            def product(c):
                b, u = c // 2, c % 2
                dve.wait_ge(s_y, c + 1)
                nc.vector.tensor_tensor(out=pr[:, u, :], in0=E0[:, b, 1 + u * CW:1 + (u + 1) * CW],
                                        in1=vT[:, b, u * CW:(u + 1) * CW], op=ALU.mult).then_inc(s_pr, 1)

            product(0)
            for c in range(CHUNKS):
                if c + 1 < CHUNKS:
                    product(c + 1)
                dve.wait_ge(s_y, c + 3)
                xc = X[:, c * CT:(c + 1) * CT, :]
                nc.vector.tensor_tensor(out=xc, in0=ps_y[:, c % 2], in1=xc, op=ALU.add).then_inc(s_x, 1)
                if c:
                    dve.wait_ge(s_x, c + 2)
                    stats.dve(nc, (c - 1) * CT, CT)
            dve.wait_ge(s_x, CHUNKS + 2)
            stats.dve(nc, TILES - CT, CT)

        @block.tensor
        def _(pe):
            pe.wait_ge(s_w, 16)
            with pe.Fori(0, CHUNKS // 2) as k:
                for u in range(2):
                    c = k * 2 + u
                    pe.wait_ge(s_x, c + 1)
                    pe.wait_ge(s_pr, c + 1)
                    for j in range(CT):
                        last = nc.tensor.matmul(ps_y[:, u, j, :], pr[:, u, j * P:(j + 1) * P], w[:, :],
                                                start=True, stop=True)
                    last.then_inc(s_y, 1)


def stage_scan(nc, sems, W, K, XY):
    st = ExitStack()
    with st:
        m = Pool_(nc, st, sems, "s")
        Q = {"Y": XY[:, :, 1, :], "vT": m.sb("vT", [P, B, N]),
             "E": [m.sb(f"E{k}", [P, B, n]) for k, n in enumerate(LEVELS)]}
        stage_scan_in(nc, sems, W, K, Q)
        stage_scan_tree(nc, sems, K, Q)
        stage_scan_out(nc, sems, W, K, Q)


def stage_store(nc, sems, K, out):
    st = ExitStack()
    with st:
        m = Pool_(nc, st, sems, "st")
        s_out = m.sem("s_out")
        block = st.enter_context(nc.Block())

        @block.sync
        def _(sp):
            o = out.rearrange("b (n p) d -> p (b n) d", p=P)
            for q in range(4):
                sp.dma_start(o[:, q * 8:q * 8 + 8, :], K["X"][:, q * 8:q * 8 + 8, :]).then_inc(s_out, 16)
            sp.wait_ge(s_out, 64)


def program(nc, W, out, stages="fafmsm"):
    st = ExitStack()
    with st:
        sems = st
        m = Pool_(nc, st, sems, "g")
        K = {"X": m.sb("X", [P, TILES, D]), "mv": m.sb("mv", [P, TILES, 2]), "ident": m.sb("ident", [P, P]), "ones": m.sb("ones", [P, P]),
             "triu": m.sb("triu", [P, P]), "identb": m.sb("identb", [P, P], BF16),
             "onesb": m.sb("onesb", [P, P], BF16), "triub": m.sb("triub", [P, P], BF16),
             "iota": m.sb("iota", [P, CAP]), "own": m.sb("own", [P, 3 * P // CAP]), "zero": m.sb("zero", [P, 1])}
        stage_load(nc, sems, W, K)
        R = {"w1": m.sb("w1", [P, E + 1, I]), "w3": m.sb("w3", [P, E + 1, I]),
             "w2": m.sb("w2", [P, 3, E + 1, D]), "wr": m.sb("wr", [P, E]), "br": m.sb("br", [P, E]),
             "rev": m.sb("rev", [P, E]), "steps": m.sb("steps", [P, SLOT_TILES + TILES])}
        K["Hs"] = nc.dram_tensor("Hs", (SLOT_TILES * P, D), F32, kind="Internal").ap()
        K["Ys"] = nc.dram_tensor("Ys", (SLOT_TILES * P, D), F32, kind="Internal").ap()
        with nc.cleanup_on_exit():
            if stages[0] == "f":
                ffn(nc, sems, "fa", W, K, R, True)
        attn = ExitStack()
        with nc.cleanup_on_exit(), attn:
            ma = Pool_(nc, attn, sems, "a")
            A = {n: ma.sb(n, [P, PAIRS, PT_, 2 * DH]) for n in "qkvo"}
            if stages[1] == "a":
                stage_qkv(nc, sems, W, K, A)
                stage_attention(nc, sems, K, A)
                stage_project(nc, sems, W, K, A)
        if stages[2:] == "...":
            stage_store(nc, sems, K, out)
            return
        M = {"wr": m.sb("xwr", [P, EX]), "wgu": m.sb("xwgu", [P, EX, 2 * HID]),
             "wd": m.sb("xwd", [HID, EX, D])}
        XY = m.sb("XY", [P, 2, 2, P])
        with nc.cleanup_on_exit():
            if stages[2] == "f":
                ffn(nc, sems, "fb", W, K, R, stages[0] != "f", M, XY)
            elif stages[3:] != "...":
                stage_moe_weights(nc, sems, W, M)
        with nc.cleanup_on_exit():
            if stages[3] == "m":
                moe(nc, sems, "ma", K, M)
        with nc.cleanup_on_exit():
            if stages[4] == "s":
                stage_scan(nc, sems, W, K, XY)
        with nc.cleanup_on_exit():
            if stages[5] == "m":
                moe(nc, sems, "mb", K, M)
        stage_store(nc, sems, K, out)


def stage_moe_weights(nc, sems, W, M):
    st = ExitStack()
    with st:
        s_w = Pool_(nc, st, sems, "mw").sem("s_w")
        block = st.enter_context(nc.Block())

        @block.sync
        def _(sp):
            for n in ("wr", "wgu", "wd"):
                sp.dma_start(M[n][tuple(slice(None) for _ in M[n].shape)], W["x" + n]).then_inc(s_w, 16)
            sp.wait_ge(s_w, 48)


def host_arrays(i):
    import numpy as np
    c = np.ascontiguousarray
    up = np.arange(P)
    a = {"x": c(i["L0_attn_x"])}
    for n, name in (("w1", "1"), ("w3", "3")):
        e, s = np.asarray(i["L0_ffn_ew" + name]), np.asarray(i["L0_ffn_sw" + name])
        a[n] = c(np.concatenate([e, s[None]]).transpose(2, 0, 1))
    a["w2"] = c(np.concatenate([np.asarray(i["L0_ffn_ew2"]), np.asarray(i["L0_ffn_sw2"])[None]]).transpose(2, 0, 1))
    a["wr"] = c(np.asarray(i["L0_ffn_router_w"]).T)
    a["br"] = c(np.broadcast_to(np.asarray(i["L0_ffn_routing_bias"]), (P, E)))
    a["ident"] = np.eye(P, dtype=np.float32)
    a["ones"] = np.ones((P, P), np.float32)
    a["triu"] = (up[:, None] < up[None, :]).astype(np.float32)
    a["iota"] = np.tile(np.arange(CAP, dtype=np.float32), (P, 1))
    a["xwr"] = c(np.asarray(i["L1_ffn_gate_w"]).T)
    a["xwgu"] = c(np.concatenate([np.asarray(i["L1_ffn_w_" + n]) for n in ("gate", "up")], axis=1).transpose(2, 0, 1))
    a["own"] = np.tile((up[:, None] // CAP == np.arange(P // CAP)).astype(np.float32), (1, 3))
    a["xwd"] = c(np.asarray(i["L1_ffn_w_down"]).transpose(2, 0, 1))
    a["wqv"] = c(np.stack([np.asarray(i["L1_attn_W" + n]).T for n in "qv"], axis=1))
    a["identity"] = c(np.asarray(i["L1_attn_identity"]).reshape(P, 1))
    a["wp"] = c(np.stack([np.asarray(i["L1_attn_Wp1"]), np.asarray(i["L1_attn_Wp2"])]))
    a["wpt"] = c(a["wp"].transpose(0, 2, 1))
    a["wc"] = c(np.asarray(i["L1_attn_Wc"]).T)
    a["steps"] = np.tile(np.concatenate([np.arange(SLOT_TILES), P * np.arange(TILES)]).astype(np.float32), (P, 1))
    a["rev"] = np.tile(np.arange(E, 0, -1, dtype=np.float32), (P, 1))
    a["wqkv"] = c(np.concatenate([np.asarray(i["L0_attn_W" + n]).T for n in "qkv"], axis=1))
    a["wo"] = c(np.asarray(i["L0_attn_Wo"]).T)
    a["nw"] = c(np.broadcast_to(np.stack([np.asarray(i["L0_attn_qn_w"]), np.asarray(i["L0_attn_kn_w"])]), (P, 2, DH)))
    return a


def kernel(**inputs):
    import numpy as np
    import concourse.bacc as bacc
    from concourse.bass_utils import run_bass_kernel_spmd

    arrays = host_arrays(inputs)
    nc = bacc.Bacc("TRN2", target_bir_lowering=False, num_devices=1)
    W = {n: nc.dram_tensor(n, a.shape, mybir.dt.from_np(a.dtype), kind="ExternalInput").ap() for n, a in arrays.items()}
    out = nc.dram_tensor("out", (B, N, D), F32, kind="ExternalOutput").ap()
    program(nc, W, out)
    r = run_bass_kernel_spmd(nc, [arrays], core_ids=[0])
    return r.results[0]["out"]
```
